# Optimizing a Trainium2 kernel written in Bass

```python
import numpy as np
import jax
import jax.numpy as jnp

def _softmax(x, axis=-1):
    return jax.nn.softmax(x, axis=axis)

def _gelu(x):
    return jax.nn.gelu(x, approximate=True)

def _silu(x):
    return jax.nn.silu(x)

def _sigmoid(x):
    return jax.nn.sigmoid(x)

def _layernorm(x, axis=-1, eps=1e-05):
    m = jnp.mean(x, axis=axis, keepdims=True)
    v = jnp.var(x, axis=axis, keepdims=True)
    return (x - m) / jnp.sqrt(v + eps)

def _scatter_add(tgt, idx, src, axis=0):
    return tgt.at[idx].add(src)

def _segment_sum(src, seg, n):
    return jax.ops.segment_sum(src, seg, n)
kernel_name = 'mk_gps_d1_gnn_r8_81b1bc'

def setup_inputs(seed: int=0):
    np.random.seed(seed)
    _w = jnp.asarray

    def _rec_inputs():
        import jax
        import jax.numpy as jnp
        _gk = jax.random.key(seed)
        x = -0.0002117 + 1 * jax.random.normal(jax.random.fold_in(_gk, 1), (12500, 256), jnp.float32)
        src = jax.random.randint(jax.random.fold_in(_gk, 2), (200000,), 0, 12500, jnp.int32)
        dst = jax.random.randint(jax.random.fold_in(_gk, 3), (200000,), 0, 12500, jnp.int32)
        _o = jnp.argsort(dst, stable=True)
        src = src[_o]
        dst = dst[_o]
        edge_weight = jax.random.uniform(jax.random.fold_in(_gk, 12), (200000,), jnp.float32, 0.0, 1)
        return (x, src, dst, edge_weight)
    x, src, dst, edge_weight = _rec_inputs()

    def _L0_gnn_setup():
        import jax, jax.numpy as jnp
        import numpy as np
        N_NODES = 12500
        key = jax.random.key(seed)
        k = jax.random.split(key, 7)
        N, E, F_IN, F_OUT = (N_NODES, 400000, 256, 256)
        stdv = 1.0 / np.sqrt(F_OUT)
        return {'x': jax.random.normal(k[0], (N, F_IN), dtype=jnp.float32), 'edge_row': jax.random.randint(k[1], (E,), 0, N, dtype=jnp.int32), 'edge_col': jax.random.randint(k[2], (E,), 0, N, dtype=jnp.int32), 'edge_val': jax.random.uniform(k[3], (E,), dtype=jnp.float32), 'weight': jax.random.uniform(k[4], (F_IN, F_OUT), dtype=jnp.float32, minval=-stdv, maxval=stdv), 'learnable_diag': 0.01 * jax.random.normal(k[5], (F_IN,), dtype=jnp.float32), 'bias': jax.random.uniform(k[6], (F_OUT,), dtype=jnp.float32, minval=-stdv, maxval=stdv)}
    _L0_gnn_all = _L0_gnn_setup()
    _L0_gnn_in = {k: v for k, v in _L0_gnn_all.items() if k in ('weight', 'learnable_diag', 'bias')}
    del _L0_gnn_all

    def _L0_mix_setup():
        import jax, jax.numpy as jnp
        import numpy as np
        HEADS = 8
        DIM_HEAD = 64
        EPS = 1e-05

        def _inst_norm_lastdim(t):
            mu = jnp.mean(t, axis=-1, keepdims=True)
            var = jnp.mean(jnp.square(t - mu), axis=-1, keepdims=True)
            return (t - mu) * jax.lax.rsqrt(var + EPS)
        key = jax.random.key(seed)
        k1, k2, k3, k4 = jax.random.split(key, 4)
        b, n, dim = (4, 1024, 256)
        inner = HEADS * DIM_HEAD
        x = jax.random.normal(k1, (b, n, dim), dtype=jnp.float32)
        Wqkv = jax.random.normal(k2, (3 * inner, dim), dtype=jnp.float32) * (1.0 / np.sqrt(dim))
        Wout = jax.random.normal(k3, (dim, inner), dtype=jnp.float32) * (1.0 / np.sqrt(inner))
        bout = jax.random.normal(k4, (dim,), dtype=jnp.float32) * 0.01
        return {'x': x, 'Wqkv': Wqkv, 'Wout': Wout, 'bout': bout}
    _L0_mix_all = _L0_mix_setup()
    _L0_mix_in = {k: v for k, v in _L0_mix_all.items() if k in ('Wqkv', 'Wout', 'bout')}
    del _L0_mix_all

    def _L0_ffn_setup():
        import jax, jax.numpy as jnp
        import numpy as np
        DIM = 256
        H = 8
        D = 64
        G = 64
        INNER = H * D
        SCALE = D ** (-0.5)
        key = jax.random.key(seed)
        ks = jax.random.split(key, 12)
        B, N = (4, 2048)
        x = jax.random.normal(ks[0], (B, N, DIM), dtype=jnp.float32)
        s = lambda fan_in: 1.0 / np.sqrt(fan_in)
        W_fx = jax.random.normal(ks[1], (DIM, INNER), dtype=jnp.float32) * s(DIM)
        b_fx = jnp.zeros((INNER,), dtype=jnp.float32)
        W_x = jax.random.normal(ks[2], (DIM, INNER), dtype=jnp.float32) * s(DIM)
        b_x = jnp.zeros((INNER,), dtype=jnp.float32)
        A = jax.random.normal(ks[3], (G, D), dtype=jnp.float32)
        Q, _ = jnp.linalg.qr(A.T)
        W_slice = Q[:, :G].astype(jnp.float32)
        b_slice = jnp.zeros((G,), dtype=jnp.float32)
        W_q = jax.random.normal(ks[4], (D, D), dtype=jnp.float32) * s(D)
        W_k = jax.random.normal(ks[5], (D, D), dtype=jnp.float32) * s(D)
        W_v = jax.random.normal(ks[6], (D, D), dtype=jnp.float32) * s(D)
        W_out = jax.random.normal(ks[7], (INNER, DIM), dtype=jnp.float32) * s(INNER)
        b_out = jnp.zeros((DIM,), dtype=jnp.float32)
        temperature = jnp.ones((1, H, 1, 1), dtype=jnp.float32) * 0.5
        return {'x': x, 'W_fx': W_fx, 'b_fx': b_fx, 'W_x': W_x, 'b_x': b_x, 'W_slice': W_slice, 'b_slice': b_slice, 'W_q': W_q, 'W_k': W_k, 'W_v': W_v, 'W_out': W_out, 'b_out': b_out, 'temperature': temperature}
    _L0_ffn_all = _L0_ffn_setup()
    _L0_ffn_in = {k: v for k, v in _L0_ffn_all.items() if k in ('W_fx', 'b_fx', 'W_x', 'b_x', 'W_slice', 'b_slice', 'W_q', 'W_k', 'W_v', 'W_out', 'b_out', 'temperature')}
    del _L0_ffn_all
    return {'x': x, 'src': src, 'dst': dst, 'edge_weight': edge_weight, 'L0_gnn_weight': _L0_gnn_in['weight'], 'L0_gnn_learnable_diag': _L0_gnn_in['learnable_diag'], 'L0_gnn_bias': _L0_gnn_in['bias'], 'L0_mix_Wqkv': _L0_mix_in['Wqkv'], 'L0_mix_Wout': _L0_mix_in['Wout'], 'L0_mix_bout': _L0_mix_in['bout'], 'L0_ffn_W_fx': _L0_ffn_in['W_fx'], 'L0_ffn_b_fx': _L0_ffn_in['b_fx'], 'L0_ffn_W_x': _L0_ffn_in['W_x'], 'L0_ffn_b_x': _L0_ffn_in['b_x'], 'L0_ffn_W_slice': _L0_ffn_in['W_slice'], 'L0_ffn_b_slice': _L0_ffn_in['b_slice'], 'L0_ffn_W_q': _L0_ffn_in['W_q'], 'L0_ffn_W_k': _L0_ffn_in['W_k'], 'L0_ffn_W_v': _L0_ffn_in['W_v'], 'L0_ffn_W_out': _L0_ffn_in['W_out'], 'L0_ffn_b_out': _L0_ffn_in['b_out'], 'L0_ffn_temperature': _L0_ffn_in['temperature']}

def reference(x, src, dst, edge_weight, L0_gnn_weight, L0_gnn_learnable_diag, L0_gnn_bias, L0_mix_Wqkv, L0_mix_Wout, L0_mix_bout, L0_ffn_W_fx, L0_ffn_b_fx, L0_ffn_W_x, L0_ffn_b_x, L0_ffn_W_slice, L0_ffn_b_slice, L0_ffn_W_q, L0_ffn_W_k, L0_ffn_W_v, L0_ffn_W_out, L0_ffn_b_out, L0_ffn_temperature):
    import jax
    import jax.numpy as jnp

    def _L0_gnn_ref(x, edge_row, edge_col, edge_val, weight, learnable_diag, bias):
        import jax, jax.numpy as jnp
        import numpy as np
        N_NODES = 12500
        gathered = edge_val[:, None] * x[edge_col]
        e1 = jax.ops.segment_sum(gathered, edge_row, num_segments=N_NODES)
        e2 = e1 * (learnable_diag + 1.0)
        e4 = x - e2
        out = e4 @ weight + bias
        return out

    def _L0_mix_ref(x, Wqkv, Wout, bout):
        import jax, jax.numpy as jnp
        import numpy as np
        HEADS = 8
        DIM_HEAD = 64
        EPS = 1e-05

        def _inst_norm_lastdim(t):
            mu = jnp.mean(t, axis=-1, keepdims=True)
            var = jnp.mean(jnp.square(t - mu), axis=-1, keepdims=True)
            return (t - mu) * jax.lax.rsqrt(var + EPS)
        b, n, dim = x.shape
        qkv = jnp.einsum('bnc,fc->bnf', x, Wqkv)
        q, k, v = jnp.split(qkv, 3, axis=-1)

        def to_heads(t):
            return t.reshape(b, n, HEADS, DIM_HEAD).transpose(0, 2, 1, 3)
        q, k, v = (to_heads(q), to_heads(k), to_heads(v))
        k = _inst_norm_lastdim(k)
        v = _inst_norm_lastdim(v)
        dots = jnp.einsum('bhnd,bhne->bhde', k, v)
        out = jnp.einsum('bhnd,bhde->bhne', q, dots) / n
        out = out.transpose(0, 2, 1, 3).reshape(b, n, HEADS * DIM_HEAD)
        return jnp.einsum('bnf,cf->bnc', out, Wout) + bout

    def _L0_ffn_ref(x, W_fx, b_fx, W_x, b_x, W_slice, b_slice, W_q, W_k, W_v, W_out, b_out, temperature):
        import jax, jax.numpy as jnp
        import numpy as np
        DIM = 256
        H = 8
        D = 64
        G = 64
        INNER = H * D
        SCALE = D ** (-0.5)
        B, N, _ = x.shape
        fx_mid = (x @ W_fx + b_fx).reshape(B, N, H, D).transpose(0, 2, 1, 3)
        x_mid = (x @ W_x + b_x).reshape(B, N, H, D).transpose(0, 2, 1, 3)
        temp = jnp.clip(temperature, 0.1, 5.0)
        slice_weights = jax.nn.softmax((x_mid @ W_slice + b_slice) / temp, axis=-1)
        slice_norm = slice_weights.sum(axis=2)
        slice_token = jnp.einsum('bhnc,bhng->bhgc', fx_mid, slice_weights)
        slice_token = slice_token / (slice_norm[..., None] + 1e-05)
        q = slice_token @ W_q
        k = slice_token @ W_k
        v = slice_token @ W_v
        attn = jax.nn.softmax(jnp.einsum('bhgc,bhkc->bhgk', q, k) * SCALE, axis=-1)
        out_slice = jnp.einsum('bhgk,bhkc->bhgc', attn, v)
        out_x = jnp.einsum('bhgc,bhng->bhnc', out_slice, slice_weights)
        out_x = out_x.transpose(0, 2, 1, 3).reshape(B, N, INNER)
        return out_x @ W_out + b_out
    xn = _layernorm(x, axis=-1)
    x = x + _L0_gnn_ref(xn, src, dst, edge_weight, L0_gnn_weight, L0_gnn_learnable_diag, L0_gnn_bias) + _L0_mix_ref(xn[None], L0_mix_Wqkv, L0_mix_Wout, L0_mix_bout)[0]
    x = x + _L0_ffn_ref(_layernorm(x, axis=-1)[None], L0_ffn_W_fx, L0_ffn_b_fx, L0_ffn_W_x, L0_ffn_b_x, L0_ffn_W_slice, L0_ffn_b_slice, L0_ffn_W_q, L0_ffn_W_k, L0_ffn_W_v, L0_ffn_W_out, L0_ffn_b_out, L0_ffn_temperature)[0]
    return x

_drawn_inputs = setup_inputs


def setup_inputs(seed=0):
    import zlib

    import numpy as np

    out = dict(_drawn_inputs(seed))
    spreads = {'L0_ffn_b_fx': (0.0, 0.1),
     'L0_ffn_b_x': (0.0, 0.8),
     'L0_ffn_b_slice': (0.0, 0.8),
     'L0_ffn_b_out': (0.0, 0.1),
     'L0_ffn_temperature': (0.5, 0.6)}
    factors = {'L0_gnn_learnable_diag': 7.472,
     'L0_mix_bout': 8.0,
     'L0_ffn_W_fx': 3.091,
     'L0_ffn_W_x': 8.0,
     'L0_ffn_W_slice': 8.0,
     'L0_ffn_W_q': 8.0,
     'L0_ffn_W_k': 8.0}
    for name, (base, spread) in spreads.items():
        noise = np.random.default_rng([zlib.crc32(name.encode()), seed]).standard_normal(out[name].shape)
        drawn = base * np.exp(spread * noise) if base else spread * noise
        out[name] = jnp.asarray(drawn.astype(out[name].dtype))
    for name, factor in factors.items():
        out[name] = (out[name] * factor).astype(out[name].dtype)
    return out
```

```python
from contextlib import ExitStack

import concourse.bass as bass
from concourse import mybir

F32 = mybir.dt.float32
BF16 = mybir.dt.bfloat16
I32 = mybir.dt.int32
ALU = mybir.AluOpType
ACT = mybir.ActivationFunctionType
AX = mybir.AxisListType

P = 128
N, D = 12500, 256
E = 200000
H, DH, G = 8, 64, 64
INNER = H * DH
NPAIR = H // 2
NBLK = -(-N // P)
LAST = N - (NBLK - 1) * P
NPAD = NBLK * P
EPS = 1e-5
KC = D // P

GC = 4
GU = 4
NGRP = NBLK * GU
ECOL = NGRP * GC
EFULL = E // P
NBK = NBLK + 1
UT = 8
NT = -(-(E + NBLK * (P - 1)) // P)
NT = -(-NT // P) * P
NTX = NT + UT
assert (ECOL * P - E) // P + 1 + (E + NBLK * (P - 1)) // P <= NTX
assert ECOL >= EFULL + 1


class Chain:

    def __init__(self, engine, sem):
        self.engine, self.sem, self.n = engine, sem, 0

    def __call__(self, instruction):
        self.n += 1
        instruction.then_inc(self.sem, 1)
        self.engine.wait_ge(self.sem, self.n)


def split_rows(link, vec, out, rows, masks, t1, t2, acc):
    n = rows.shape[1]
    b = out
    link(vec.tensor_copy(b, rows))
    link(vec.tensor_tensor(t1, rows, b, ALU.subtract))
    link(vec.tensor_scalar(acc, b, masks[0:3, 0:1], None, ALU.mult))
    link(vec.tensor_copy(b, t1))
    link(vec.tensor_tensor(t2, t1, b, ALU.subtract))
    link(vec.scalar_tensor_tensor(out=acc, in0=b, scalar=masks[0:3, 1:2], in1=acc, op0=ALU.mult, op1=ALU.add))
    link(vec.scalar_tensor_tensor(out=acc, in0=t2, scalar=masks[0:3, 2:3], in1=acc, op0=ALU.mult, op1=ALU.add))
    link(vec.tensor_copy(b, acc))


def norm_stats(link, vec, st, tmp, var):
    link(vec.tensor_tensor(tmp[:, 0, :], st[:, :, 1], st[:, :, 4], ALU.add))
    link(vec.tensor_tensor(tmp[:, 1, :], st[:, :, 1], st[:, :, 4], ALU.subtract))
    link(vec.tensor_tensor(tmp[:, 1, :], tmp[:, 1, :], tmp[:, 1, :], ALU.mult))
    link(vec.tensor_tensor(var, st[:, :, 2], st[:, :, 5], ALU.add))
    link(vec.scalar_tensor_tensor(out=var, in0=tmp[:, 1, :], scalar=D / 4.0, in1=var, op0=ALU.mult, op1=ALU.add))
    link(vec.tensor_scalar(var, var, 1.0 / D, EPS, ALU.mult, ALU.add))


def gps_layer(nc, x, src, dst, edge_weight, gnn_w, gnn_diag, gnn_b, wqkv, wqkv_t, wout_t, bout,
              w_fx, b_fx, w_x_t, b_x, w_slice, b_slice, w_q, w_k, w_v, w_out, b_out, temp, out):
    with ExitStack() as ctx:
        def allocator(stack):
            def sb(name, shape, dt=F32):
                return stack.enter_context(nc.sbuf_tensor(name, shape, dt))

            def ps(name, shape, dt=F32):
                return stack.enter_context(nc.psum_tensor(name, shape, dt))
            return sb, ps

        def sem(name):
            return ctx.enter_context(nc.semaphore(name))

        def sems(name, n):
            return [sem(f"{name}{k}") for k in range(n)]

        xn_d = nc.dram_tensor("xn_table", (NPAD, D), F32).ap()
        xnt_d = nc.dram_tensor("xn_transposed", (NBLK, P, D), F32).ap()
        rec_d = nc.dram_tensor("sorted_edges", (NTX * P, 4), F32).ap()
        tb_d = nc.dram_tensor("tile_blocks", (NTX,), I32).ap()
        swt_d = nc.dram_tensor("slice_weights_t", (NBLK, P, INNER), F32).ap()

        sb, _ = allocator(ctx)
        big = sb("big", [P, NBLK, D])
        ident = sb("ident", [P, P])
        wx1 = sb("wx1", [P, 2 * KC, D])
        wls = sb("wls", [P, KC, INNER])
        b1_3 = sb("b1_3", [3, D], BF16)
        bl_3 = sb("bl_3", [3, INNER], BF16)
        b2_3 = sb("b2_3", [3, D], BF16)
        ones3 = sb("ones3", [3, P], BF16)
        mask = sb("mask", [P, NBLK])
        stats = sb("stats", [P, NBLK, 6])
        lnt = sb("lnt", [P, 2, NBLK])
        rstd = sb("rstd", [P, NBLK])
        nmr = sb("nmr", [P, NBLK])
        tblk = sb("tblk", [1, NTX], I32)
        wkv = sb("wkv", [P, KC, 2 * INNER])
        base0 = sb("base0", [P, NBK])
        slt = sb("slt", [P, P], BF16)
        onesb = sb("onesb", [P, P], BF16)
        iob = sb("iob", [P, NBK], BF16)
        ion = sb("ion", [P, P])

        edges = ExitStack()
        esb, _ = allocator(edges)
        rec = esb("rec", [P, ECOL, 4])
        blk = esb("blk", [P, ECOL], BF16)

        oh_shape = [P, GC, NBK]
        iob_b = iob[:, :].unsqueeze(1).to_broadcast(oh_shape)

        def blk_b(col):
            return blk[:, bass.ds(col, GC)].unsqueeze(2).to_broadcast(oh_shape)

        phase = ExitStack()
        sb, ps = allocator(phase)
        srci = sb("srci", [P, ECOL], I32)
        dsti = sb("dsti", [P, ECOL], I32)
        wf = sb("wf", [P, ECOL])
        zer = sb("zer", [P, 512])
        oh = sb("oha", [P, GU, GC, NBK], BF16)
        cnt = sb("cnt", [P, NBK])
        ntl = sb("ntl", [P, NBK], I32)
        ntf = sb("ntf", [P, NBK])
        incl = sb("incl", [P, NBK])
        onek = sb("onek", [P, NBK])
        tno = sb("tno", [P, NT // P])
        tcm = sb("tcm", [P, NT // P, NBLK])
        tbf = sb("tbf", [P, NT // P])
        tbi = sb("tbi", [P, NT // P], I32)
        diag = sb("diag", [P, KC])
        wxt = sb("wxt", [DH, H, D])
        wsl = sb("wsl", [DH, G])
        bxc = sb("bxc", [DH, H])
        bx3 = sb("bx3", [DH, H, 3])
        tmp8 = sb("tmp8", [P, H])
        rt8 = sb("rt8", [P, H])
        rows = sb("rows", [3, INNER])
        row2 = sb("row2", [3, INNER])
        sp1 = sb("sp1", [3, INNER])
        sp2 = sb("sp2", [3, INNER])
        wmean = sb("wmean", [P, KC, 2 * H])
        pcnt = ps("pcnt", [P, GC, NBK])
        pls = ps("pls", [P, KC, INNER])
        pbl = ps("pbl", [3, INNER])

        a_zero = sem("a_zero")
        a_x = sems("a_x", 7)
        a_edge = sem("a_edge")
        a_tail = sem("a_tail")
        a_memset = sem("a_memset")
        a_zrec = sem("a_zrec")
        a_w = sem("a_w")
        a_wx = sem("a_wx")
        a_pool = sem("a_pool")
        a_poolc = sem("a_poolc")
        a_chain = sem("a_chain")
        a_oh = sem("a_oh")
        a_ohfree = sems("a_ohfree", GU)
        a_cnt = sem("a_cnt")
        a_var = sem("a_var")
        a_sqrt = sem("a_sqrt")
        a_xn = sem("a_xn")
        a_store = sem("a_store")
        a_fold = sem("a_fold")
        a_bx = sem("a_bx")
        a_tb = sem("a_tb")
        a_tbd = sem("a_tbd")
        a_tbl = sem("a_tbl")
        XB = NBLK // 7
        NW = 12

        with nc.Block() as block:
            @block.sync
            def _(sp):
                sp.dma_start(srci[:, 0:EFULL], src[0:EFULL * P].rearrange("(p c) -> p c", p=P)).then_inc(a_edge, 16)
                for k in range(7):
                    b0, b1 = k * XB, (k + 1) * XB
                    full = b1 if b1 < NBLK else NBLK - 1
                    sp.dma_start(big[:, b0:full, :],
                                 x[b0 * P:full * P, :].rearrange("(b p) f -> p b f", p=P)).then_inc(a_x[k], 16)
                sp.wait_ge(a_zero, 1)
                sp.dma_start(big[0:LAST, NBLK - 1, :], x[(NBLK - 1) * P:N, :]).then_inc(a_x[6], 16)
                sp.dma_start(dsti[:, 0:EFULL], dst[0:EFULL * P].rearrange("(p c) -> p c", p=P)).then_inc(a_edge, 16)
                sp.dma_start(wf[:, 0:EFULL], edge_weight[0:EFULL * P].rearrange("(p c) -> p c", p=P)).then_inc(a_edge, 16)
                for k in range(7):
                    sp.wait_ge(a_xn, (k + 1) * XB)
                    sp.dma_start(xn_d[k * XB * P:(k + 1) * XB * P, :].rearrange("(b p) f -> p b f", p=P),
                                 big[:, k * XB:(k + 1) * XB, :]).then_inc(a_store, 16)
                sp.wait_ge(a_tb, 1)
                sp.dma_start(tb_d[0:NT].rearrange("(p j) -> p j", p=P), tbi[:, :]).then_inc(a_tbd, 16)
                sp.wait_ge(a_tbd, 16)
                sp.dma_start(tblk[0:1, 0:NT], tb_d[0:NT].rearrange("(o t) -> o t", o=1)).then_inc(a_tbl, 16)
                sp.wait_ge(a_store, 7 * 16)
                sp.wait_ge(a_tbl, 16)

            @block.gpsimd
            def _(pool):
                pool.memset(ident[:, :], 0.0).then_inc(a_poolc, 1)
                pool.memset(slt[:, :], 1.0).then_inc(a_poolc, 1)
                pool.iota(ion[:, :], pattern=[[1, P]], base=0, channel_multiplier=0,
                          allow_small_or_imprecise_dtypes=True).then_inc(a_pool, 1)
                pool.iota(iob[:, :], pattern=[[1, NBK]], base=0, channel_multiplier=0,
                          allow_small_or_imprecise_dtypes=True).then_inc(a_pool, 1)
                pool.iota(tno[:, :], pattern=[[1, NT // P]], base=0, channel_multiplier=NT // P,
                          allow_small_or_imprecise_dtypes=True).then_inc(a_pool, 1)
                pool.memset(onesb[:, :], 1.0).then_inc(a_pool, 1)
                pool.memset(ones3[:, :], 1.0).then_inc(a_pool, 1)
                pool.memset(onek[:, :], 1.0).then_inc(a_pool, 1)
                pool.memset(mask[:, :], 1.0).then_inc(a_poolc, 1)
                pool.wait_ge(a_poolc, 3)
                pool.affine_select(out=ident[:, :], in_=ident[:, :], compare_op=ALU.not_equal, fill=1.0,
                                   base=0, pattern=[[-1, P]], channel_multiplier=1).then_inc(a_pool, 1)
                pool.affine_select(out=slt[:, :], in_=slt[:, :], compare_op=ALU.is_ge, fill=0.0,
                                   base=-1, pattern=[[1, P]], channel_multiplier=-1).then_inc(a_pool, 1)
                pool.affine_select(out=mask[:, :], in_=mask[:, :], compare_op=ALU.is_ge, fill=0.0,
                                   base=N - 1, pattern=[[-P, NBLK]], channel_multiplier=-1).then_inc(a_pool, 1)

            @block.scalar
            def _(act):
                act.wait_ge(a_memset, 1)
                act.dma_start(srci[0:E - EFULL * P, EFULL:EFULL + 1],
                              src[EFULL * P:E].rearrange("(p o) -> p o", o=1)).then_inc(a_tail, 16)
                act.dma_start(dsti[0:E - EFULL * P, EFULL:EFULL + 1],
                              dst[EFULL * P:E].rearrange("(p o) -> p o", o=1)).then_inc(a_tail, 16)
                act.dma_start(wf[0:E - EFULL * P, EFULL:EFULL + 1],
                              edge_weight[EFULL * P:E].rearrange("(p o) -> p o", o=1)).then_inc(a_tail, 16)
                act.dma_start(wx1[:, KC:2 * KC, :], gnn_w.rearrange("(c p) n -> p c n", p=P)).then_inc(a_w, 16)
                with nc.allow_non_contiguous_dma("small columns"):
                    act.dma_start(diag[:, :], gnn_diag.rearrange("(c p) -> p c", p=P)).then_inc(a_w, 16)
                    act.dma_start(bxc[:, :], b_x.rearrange("(h d) -> d h", h=H)).then_inc(a_w, 16)
                act.dma_start(wxt[:, :, :], w_x_t.rearrange("(h d) f -> d h f", h=H)).then_inc(a_w, 16)
                act.dma_start(wsl[:, :], w_slice).then_inc(a_w, 16)
                act.dma_start(tmp8[:, :], temp.partition_broadcast(P)).then_inc(a_w, 16)
                act.dma_start(rows[:, 0:D], gnn_b.partition_broadcast(3)).then_inc(a_w, 16)
                act.dma_start(rows[:, D:2 * D], bout.partition_broadcast(3)).then_inc(a_w, 16)
                for h in range(H):
                    act.dma_start(row2[:, h * G:(h + 1) * G], b_slice.partition_broadcast(3)).then_inc(a_w, 16)
                act.dma_start(wkv[:, :, :], wqkv_t[:, INNER:3 * INNER].rearrange("(c p) n -> p c n", p=P)).then_inc(a_w, 16)
                act.wait_ge(a_zero, 1)
                zrows = NTX * P * 4 // (P * 512)
                for k in range(zrows):
                    act.dma_start(rec_d[k * P * P:(k + 1) * P * P, :].rearrange("(p r) f -> p (r f)", p=P),
                                  zer[:, :]).then_inc(a_zrec, 16)
                left = NTX * P - zrows * P * P
                if left:
                    act.dma_start(rec_d[zrows * P * P:NTX * P, :].rearrange("(p r) f -> p (r f)", p=P),
                                  zer[:, 0:left * 4 // P]).then_inc(a_zrec, 16)
                act.wait_ge(a_zrec, 16 * (zrows + (left > 0)))
                act.wait_ge(a_var, 1)
                act.activation(rstd[:, :], rstd[:, :], ACT.Sqrt).then_inc(a_sqrt, 1)

            @block.tensor
            def _(pe):
                pe.wait_ge(a_pool, 9)
                pe.wait_ge(a_zero, 1)
                nc.tensor.matmul(pcnt[:, :, :], ident[:, :], zer[:, 0:GC * NBK].rearrange("p (c b) -> p c b", b=NBK),
                                 start=True, stop=False, skip_group_check=True)
                with pe.Fori(0, NBLK) as i:
                    for u in range(GU):
                        pe.wait_ge(a_oh, i * GU + u + 1)
                        nc.tensor.matmul(pcnt[:, :, :], onesb[:, :], oh[:, u, :, :], start=False, stop=False,
                                         skip_group_check=True).then_inc(a_ohfree[u], 1)
                pe.wait_ge(a_w, 17 * 16)
                pe.wait_ge(a_bx, 1)
                for h in range(H):
                    for c in range(KC):
                        nc.tensor.matmul(pls[:, c, h * G:(h + 1) * G], wxt[:, h, c * P:(c + 1) * P], wsl[:, :],
                                         start=True, stop=True)
                    last = nc.tensor.matmul(pbl[:, h * G:(h + 1) * G], bx3[:, h, :], wsl[:, :], start=True, stop=True)
                last.then_inc(a_fold, 1)

            @block.vector
            def _(dve):
                link = Chain(dve, a_chain)
                nc.vector.memset(srci[:, EFULL:ECOL], NBLK * P)
                nc.vector.memset(dsti[:, EFULL:ECOL], 0)
                nc.vector.memset(wf[:, EFULL:ECOL], 0.0).then_inc(a_memset, 1)
                nc.vector.memset(zer[:, :], 0.0)
                nc.vector.memset(tblk[0:1, NT:NTX], 0)
                nc.vector.memset(big[64:P, NBLK - 1, :], 0.0).then_inc(a_zero, 1)
                link(nc.vector.memset(rec[:, :, :], 0.0))
                dve.wait_ge(a_tail, 48)
                dve.wait_ge(a_edge, 48)
                i7 = dsti
                link(nc.vector.tensor_copy(rec[:, :, 0], dsti[:, :]))
                link(nc.vector.tensor_copy(rec[:, :, 2], wf[:, :]))
                link(nc.vector.tensor_scalar(i7[:, :], srci[:, :], 7, None, ALU.arith_shift_right))
                link(nc.vector.tensor_copy(blk[:, :], i7[:, :]))
                link(nc.vector.tensor_scalar(i7[:, :], srci[:, :], P - 1, None, ALU.bitwise_and))
                link(nc.vector.tensor_copy(rec[:, :, 1], i7[:, :]))
                dve.wait_ge(a_pool, 9)
                with dve.Fori(0, NBLK) as i:
                    for u in range(GU):
                        dve.wait_ge(a_ohfree[u], i)
                        nc.vector.tensor_tensor(oh[:, u, :, :], blk_b((i * GU + u) * GC), iob_b,
                                                ALU.is_equal).then_inc(a_oh, 1)
                for u in range(GU):
                    dve.wait_ge(a_ohfree[u], NBLK)
                link(nc.vector.tensor_reduce(cnt[:, :], pcnt[:, :, :].rearrange("p c b -> p b c"), AX.X, ALU.add))
                link(nc.vector.tensor_scalar(ntl[:, :], cnt[:, :], float(P - 1), None, ALU.add))
                link(nc.vector.tensor_scalar(ntl[:, :], ntl[:, :], 7, None, ALU.arith_shift_right))
                link(nc.vector.tensor_copy(ntf[:, :], ntl[:, :]))
                link(nc.vector.tensor_tensor_scan(incl[:, :], onek[:, :], ntf[:, :], 0.0, ALU.mult, ALU.add))
                link(nc.vector.tensor_tensor(cnt[:, :], incl[:, :], ntf[:, :], ALU.subtract))
                link(nc.vector.tensor_scalar(base0[:, :], cnt[:, :], float(P), None, ALU.mult))
                shape = [P, NT // P, NBLK]
                link(nc.vector.tensor_tensor(tcm[:, :, :], incl[:, 0:NBLK].unsqueeze(1).to_broadcast(shape),
                                             tno[:, :].unsqueeze(2).to_broadcast(shape), ALU.is_le))
                link(nc.vector.tensor_reduce(tbf[:, :], tcm[:, :, :], AX.X, ALU.add))
                nc.vector.tensor_scalar(tbi[:, :], tbf[:, :], float(NBLK - 1), None, ALU.min).then_inc(a_tb, 1)
                for k in range(7):
                    dve.wait_ge(a_x[k], 16 if k < 6 else 32)
                with dve.Fori(0, NBLK) as i:
                    nc.vector.bn_stats(stats[:, bass.ds(i, 1), :].rearrange("p a b -> p (a b)"),
                                       big[:, bass.ds(i, 1), :].rearrange("p a b -> p (a b)")).then_inc(a_cnt, 1)
                dve.wait_ge(a_cnt, NBLK)
                norm_stats(link, nc.vector, stats, lnt, rstd[:, :])
                link(nc.vector.tensor_scalar(nmr[:, :], lnt[:, 0, :], -0.5, None, ALU.mult))
                nc.vector.tensor_copy(lnt[:, 1, :], rstd[:, :]).then_inc(a_var, 1)
                dve.wait_ge(a_sqrt, 1)
                link(nc.vector.reciprocal(rstd[:, :], rstd[:, :]))
                link(nc.vector.tensor_tensor(nmr[:, :], nmr[:, :], rstd[:, :], ALU.mult))
                with dve.Fori(0, NBLK) as i:
                    row = big[:, bass.ds(i, 1), :].rearrange("p a b -> p (a b)")
                    nc.vector.tensor_scalar(row, row, rstd[:, bass.ds(i, 1)], nmr[:, bass.ds(i, 1)],
                                            ALU.mult, ALU.add).then_inc(a_xn, 1)
                dve.wait_ge(a_w, 17 * 16)
                for h in range(H):
                    last = nc.vector.tensor_copy(bx3[:, h, :], bxc[:, h:h + 1].to_broadcast([DH, 3]))
                last.then_inc(a_bx, 1)
                link(nc.vector.tensor_scalar(diag[:, :], diag[:, :], 1.0, -1.0, ALU.add, ALU.mult))
                for c in range(KC):
                    link(nc.vector.tensor_scalar(wx1[:, KC + c, :], wx1[:, KC + c, :], diag[:, c:c + 1], None, ALU.mult))
                for c in range(KC):
                    w3 = wkv[:, c, :].rearrange("p (h d) -> p h d", d=DH)
                    link(nc.vector.tensor_reduce(wmean[:, c, :], w3, AX.X, ALU.add))
                    link(nc.vector.tensor_scalar(wmean[:, c, :], wmean[:, c, :], -1.0 / DH, None, ALU.mult))
                    link(nc.vector.tensor_tensor(w3, w3, wmean[:, c, :].unsqueeze(2).to_broadcast([P, 2 * H, DH]), ALU.add))
                link(nc.vector.tensor_scalar(tmp8[:, :], tmp8[:, :], 0.1, 5.0, ALU.max, ALU.min))
                link(nc.vector.reciprocal(rt8[:, :], tmp8[:, :]))
                dve.wait_ge(a_fold, 1)
                for c in range(KC):
                    nc.vector.tensor_tensor(wls[:, c, :].rearrange("p (h g) -> p h g", g=G),
                                            pls[:, c, :].rearrange("p (h g) -> p h g", g=G),
                                            rt8[:, :].unsqueeze(2).to_broadcast([P, H, G]), ALU.mult)
                link(nc.vector.tensor_tensor(row2[:, :], pbl[:, :], row2[:, :], ALU.add))
                r3 = row2[:, :].rearrange("p (h g) -> p h g", g=G)
                link(nc.vector.tensor_tensor(r3, r3, rt8[0:3, :].unsqueeze(2).to_broadcast([3, H, G]), ALU.mult))
                link(nc.vector.tensor_tensor(rows[:, 0:D], rows[:, 0:D], rows[:, D:2 * D], ALU.add))
                split_rows(link, nc.vector, b1_3[:, :], rows[:, 0:D], ident, sp1[:, 0:D], sp2[:, 0:D], rows[:, D:2 * D])
                split_rows(link, nc.vector, bl_3[:, :], row2[:, :], ident, sp1[:, :], sp2[:, :], rows[:, :])
        phase.close()

        phase = ExitStack()
        sb, ps = allocator(phase)
        oh = sb("ohb", [P, GU, GC, NBK], BF16)
        prod = sb("prod", [P, 2, GC, NBK])
        pos = sb("pos", [P, GU, GC], I32)
        recs = sb("recs", [P, GU, GC, 4])
        base = sb("base", [P, 2, NBK])
        xs = sb("xs", [P, D])
        xnt = sb("xnt", [P, KC, P])
        sq = sb("sq", [P, 2 * H, DH])
        ksb = sb("ksb", [P, INNER])
        vsb = sb("vsb", [P, H, DH])
        ss = sb("ss", [P, 2 * H])
        ms = sb("ms", [P, 2 * H])
        sc = sb("sc", [P, H])
        rt = sb("rt", [P, H])
        rs = sb("rs", [P, H])
        zero5 = sb("zero5", [P, INNER])
        ndots = sb("ndots", [P, NPAIR, P])
        wq = sb("wq", [P, NPAIR, D])
        wot = sb("wot", [P, NPAIR, D])
        at = sb("at", [P, NPAIR, D])
        pr = ps("pr", [P, 2, 512])
        pt = ps("pt", [P, 512])
        pkv = ps("pkv", [P, 2, 512])
        pdots = ps("pdots", [P, 512])
        ptr = ps("ptr", [P, 512])

        def ranks(k):
            return pr[:, k, 0:GC * NBK].rearrange("p (c b) -> p c b", b=NBK)

        b_oh = sem("b_oh")
        b_ranks = sem("b_ranks")
        b_total = sem("b_total")
        b_base = sem("b_base")
        b_prod = sems("b_prod", 2)
        b_pos = sems("b_pos", GU)
        b_rec = sems("b_rec", GU)
        b_scat = sems("b_scat", GU)
        b_zero = sem("b_zero")
        b_xs = sem("b_xs")
        b_tr = sem("b_tr")
        b_xnt = sem("b_xnt")
        b_xst = sem("b_xst")
        b_kv = sem("b_kv")
        b_sq = sem("b_sq")
        b_k = sem("b_k")
        b_ss = sem("b_ss")
        b_ms = sem("b_ms")
        b_sc = sem("b_sc")
        b_rt = sem("b_rt")
        b_rs = sem("b_rs")
        b_vs = sem("b_vs")
        b_dots = sem("b_dots")
        b_w = sem("b_w")
        b_nd = sem("b_nd")
        b_at = sem("b_at")
        b_ats = sem("b_ats")
        b_m = sem("b_m")
        with nc.Block() as block:
            @block.sync
            def _(sp):
                with sp.Fori(0, NBLK) as i:
                    sp.wait_ge(b_tr, i)
                    sp.dma_start(xs[:, :], xn_d[bass.ds(i * P, P), :]).then_inc(b_xs, 16)
                    sp.wait_ge(b_xnt, i + 1)
                    sp.dma_start(xnt_d[bass.ds(i, 1), :, :].rearrange("o p f -> (o p) f"),
                                 xnt[:, :, :].rearrange("p c n -> p (c n)")).then_inc(b_xst, 16)
                sp.wait_ge(b_xst, 16 * NBLK)

            @block.gpsimd
            def _(pool):
                with pool.Fori(1, NBLK + 1) as turn:
                    for u in range(GU):
                        pool.wait_ge(a_zrec, 16)
                        pool.wait_ge(b_pos[u], turn)
                        pool.wait_ge(b_rec[u], turn)
                        for c in range(GC):
                            pool.indirect_dma_start(
                                out=rec_d, out_offset=bass.IndirectOffsetOnAxis(ap=pos[:, u, c:c + 1], axis=0),
                                in_=recs[:, u, c, :], in_offset=None).then_inc(b_scat[u], 16)
                for u in range(GU):
                    pool.wait_ge(b_scat[u], 16 * GC * NBLK)

            @block.scalar
            def _(act):
                act.dma_start(wq[:, :, :], wqkv[0:INNER, :].rearrange("(j p) f -> p j f", p=P)).then_inc(b_w, 16)
                act.dma_start(wot[:, :, :], wout_t.rearrange("(j p) f -> p j f", p=P)).then_inc(b_w, 16)
                act.wait_ge(b_total, 1)
                nc.scalar.copy(base[:, 0, :], pt[:, 0:NBK]).then_inc(b_base, 1)
                with act.Fori(0, NBLK) as i:
                    def stage_records(u):
                        act.wait_ge(b_scat[u], 16 * GC * i)
                        nc.scalar.copy(recs[:, u, :, :], rec[:, bass.ds((i * GU + u) * GC, GC), :]).then_inc(b_rec[u], 1)

                    def copy_total(u):
                        act.wait_ge(b_total, i * GU + u + 2)
                        nc.scalar.copy(base[:, (u + 1) % 2, :], pt[:, 0:NBK]).then_inc(b_base, 1)

                    stage_records(0)
                    act.wait_ge(b_tr, i + 1)
                    act.wait_ge(b_kv, i)
                    act.wait_ge(b_xst, 16 * i)
                    nc.scalar.copy(xnt[:, :, :].rearrange("p c n -> p (c n)"), ptr[:, 0:D]).then_inc(b_xnt, 1)
                    copy_total(0)
                    stage_records(1)
                    act.wait_ge(b_kv, i + 1)
                    act.wait_ge(b_ss, i)
                    for k in range(2):
                        nc.scalar.activation(sq[:, k * H:(k + 1) * H, :].rearrange("p h d -> p (h d)"), pkv[:, k, :],
                                             ACT.Square).then_inc(b_sq, 1)
                    act.wait_ge(b_dots, i)
                    nc.scalar.copy(ksb[:, :], pkv[:, 0, :]).then_inc(b_k, 1)
                    copy_total(1)
                    stage_records(2)
                    act.wait_ge(b_sc, i + 1)
                    nc.scalar.activation(rt[:, :], sc[:, :], ACT.Sqrt).then_inc(b_rt, 1)
                    copy_total(2)
                    stage_records(3)
                    copy_total(3)

            @block.tensor
            def _(pe):
                pe.wait_ge(b_zero, 1)
                nc.tensor.matmul(pt[:, 0:NBK], ident[:, :], base0[:, :], start=True, stop=False,
                                 skip_group_check=True).then_inc(b_total, 1)
                nc.tensor.matmul(pdots[:, :], ident[:, :], zero5[:, :], start=True, stop=False, skip_group_check=True)
                with pe.Fori(0, NBLK) as i:
                    def rank(u):
                        par, k = u % 2, u // 2
                        r = ranks(par)
                        pe.wait_ge(b_oh, i * GU + u + 1)
                        pe.wait_ge(b_prod[par], 2 * i + k)
                        nc.tensor.matmul(r, slt[:, :], oh[:, u, :, :], start=True, stop=False, skip_group_check=True)
                        for s in range(1, GC):
                            nc.tensor.matmul(r[:, s:GC, :], onesb[:, :], oh[:, u, 0:GC - s, :], start=False, stop=False,
                                             skip_group_check=True)
                        pe.wait_ge(b_base, i * GU + u + 1)
                        nc.tensor.matmul(r, ident[:, :], base[:, u % 2, :].unsqueeze(1).to_broadcast(oh_shape),
                                         start=False, stop=True, skip_group_check=True).then_inc(b_ranks, 1)
                        for c in range(GC):
                            last = nc.tensor.matmul(pt[:, 0:NBK], onesb[:, :], oh[:, u, c, :], start=False, stop=False,
                                                    skip_group_check=True)
                        last.then_inc(b_total, 1)

                    pe.wait_ge(b_xs, 16 * (i + 1))
                    pe.wait_ge(b_xnt, i)
                    for c in range(KC):
                        last = nc.tensor.transpose(ptr[:, c * P:(c + 1) * P], xs[:, c * P:(c + 1) * P], ident[:, :])
                    last.then_inc(b_tr, 1)
                    rank(0)
                    pe.wait_ge(b_xnt, i + 1)
                    pe.wait_ge(b_k, i)
                    pe.wait_ge(b_vs, i)
                    for k in range(2):
                        for c in range(KC):
                            last = nc.tensor.matmul(pkv[:, k, :], xnt[:, c, :], wkv[:, c, k * INNER:(k + 1) * INNER],
                                                    start=(c == 0), stop=(c == KC - 1))
                    last.then_inc(b_kv, 1)
                    rank(1)
                    rank(2)
                    pe.wait_ge(b_k, i + 1)
                    pe.wait_ge(b_vs, i + 1)
                    for j in range(NPAIR):
                        last = nc.tensor.matmul(pdots[:, j * P:(j + 1) * P], ksb[:, j * P:(j + 1) * P],
                                                vsb[:, 2 * j:2 * j + 2, :], start=False, stop=False,
                                                skip_group_check=True)
                    last.then_inc(b_dots, 1)
                    rank(3)
                pe.wait_ge(b_nd, 1)
                pe.wait_ge(b_w, 32)
                for j in range(NPAIR):
                    pe.wait_ge(b_ats, j)
                    nc.tensor.matmul(ptr[:, 0:D], ndots[:, j, :], wq[:, j, :], start=True, stop=True).then_inc(b_at, 1)
                pe.wait_ge(b_ats, NPAIR)
                for c in range(KC):
                    for j in range(NPAIR):
                        last = nc.tensor.matmul(pkv[:, c, 0:D], at[:, j, c * P:(c + 1) * P], wot[:, j, :],
                                                start=(j == 0), stop=(j == NPAIR - 1))
                last.then_inc(b_m, 1)

            @block.vector
            def _(dve):
                nc.vector.memset(zero5[:, :], 0.0).then_inc(b_zero, 1)
                nc.vector.memset(ndots[:, :, :], 0.0).then_inc(b_zero, 1)
                with dve.Fori(0, NBLK) as i:
                    def place(u):
                        par, k = u % 2, u // 2
                        dve.wait_ge(b_ranks, i * GU + u + 1)
                        nc.vector.tensor_tensor(prod[:, par, :, :], ranks(par), oh[:, u, :, :],
                                                ALU.mult).then_inc(b_prod[par], 1)
                        dve.wait_ge(b_prod[par], 2 * i + k + 1)
                        dve.wait_ge(b_scat[u], 16 * GC * i)
                        with nc.allow_low_precision(reason="one whole number below 2^24 among zeros"):
                            nc.vector.tensor_reduce(pos[:, u, :], prod[:, par, :, :], AX.X, ALU.add).then_inc(b_pos[u], 1)

                    for u in range(GU):
                        if u == 0:
                            dve.wait_ge(b_total, i * GU + 1)
                        nc.vector.tensor_tensor(oh[:, u, :, :], blk_b((i * GU + u) * GC), iob_b,
                                                ALU.is_equal).then_inc(b_oh, 1)
                    place(0)
                    place(1)
                    dve.wait_ge(b_sq, 2 * i + 2)
                    nc.vector.tensor_reduce(ss[:, :], sq[:, :, :], AX.X, ALU.add).then_inc(b_ss, 1)
                    dve.wait_ge(b_ss, i + 1)
                    nc.vector.tensor_scalar(ms[:, :], ss[:, :], 1.0 / DH, EPS, ALU.mult, ALU.add).then_inc(b_ms, 1)
                    dve.wait_ge(b_ms, i + 1)
                    nc.vector.tensor_tensor(sc[:, :], ms[:, 0:H], ms[:, H:2 * H], ALU.mult).then_inc(b_sc, 1)
                    place(2)
                    dve.wait_ge(b_rt, i + 1)
                    nc.vector.reciprocal(rs[:, :], rt[:, :]).then_inc(b_rs, 1)
                    dve.wait_ge(b_rs, i + 1)
                    dve.wait_ge(b_dots, i)
                    nc.vector.tensor_tensor(vsb[:, :, :], pkv[:, 1, :].rearrange("p (h d) -> p h d", d=DH),
                                            rs[:, :].unsqueeze(2).to_broadcast([P, H, DH]), ALU.mult).then_inc(b_vs, 1)
                    place(3)
                dve.wait_ge(b_dots, NBLK)
                for j in range(NPAIR):
                    for a in range(2):
                        q = slice(a * DH, (a + 1) * DH)
                        last = nc.vector.tensor_scalar(ndots[q, j, q], pdots[q, j * P + a * DH:j * P + (a + 1) * DH],
                                                       1.0 / N, None, ALU.mult)
                last.then_inc(b_nd, 1)
                for j in range(NPAIR):
                    dve.wait_ge(b_at, j + 1)
                    nc.vector.tensor_copy(at[:, j, :], ptr[:, 0:D]).then_inc(b_ats, 1)
                dve.wait_ge(b_m, 1)
                nc.vector.tensor_copy(wx1[:, 0, :], pkv[:, 0, 0:D])
                nc.vector.tensor_copy(wx1[:, 1, :], pkv[:, 1, 0:D])
        phase.close()
        edges.close()

        phase = ExitStack()
        sb, ps = allocator(phase)
        NCH = NT // P
        tl = sb("tl", [P, NCH, P, 4])
        gidx = sb("gidx", [P, NTX], I32)
        place_c = sb("place_c", [P, NTX])
        weight_c = sb("weight_c", [P, NTX])
        idxs = sb("idxs", [P, UT], I32)
        X = sb("X", [P, UT, D])
        ohw = sb("ohw", [P, UT, P])
        gw = sb("gw", [P, KC, D])
        ptf = ps("ptf", [P, 3, 512])
        NPB = 4
        pacc = ps("pacc", [P, NPB, 512])
        c_tl = sem("c_tl")
        c_tr = sem("c_tr")
        c_ev = sem("c_ev")
        c_zero = sem("c_zero")
        c_idx = sems("c_idx", 2)
        c_g = sems("c_g", UT)
        c_xfree = sems("c_xfree", UT)
        c_oh = sem("c_oh")
        c_acc = sems("c_acc", NPB)
        c_last = sem("c_last")
        c_w = sem("c_w")
        HU = UT // 2
        NIT = NT // UT
        with nc.Block() as block:
            @block.sync
            def _(sp):
                sp.dma_start(tl[:, :, :, :], rec_d[0:NT * P, :].rearrange("(c t s) f -> t c s f", t=P, s=P)).then_inc(c_tl, 16)
                sp.dma_start(gw[:, :, :], gnn_w.rearrange("(c p) n -> p c n", p=P)).then_inc(c_w, 16)
                sp.wait_ge(c_w, 16)

            @block.scalar
            def _(act):
                with act.Fori(0, NIT) as i:
                    for hf in range(2):
                        for u in range(hf * HU, (hf + 1) * HU):
                            act.wait_ge(c_g[u], 16 * i)
                        act.wait_ge(c_ev, 3 * NCH + 3)
                        nc.scalar.copy(idxs[:, hf * HU:(hf + 1) * HU],
                                       gidx[:, bass.ds(i * UT + hf * HU, HU)]).then_inc(c_idx[hf], 1)

            @block.gpsimd
            def _(pool):
                with pool.Fori(1, NIT + 1) as turn:
                    for u in range(UT):
                        pool.wait_ge(c_tl, 16)
                        if u % HU == 0:
                            pool.wait_ge(c_idx[u // HU], turn)
                        pool.wait_ge(c_xfree[u], turn)
                        pool.indirect_dma_start(out=X[:, u, :], out_offset=None, in_=xn_d,
                                                in_offset=bass.IndirectOffsetOnAxis(ap=idxs[:, u:u + 1], axis=0)
                                                ).then_inc(c_g[u], 16)

            @block.tensor
            def _(pe):
                pe.wait_ge(c_tl, 16)
                for c in range(NCH):
                    pe.wait_ge(c_ev, 3 * c + 3) if c else None
                    for f in range(3):
                        last = nc.tensor.transpose(ptf[:, f, 0:P], tl[:, c, :, f], ident[:, :])
                    last.then_inc(c_tr, 1)
                for u in range(UT):
                    nc.tensor.sem_inc(c_xfree[u], 1)
                with pe.Fori(0, NIT) as i:
                    for u in range(UT):
                        pe.wait_ge(c_oh, i * UT + u + 1)
                        pe.wait_ge(c_acc[u % NPB], i * (UT // NPB) + u // NPB)
                        pe.wait_ge(c_g[u], 16 * (i + 1))
                        nc.tensor.matmul(pacc[:, u % NPB, 0:D], ohw[:, u, :], X[:, u, :], start=True, stop=True
                                         ).then_inc(c_xfree[u], 1)

            @block.vector
            def _(dve):
                for t in (gidx, place_c, weight_c):
                    nc.vector.memset(t[:, NT:NTX], 0).then_inc(c_ev, 1)
                for k in range(7):
                    last = nc.vector.memset(big[:, k * (NBLK // 7):(k + 1) * (NBLK // 7), :], 0.0)
                last.then_inc(c_zero, 1)
                for c in range(NCH):
                    dve.wait_ge(c_tr, c + 1)
                    for f, t in enumerate((gidx, place_c, weight_c)):
                        nc.vector.tensor_copy(t[:, c * P:(c + 1) * P], ptf[:, f, 0:P]).then_inc(c_ev, 1)

                def onehot(t, u):
                    nc.vector.tensor_scalar(ohw[:, u, :], ion[:, :], place_c[:, bass.ds(t, 1)],
                                            weight_c[:, bass.ds(t, 1)], ALU.is_equal, ALU.mult).then_inc(c_oh, 1)

                dve.wait_ge(c_ev, 3 * NCH + 3)
                dve.wait_ge(c_zero, 1)
                for u in range(UT):
                    onehot(u, u)
                with dve.Fori(0, NIT) as i:
                    _, blocks = nc.values_load_multi_w_load_instructions(
                        tblk[0:1, bass.ds(i * UT, UT)], engines=[mybir.EngineType.DVE], min_val=0, max_val=NBLK - 1)
                    for u in range(UT):
                        dst_ = big[:, bass.ds(blocks[u], 1), :].rearrange("p a b -> p (a b)")
                        dve.wait_ge(c_xfree[u], i + 2)
                        dve.wait_ge(c_last, i * UT + u)
                        ins = nc.vector.tensor_tensor(dst_, pacc[:, u % NPB, 0:D], dst_, ALU.add)
                        ins.then_inc(c_acc[u % NPB], 1)
                        onehot(i * UT + u + UT, u)
                        dve.wait_ge(c_acc[u % NPB], i * (UT // NPB) + u // NPB + 1)
                        nc.vector.sem_inc(c_last, 1)
        phase.close()

        phase = ExitStack()
        sb, ps = allocator(phase)
        xr = sb("xr", [P, 2, D])
        xt = sb("xt", [P, 2, D])
        en = sb("en", [P, 2, D])
        et = sb("et", [P, 2, D])
        gw2 = sb("gw2", [P, KC, D])
        px = ps("px", [P, 2, 512])
        pet = ps("pet", [P, 2, 512])
        d_w = sem("d_w")
        d_wm = sem("d_wm")
        d_x = sems("d_x", 2)
        d_en = sems("d_en", 2)
        d_tr = sems("d_tr", 2)
        d_et = sems("d_et", 2)
        d_mm = sems("d_mm", 2)
        d_add = sems("d_add", 2)
        d_st = sem("d_st")
        d_z = sem("d_z")
        d_chain = sem("d_chain")
        d_b2 = sem("d_b2")
        d_var = sem("d_var")
        d_sqrt = sem("d_sqrt")
        rows = sb("rows_d", [3, D])
        sp1 = sb("sp1_d", [3, D])
        sp2 = sb("sp2_d", [3, D])
        sp3 = sb("sp3_d", [3, D])
        assert NBLK % 2 == 0
        with nc.Block() as block:
            @block.sync
            def _(sp):
                sp.dma_start(gw2[:, :, :], gnn_w.rearrange("(c p) n -> p c n", p=P)).then_inc(d_w, 16)
                sp.dma_start(rows[:, :], b_out.partition_broadcast(3)).then_inc(d_b2, 16)

                def load(b, par, real):
                    sp.dma_start(xt[:, par, :], xnt_d[bass.ds(b, 1), :, :].rearrange("o p f -> (o p) f")
                                 ).then_inc(d_x[par], 16)
                    if real == P:
                        sp.dma_start(xr[:, par, :], x[bass.ds(b * P, P), :]).then_inc(d_x[par], 16)
                    else:
                        sp.wait_ge(d_z, 1)
                        sp.dma_start(xr[0:real, par, :], x[N - real:N, :]).then_inc(d_x[par], 16)

                with sp.Fori(0, NBLK // 2 - 1) as i:
                    for par in range(2):
                        sp.wait_ge(d_add[par], i)
                        load(i * 2 + par, par, P)
                sp.wait_ge(d_add[0], NBLK // 2 - 1)
                load(NBLK - 2, 0, P)
                sp.wait_ge(d_add[1], NBLK // 2 - 1)
                load(NBLK - 1, 1, LAST)

            @block.scalar
            def _(act):
                with act.Fori(0, NBLK // 2) as i:
                    for par in range(2):
                        act.wait_ge(d_tr[par], i)
                        nc.scalar.copy(en[:, par, :], big[:, bass.ds(i * 2 + par, 1), :].rearrange("p a b -> p (a b)")
                                       ).then_inc(d_en[par], 1)
                        act.wait_ge(d_tr[par], i + 1)
                        act.wait_ge(d_mm[par], i)
                        nc.scalar.copy(et[:, par, :], pet[:, par, 0:D]).then_inc(d_et[par], 1)
                act.wait_ge(d_var, 1)
                nc.scalar.activation(rstd[:, :], rstd[:, :], ACT.Sqrt).then_inc(d_sqrt, 1)

            @block.tensor
            def _(pe):
                pe.wait_ge(d_wm, 1)
                with pe.Fori(0, NBLK // 2) as i:
                    for par in range(2):
                        pe.wait_ge(d_et[par], i)
                        pe.wait_ge(d_en[par], i + 1)
                        for c in range(KC):
                            last = nc.tensor.transpose(pet[:, par, c * P:(c + 1) * P], en[:, par, c * P:(c + 1) * P],
                                                       ident[:, :])
                        last.then_inc(d_tr[par], 1)
                        pe.wait_ge(d_add[par], i)
                        nc.tensor.matmul(px[:, par, 0:D], ones3[:, :], b1_3[:, :], start=True, stop=False)
                        pe.wait_ge(d_x[par], 32 * (i + 1))
                        for c in range(KC):
                            nc.tensor.matmul(px[:, par, 0:D], xt[:, par, c * P:(c + 1) * P], wx1[:, c, :],
                                             start=False, stop=False)
                        pe.wait_ge(d_et[par], i + 1)
                        for c in range(KC):
                            last = nc.tensor.matmul(px[:, par, 0:D], et[:, par, c * P:(c + 1) * P], wx1[:, KC + c, :],
                                                    start=False, stop=(c == KC - 1))
                        last.then_inc(d_mm[par], 1)

            @block.vector
            def _(dve):
                link = Chain(dve, d_chain)
                dve.wait_ge(d_w, 16)
                nc.vector.tensor_tensor(wx1[:, 0:KC, :], wx1[:, 0:KC, :], gw2[:, :, :], ALU.add).then_inc(d_wm, 1)
                dve.wait_ge(d_b2, 16)
                split_rows(link, nc.vector, b2_3[:, :], rows[:, :], ident, sp1[:, :], sp2[:, :], sp3[:, :])

                def add(b, par, n):
                    dve.wait_ge(d_mm[par], n + 1)
                    row = big[:, bass.ds(b, 1), :].rearrange("p a b -> p (a b)")
                    nc.vector.tensor_tensor(row, px[:, par, 0:D], xr[:, par, :], ALU.add).then_inc(d_add[par], 1)
                    dve.wait_ge(d_add[par], n + 1)
                    dve.wait_ge(d_w, 16)
                    nc.vector.bn_stats(stats[:, bass.ds(b, 1), :].rearrange("p a b -> p (a b)"), row).then_inc(d_st, 1)

                with dve.Fori(0, NBLK // 2 - 1) as i:
                    for par in range(2):
                        add(i * 2 + par, par, i)
                nc.vector.memset(xr[64:P, 1, :], 0.0).then_inc(d_z, 1)
                add(NBLK - 2, 0, NBLK // 2 - 1)
                add(NBLK - 1, 1, NBLK // 2 - 1)
                dve.wait_ge(d_st, NBLK)
                norm_stats(link, nc.vector, stats, lnt, rstd[:, :])
                nc.vector.tensor_scalar(nmr[:, :], lnt[:, 0, :], -0.5, None, ALU.mult).then_inc(d_var, 1)
                dve.wait_ge(d_sqrt, 1)
                link(nc.vector.reciprocal(rstd[:, :], rstd[:, :]))
                link(nc.vector.tensor_tensor(rstd[:, :], rstd[:, :], mask[:, :], ALU.mult))
                link(nc.vector.tensor_tensor(nmr[:, :], nmr[:, :], rstd[:, :], ALU.mult))
        phase.close()

        sb, _ = allocator(ctx)
        sfx = sb("sfx", [P, NPAIR, D])
        snorm = sb("snorm", [P, NPAIR])
        pmat = sb("pmat", [P, NPAIR, D])

        phase = ExitStack()
        sb, ps = allocator(phase)
        ya = sb("ya", [P, 2, D])
        yt = sb("yt", [P, 2, D])
        mx = sb("mx", [P, 2, H])
        sh = sb("sh", [P, 2, H, G])
        ex = sb("ex", [P, 2, H, G])
        sm = sb("sm", [P, 2, H])
        rc = sb("rc", [P, 2, H])
        sw = sb("sw", [P, 2, H, G])
        swt = sb("swt", [P, 2, INNER])
        zero5 = sb("zero5e", [P, INNER])
        pyt = ps("pyt", [P, 512])
        pl = ps("pl", [P, 2, 512])
        psw = ps("psw", [P, 512])
        pS = ps("pS", [P, NPAIR, D])
        pn = ps("pn", [P, 512])
        e_z = sem("e_z")
        e_y = sem("e_y")
        e_yt = sem("e_yt")
        e_yts = sem("e_yts")
        e_log = sems("e_log", 2)
        e_mx = sem("e_mx")
        e_sh = sems("e_sh", 2)
        e_ex = sem("e_ex")
        e_sm = sem("e_sm")
        e_rc = sem("e_rc")
        e_sw = sem("e_sw")
        e_swt = sem("e_swt")
        e_swts = sem("e_swts")
        e_S = sems("e_S", 2)
        e_st = sems("e_st", 2)
        e_end = sem("e_end")

        def b3(t):
            return t.unsqueeze(2).to_broadcast([P, H, G])

        with nc.Block() as block:
            @block.sync
            def _(sp):
                with sp.Fori(0, NBLK // 2) as i:
                    for par in range(2):
                        sp.wait_ge(e_swts, 2 * i + par + 1)
                        sp.dma_start(swt_d[bass.ds(i * 2 + par, 1), :, :].rearrange("o p f -> (o p) f"),
                                     swt[:, par, :]).then_inc(e_st[par], 16)
                for par in range(2):
                    sp.wait_ge(e_st[par], 8 * NBLK)

            @block.scalar
            def _(act):
                with act.Fori(0, NBLK // 2) as i:
                    for par in range(2):
                        t = 2 * i + par
                        act.wait_ge(e_S[par], i)
                        act.wait_ge(e_z, 1)
                        nc.scalar.activation(ya[:, par, :], big[:, bass.ds(t, 1), :].rearrange("p a b -> p (a b)"),
                                             ACT.Identity, bias=nmr[:, bass.ds(t, 1)],
                                             scale=rstd[:, bass.ds(t, 1)]).then_inc(e_y, 1)
                        act.wait_ge(e_yt, t + 1)
                        act.wait_ge(e_log[par], i)
                        nc.scalar.copy(yt[:, par, :], pyt[:, 0:D]).then_inc(e_yts, 1)
                        act.wait_ge(e_sh[par], i + 1)
                        act.wait_ge(e_sw, t)
                        nc.scalar.activation(ex[:, par, :, :], sh[:, par, :, :], ACT.Exp).then_inc(e_ex, 1)
                        act.wait_ge(e_swt, t + 1)
                        act.wait_ge(e_st[par], 16 * i)
                        nc.scalar.copy(swt[:, par, :], psw[:, :]).then_inc(e_swts, 1)

            @block.tensor
            def _(pe):
                pe.wait_ge(e_z, 1)
                for k in range(2):
                    nc.tensor.matmul(pS[:, 2 * k:2 * k + 2, :], ident[:, :], zero5[:, :], start=True, stop=False,
                                     skip_group_check=True)
                nc.tensor.matmul(pn[:, 0:NPAIR], ident[:, :], zero5[:, 0:NPAIR], start=True, stop=False,
                                 skip_group_check=True)
                with pe.Fori(0, NBLK // 2) as i:
                    for par in range(2):
                        t = 2 * i + par
                        pe.wait_ge(e_yts, t)
                        pe.wait_ge(e_y, t + 1)
                        for c in range(KC):
                            last = nc.tensor.transpose(pyt[:, c * P:(c + 1) * P], ya[:, par, c * P:(c + 1) * P],
                                                       ident[:, :])
                        last.then_inc(e_yt, 1)
                        pe.wait_ge(e_sh[par], i)
                        nc.tensor.matmul(pl[:, par, :], ones3[:, :], bl_3[:, :], start=True, stop=False)
                        pe.wait_ge(e_yts, t + 1)
                        for c in range(KC):
                            last = nc.tensor.matmul(pl[:, par, :], yt[:, par, c * P:(c + 1) * P], wls[:, c, :],
                                                    start=False, stop=(c == KC - 1))
                        last.then_inc(e_log[par], 1)
                        pe.wait_ge(e_swts, t)
                        pe.wait_ge(e_sw, t + 1)
                        for j in range(NPAIR):
                            last = nc.tensor.transpose(psw[:, j * P:(j + 1) * P], sw[:, par, 2 * j:2 * j + 2, :],
                                                       ident[:, :])
                        last.then_inc(e_swt, 1)
                        for j in range(NPAIR):
                            nc.tensor.matmul(pS[:, j, :], sw[:, par, 2 * j:2 * j + 2, :], ya[:, par, :],
                                             start=False, stop=False, skip_group_check=True)
                            last = nc.tensor.matmul(pn[:, j:j + 1], sw[:, par, 2 * j:2 * j + 2, :],
                                                    mask[:, bass.ds(t, 1)], start=False, stop=False,
                                                    skip_group_check=True)
                        last.then_inc(e_S[par], 1)

            @block.vector
            def _(dve):
                nc.vector.memset(zero5[:, :], 0.0).then_inc(e_z, 1)
                with dve.Fori(0, NBLK // 2) as i:
                    for par in range(2):
                        t = 2 * i + par
                        lg = pl[:, par, :].rearrange("p (h g) -> p h g", g=G)
                        dve.wait_ge(e_log[par], i + 1)
                        nc.vector.tensor_reduce(mx[:, par, :], lg, AX.X, ALU.max).then_inc(e_mx, 1)
                        dve.wait_ge(e_mx, t + 1)
                        nc.vector.tensor_tensor(sh[:, par, :, :], lg, b3(mx[:, par, :]), ALU.subtract
                                                ).then_inc(e_sh[par], 1)
                        dve.wait_ge(e_ex, t + 1)
                        nc.vector.tensor_reduce(sm[:, par, :], ex[:, par, :, :], AX.X, ALU.add).then_inc(e_sm, 1)
                        dve.wait_ge(e_sm, t + 1)
                        nc.vector.reciprocal(rc[:, par, :], sm[:, par, :]).then_inc(e_rc, 1)
                        dve.wait_ge(e_rc, t + 1)
                        dve.wait_ge(e_S[par], i)
                        nc.vector.tensor_tensor(sw[:, par, :, :], ex[:, par, :, :], b3(rc[:, par, :]), ALU.mult
                                                ).then_inc(e_sw, 1)
                for par in range(2):
                    dve.wait_ge(e_S[par], NBLK // 2)
                nc.vector.tensor_copy(sfx[:, :, :], pS[:, :, :])
                nc.vector.tensor_copy(snorm[:, :], pn[:, 0:NPAIR])
        phase.close()

        phase = ExitStack()
        sb, ps = allocator(phase)
        wfx = sb("wfx", [P, KC, INNER])
        bfx = sb("bfx", [P, INNER])
        wo = sb("wo", [P, NPAIR, D])
        w2 = sb("w2", [P, 3, P])
        st_ = sb("st_", [P, KC, P])
        tok = sb("tok", [P, P])
        tb2 = sb("tb2", [P, P])
        den = sb("den", [P, NPAIR])
        rden = sb("rden", [P, NPAIR])
        tt = sb("tt", [P, P])
        qt = sb("qt", [P, 3, P])
        am = sb("am", [P, G])
        mxf = sb("mxf", [P, 1])
        smf = sb("smf", [P, 1])
        rcf = sb("rcf", [P, 1])
        ab = sb("ab", [P, P])
        abt = sb("abt", [P, P])
        vw = sb("vw", [P, D])
        pa = ps("pa", [P, 512])
        pb = ps("pb", [P, 512])
        pc = ps("pc", [P, 512])
        f_w = sem("f_w")
        f_z = sem("f_z")
        f_pe = sem("f_pe")
        f_chain = sem("f_chain")
        f_exp = sem("f_exp")
        f_sh = sem("f_sh")
        with nc.Block() as block:
            @block.sync
            def _(sp):
                sp.dma_start(wfx[:, :, :], w_fx.rearrange("(c p) n -> p c n", p=P)).then_inc(f_w, 16)
                sp.dma_start(bfx[:, :], b_fx.partition_broadcast(P)).then_inc(f_w, 16)
                sp.dma_start(wo[:, :, :], w_out.rearrange("(j p) n -> p j n", p=P)).then_inc(f_w, 16)
                sp.wait_ge(f_z, 1)
                for k, w in enumerate((w_q, w_k, w_v)):
                    for a in range(2):
                        q = slice(a * DH, (a + 1) * DH)
                        sp.dma_start(w2[q, k, q], w).then_inc(f_w, 16)
                sp.wait_ge(f_w, 9 * 16)

            TURNS = 7

            @block.tensor
            def _(pe):
                pe.wait_ge(f_w, 9 * 16)
                for j in range(NPAIR):
                    def turn(k):
                        pe.wait_ge(f_sh, j * TURNS + k)

                    turn(0)
                    for c in range(KC):
                        last = nc.tensor.transpose(pa[:, c * P:(c + 1) * P], sfx[:, j, c * P:(c + 1) * P], ident[:, :])
                    last.then_inc(f_pe, 1)
                    turn(1)
                    for c in range(KC):
                        last = nc.tensor.matmul(pb[:, 0:P], st_[:, c, :], wfx[:, c, j * P:(j + 1) * P],
                                                start=(c == 0), stop=(c == KC - 1))
                    last.then_inc(f_pe, 1)
                    turn(2)
                    nc.tensor.transpose(pa[:, 0:P], tb2[:, :], ident[:, :]).then_inc(f_pe, 1)
                    turn(3)
                    for k in range(3):
                        last = nc.tensor.matmul(pb[:, k * P:(k + 1) * P], w2[:, k, :], tt[:, :], start=True, stop=True)
                    last.then_inc(f_pe, 1)
                    turn(4)
                    nc.tensor.matmul(pa[:, 0:P], qt[:, 0, :], qt[:, 1, :], start=True, stop=True)
                    nc.tensor.matmul(pc[:, 0:D], qt[:, 2, :], wo[:, j, :], start=True, stop=True).then_inc(f_pe, 1)
                    turn(5)
                    nc.tensor.transpose(pb[:, 0:P], ab[:, :], ident[:, :]).then_inc(f_pe, 1)
                    turn(6)
                    nc.tensor.matmul(pa[:, 0:D], abt[:, :], vw[:, :], start=True, stop=True).then_inc(f_pe, 1)

            @block.scalar
            def _(act):
                for j in range(NPAIR):
                    act.wait_ge(f_exp, 2 * j + 1)
                    nc.scalar.activation(am[:, :], am[:, :], ACT.Exp).then_inc(f_exp, 1)

            @block.vector
            def _(dve):
                link = Chain(dve, f_chain)
                nc.vector.memset(w2[:, :, :], 0.0).then_inc(f_z, 1)
                nc.vector.memset(tb2[:, :], 0.0)
                link(nc.vector.memset(ab[:, :], 0.0))
                dve.wait_ge(f_w, 9 * 16)
                link(nc.vector.tensor_scalar(den[:, :], snorm[:, :], EPS, None, ALU.add))
                link(nc.vector.reciprocal(rden[:, :], den[:, :]))
                for j in range(NPAIR):
                    def turn(k):
                        dve.wait_ge(f_pe, j * TURNS + k + 1)

                    turn(0)
                    nc.vector.tensor_copy(st_[:, :, :].rearrange("p c n -> p (c n)"), pa[:, 0:D]).then_inc(f_sh, 1)
                    turn(1)
                    link(nc.vector.scalar_tensor_tensor(out=tok[:, :], in0=bfx[:, j * P:(j + 1) * P],
                                                        scalar=snorm[:, j:j + 1], in1=pb[:, 0:P],
                                                        op0=ALU.mult, op1=ALU.add))
                    for a in range(2):
                        q = slice(a * DH, (a + 1) * DH)
                        last = nc.vector.tensor_scalar(tb2[q, q], tok[q, q], rden[q, j:j + 1], None, ALU.mult)
                    last.then_inc(f_sh, 1)
                    turn(2)
                    nc.vector.tensor_copy(tt[:, :], pa[:, 0:P]).then_inc(f_sh, 1)
                    turn(3)
                    nc.vector.tensor_copy(qt[:, :, :].rearrange("p c n -> p (c n)"), pb[:, 0:3 * P]).then_inc(f_sh, 1)
                    turn(4)
                    link(nc.vector.tensor_copy(vw[:, :], pc[:, 0:D]))
                    for a in range(2):
                        q = slice(a * DH, (a + 1) * DH)
                        link(nc.vector.tensor_scalar(am[q, :], pa[q, a * DH:(a + 1) * DH], DH ** -0.5, None, ALU.mult))
                    link(nc.vector.tensor_reduce(mxf[:, :], am[:, :], AX.X, ALU.max))
                    nc.vector.tensor_scalar(am[:, :], am[:, :], mxf[:, :], None, ALU.subtract).then_inc(f_exp, 1)
                    dve.wait_ge(f_exp, 2 * j + 2)
                    link(nc.vector.tensor_reduce(smf[:, :], am[:, :], AX.X, ALU.add))
                    link(nc.vector.reciprocal(rcf[:, :], smf[:, :]))
                    for a in range(2):
                        q = slice(a * DH, (a + 1) * DH)
                        last = nc.vector.tensor_scalar(ab[q, q], am[q, :], rcf[q, :], None, ALU.mult)
                    last.then_inc(f_sh, 1)
                    turn(5)
                    nc.vector.tensor_copy(abt[:, :], pb[:, 0:P]).then_inc(f_sh, 1)
                    turn(6)
                    nc.vector.tensor_copy(pmat[:, j, :], pa[:, 0:D]).then_inc(f_sh, 1)
        phase.close()

        phase = ExitStack()
        sb, ps = allocator(phase)
        NB4 = 4
        st4 = sb("st4", [P, NB4, INNER])
        ob = sb("ob", [P, 2, D])
        po = ps("po", [P, 2, 512])
        g_l = sems("g_l", NB4)
        g_mm = sem("g_mm")
        g_o = sem("g_o")
        g_st = sems("g_st", 2)
        NG4 = NBLK // NB4
        with nc.Block() as block:
            @block.sync
            def _(sp):
                def load(t, q):
                    sp.dma_start(st4[:, q, :], swt_d[bass.ds(t, 1), :, :].rearrange("o p f -> (o p) f")
                                 ).then_inc(g_l[q], 16)

                for q in range(NB4):
                    load(q, q)
                with sp.Fori(0, NG4 - 1) as i:
                    for q in range(NB4):
                        sp.wait_ge(g_mm, i * NB4 + q + 1)
                        load(i * NB4 + q + NB4, q)
                for q in range(NBLK - NG4 * NB4):
                    sp.wait_ge(g_mm, (NG4 - 1) * NB4 + q + 1)
                    load(NG4 * NB4 + q, q)

            @block.gpsimd
            def _(pool):
                def store(t, par, n, rows_):
                    pool.wait_ge(g_o, n)
                    pool.wait_ge(g_l[0], 16)
                    if rows_ == P:
                        pool.dma_start(out[bass.ds(t * P, P), :], ob[:, par, :]).then_inc(g_st[par], 16)
                    else:
                        pool.dma_start(out[N - rows_:N, :], ob[0:rows_, par, :]).then_inc(g_st[par], 16)

                with pool.Fori(0, NBLK // 2 - 1) as i:
                    for par in range(2):
                        store(2 * i + par, par, 2 * i + par + 1, P)
                store(NBLK - 2, 0, NBLK - 1, P)
                store(NBLK - 1, 1, NBLK, LAST)
                for par in range(2):
                    pool.wait_ge(g_st[par], 16 * (NBLK // 2))

            def product(pe, t, q, n):
                pe.wait_ge(g_o, t - 1) if not isinstance(t, int) or t > 1 else None
                nc.tensor.matmul(po[:, q % 2, 0:D], ones3[:, :], b2_3[:, :], start=True, stop=False)
                pe.wait_ge(g_l[q], n)
                for j in range(NPAIR):
                    last = nc.tensor.matmul(po[:, q % 2, 0:D], st4[:, q, j * P:(j + 1) * P], pmat[:, j, :],
                                            start=False, stop=(j == NPAIR - 1))
                last.then_inc(g_mm, 1)

            @block.tensor
            def _(pe):
                for q in range(NB4):
                    product(pe, q, q, 16)
                with pe.Fori(1, NG4) as i:
                    for q in range(NB4):
                        product(pe, i * NB4 + q, q, 16 * (i + 1))
                for q in range(NBLK - NG4 * NB4):
                    product(pe, NG4 * NB4 + q, q, 16 * (NG4 + 1))

            @block.vector
            def _(dve):
                with dve.Fori(0, NBLK // 2) as i:
                    for par in range(2):
                        t = 2 * i + par
                        dve.wait_ge(g_mm, t + 1)
                        dve.wait_ge(g_st[par], 16 * i)
                        nc.vector.tensor_tensor(ob[:, par, :], po[:, par, 0:D],
                                                big[:, bass.ds(t, 1), :].rearrange("p a b -> p (a b)"), ALU.add
                                                ).then_inc(g_o, 1)
        phase.close()


def kernel(**inputs):
    import numpy as np
    import concourse.bacc as bacc
    from concourse.bass_utils import run_bass_kernel_spmd

    a = {k.replace("L0_", ""): np.asarray(v) for k, v in inputs.items()}
    wqkv = a["mix_Wqkv"]
    arrays = {
        "x": a["x"], "src": a["src"], "dst": a["dst"], "edge_weight": a["edge_weight"],
        "gnn_w": a["gnn_weight"], "gnn_diag": a["gnn_learnable_diag"], "gnn_b": a["gnn_bias"],
        "wqkv": wqkv, "wqkv_t": wqkv.T, "wout_t": a["mix_Wout"].T, "bout": a["mix_bout"],
        "w_fx": a["ffn_W_fx"], "b_fx": a["ffn_b_fx"], "w_x_t": a["ffn_W_x"].T, "b_x": a["ffn_b_x"],
        "w_slice": a["ffn_W_slice"], "b_slice": a["ffn_b_slice"], "w_q": a["ffn_W_q"], "w_k": a["ffn_W_k"],
        "w_v": a["ffn_W_v"], "w_out": a["ffn_W_out"], "b_out": a["ffn_b_out"],
        "temp": a["ffn_temperature"].reshape(-1),
    }
    nc = bacc.Bacc("TRN2", target_bir_lowering=False, num_devices=1)
    arrays = {f"in_{k}": np.ascontiguousarray(v) for k, v in arrays.items()}
    aps = [nc.dram_tensor(k, v.shape, mybir.dt.from_np(v.dtype), kind="ExternalInput").ap() for k, v in arrays.items()]
    out = nc.dram_tensor("out_x", (N, D), F32, kind="ExternalOutput").ap()
    gps_layer(nc, *aps, out)
    r = run_bass_kernel_spmd(nc, [arrays], core_ids=[0])
    return r.results[0]["out_x"]
```

```python
from contextlib import ExitStack

import concourse.bass as bass
from concourse import mybir

F32 = mybir.dt.float32
BF16 = mybir.dt.bfloat16
I32 = mybir.dt.int32
ALU = mybir.AluOpType
ACT = mybir.ActivationFunctionType
AX = mybir.AxisListType

P = 128
N, D = 12500, 256
E = 200000
H, DH, G = 8, 64, 64
INNER = H * DH
NPAIR = H // 2
NBLK = -(-N // P)
LAST = N - (NBLK - 1) * P
NPAD = NBLK * P
EPS = 1e-5
KC = D // P

GC = 4
GU = 4
NGRP = NBLK * GU
ECOL = NGRP * GC
EFULL = E // P
NBK = NBLK + 1
NLO = 8
NHI = -(-NBK // NLO)
CG = 8
TMAX = (E + NBLK * (P - 1)) // P
RT = -(-TMAX // NBLK)
NTILE = NBLK * RT
NT = -(-TMAX // P) * P
NTX = NT + 2 * RT
LAG = 2
assert (ECOL * P - E) // P + 1 + TMAX <= NTX and NTILE + RT <= NTX
assert ECOL >= EFULL + 1 and ECOL % (2 * CG) == 0


class Chain:

    def __init__(self, engine, sem):
        self.engine, self.sem, self.n = engine, sem, 0

    def __call__(self, instruction):
        self.n += 1
        instruction.then_inc(self.sem, 1)
        self.engine.wait_ge(self.sem, self.n)


def split_rows(link, vec, out, rows, masks, t1, t2, acc):
    n = rows.shape[1]
    b = out
    link(vec.tensor_copy(b, rows))
    link(vec.tensor_tensor(t1, rows, b, ALU.subtract))
    link(vec.tensor_scalar(acc, b, masks[0:3, 0:1], None, ALU.mult))
    link(vec.tensor_copy(b, t1))
    link(vec.tensor_tensor(t2, t1, b, ALU.subtract))
    link(vec.scalar_tensor_tensor(out=acc, in0=b, scalar=masks[0:3, 1:2], in1=acc, op0=ALU.mult, op1=ALU.add))
    link(vec.scalar_tensor_tensor(out=acc, in0=t2, scalar=masks[0:3, 2:3], in1=acc, op0=ALU.mult, op1=ALU.add))
    link(vec.tensor_copy(b, acc))


def gps_layer(nc, x, src, dst, edge_weight, gnn_w, gnn_diag, gnn_b, wqkv, wqkv_t, wout_t, bout,
              w_fx, b_fx, w_x_t, b_x, w_slice, b_slice, w_q, w_k, w_v, w_out, b_out, temp, out):
    with ExitStack() as ctx:
        def allocator(stack):
            def sb(name, shape, dt=F32):
                return stack.enter_context(nc.sbuf_tensor(name, shape, dt))

            def ps(name, shape, dt=F32):
                return stack.enter_context(nc.psum_tensor(name, shape, dt))
            return sb, ps

        def sem(name):
            return ctx.enter_context(nc.semaphore(name))

        def sems(name, n):
            return [sem(f"{name}{k}") for k in range(n)]

        xn_d = nc.dram_tensor("xn_table", (NPAD, D), F32).ap()
        xnt_d = nc.dram_tensor("xn_transposed", (NBLK, P, D), F32).ap()
        rec_d = nc.dram_tensor("sorted_edges", (NTX * P, 4), F32).ap()
        tb_d = nc.dram_tensor("tile_blocks", (NTX,), I32).ap()
        swt_d = nc.dram_tensor("slice_weights_t", (NBLK, P, INNER), F32).ap()

        sb, _ = allocator(ctx)
        big = sb("big", [P, NBLK, D])
        ident = sb("ident", [P, P])
        ones3 = sb("ones3", [3, P], BF16)
        mask = sb("mask", [P, NBLK])
        tblk = sb("tblk", [1, NTX], I32)
        apart = sb("apart", [1, 1], I32)
        base0 = sb("base0", [P, NBK])
        slt = sb("slt", [P, P], BF16)
        onesb = sb("onesb", [P, P], BF16)
        iob = sb("iob", [P, NBK], BF16)
        ion = sb("ion", [P, P])
        wx1 = sb("wx1", [P, 2 * KC, D])
        b2_3 = sb("b2_3", [3, D], BF16)

        def row_of(t):
            return big[:, bass.ds(t, 1), :].rearrange("p a b -> p (a b)")

        passed = sem("passed")

        edges = ExitStack()
        esb, _ = allocator(edges)
        rec = esb("rec", [P, ECOL, 4])
        blk = esb("blk", [P, ECOL], BF16)
        zer = esb("zer", [P, 512])
        ohz = esb("ohz", [P, CG * NLO], BF16)
        oh_shape = [P, GC, NBK]

        phase = ExitStack()
        sb, ps = allocator(phase)
        NCG = ECOL // CG
        CB = 14
        NCB = NCG // CB
        assert NCB * CB == NCG and NCB % 2 == 0
        srci = sb("srci", [P, ECOL], I32)
        dsti = sb("dsti", [P, ECOL], I32)
        wf = sb("wf", [P, ECOL])
        hi = sb("hi", [P, ECOL], I32)
        lo = sb("lo", [P, ECOL], I32)
        ohh = sb("ohh", [P, 2, CB * CG, NHI], BF16)
        ohl = sb("ohl", [P, 2, CB * CG, NLO], BF16)
        io13 = sb("io13", [P, NHI])
        io8 = sb("io8", [P, NLO])
        dmask = sb("dmask", [CG * NHI, CG, NLO])
        hsel = sb("hsel", [CG * NHI, CG, NHI])
        hmask = sb("hmask", [CG * NHI, NHI])
        cdiag = sb("cdiag", [CG * NHI, CG, NLO])
        csum = sb("csum", [CG * NHI, NLO])
        cspread = sb("cspread", [CG * NHI, NHI, NLO])
        onesf = sb("onesf", [CG * NHI, P])
        ntl = sb("ntl", [P, NBK], I32)
        ntf = sb("ntf", [P, NBK])
        incl = sb("incl", [P, NBK])
        excl = sb("excl", [P, NBK])
        onek = sb("onek", [P, NBK])
        limit = sb("limit", [P, NBLK])
        over = sb("over", [P, NBLK])
        tno = sb("tno", [P, NT // P])
        tcm = sb("tcm", [P, NT // P, NBLK])
        tbf = sb("tbf", [P, NT // P])
        tbi = sb("tbi", [P, NT // P], I32)
        pc2 = ps("pc2", [CG * NHI, CG, NLO])
        pcnt = ps("pcnt", [P, NHI, NLO])

        a_src = sem("a_src")
        a_rest = sem("a_rest")
        a_pads = sem("a_pads")
        a_zero = sem("a_zero")
        a_zrec = sem("a_zrec")
        a_pool = sem("a_pool")
        a_poolc = sem("a_poolc")
        a_recz = sem("a_recz")
        a_chain = sem("a_chain")
        a_oh = sem("a_oh")
        a_ohfree = sems("a_ohfree", 2)
        a_pairs = sem("a_pairs")
        a_spread = sem("a_spread")
        a_cnt = sem("a_cnt")
        a_tb = sem("a_tb")
        a_tbd = sem("a_tbd")
        a_tbl = sem("a_tbl")
        NPOOL = 15
        zfull = NTX * 4 // 512

        with nc.Block() as block:
            @block.sync
            def _(sp):
                sp.dma_start(srci[:, 0:EFULL], src[0:EFULL * P].rearrange("(p c) -> p c", p=P)).then_inc(a_src, 16)
                sp.wait_ge(a_pads, 1)
                sp.dma_start(srci[0:E - EFULL * P, EFULL:EFULL + 1],
                             src[EFULL * P:E].rearrange("(p o) -> p o", o=1)).then_inc(a_src, 16)
                sp.dma_start(dsti[:, 0:EFULL], dst[0:EFULL * P].rearrange("(p c) -> p c", p=P)).then_inc(a_rest, 16)
                sp.dma_start(dsti[0:E - EFULL * P, EFULL:EFULL + 1],
                             dst[EFULL * P:E].rearrange("(p o) -> p o", o=1)).then_inc(a_rest, 16)
                sp.dma_start(wf[:, 0:EFULL],
                             edge_weight[0:EFULL * P].rearrange("(p c) -> p c", p=P)).then_inc(a_rest, 16)
                sp.dma_start(wf[0:E - EFULL * P, EFULL:EFULL + 1],
                             edge_weight[EFULL * P:E].rearrange("(p o) -> p o", o=1)).then_inc(a_rest, 16)
                sp.wait_ge(a_tb, 1)
                sp.dma_start(tb_d[0:NT].rearrange("(p j) -> p j", p=P), tbi[:, :]).then_inc(a_tbd, 16)
                sp.wait_ge(a_tbd, 16)
                sp.dma_start(tblk[0:1, 0:NT], tb_d[0:NT].rearrange("(o t) -> o t", o=1)).then_inc(a_tbl, 16)
                sp.wait_ge(a_tbl, 16)

            @block.gpsimd
            def _(pool):
                def number(out_, n, step=0):
                    pool.iota(out_, pattern=[[1, n]], base=0, channel_multiplier=step,
                              allow_small_or_imprecise_dtypes=True).then_inc(a_pool, 1)

                number(io13[:, :], NHI)
                number(io8[:, :], NLO)
                number(iob[:, :], NBK)
                number(ion[:, :], P)
                number(tno[:, :], NT // P, NT // P)
                pool.iota(limit[:, :], pattern=[[RT, NBLK]], base=RT * LAG, channel_multiplier=0,
                          allow_small_or_imprecise_dtypes=True).then_inc(a_pool, 1)
                pool.memset(onesb[:, :], 1.0).then_inc(a_pool, 1)
                pool.memset(onesf[:, :], 1.0).then_inc(a_pool, 1)
                pool.memset(ones3[:, :], 1.0).then_inc(a_pool, 1)
                pool.memset(onek[:, :], 1.0).then_inc(a_pool, 1)
                pool.memset(ident[:, :], 0.0).then_inc(a_poolc, 1)
                pool.memset(slt[:, :], 1.0).then_inc(a_poolc, 1)
                pool.memset(mask[:, :], 1.0).then_inc(a_poolc, 1)
                pool.memset(hsel[:, :, :], 0.0).then_inc(a_poolc, 1)
                pool.memset(dmask[:, :, :], 1.0).then_inc(a_poolc, 1)
                pool.wait_ge(a_poolc, 5)
                pool.affine_select(out=ident[:, :], in_=ident[:, :], compare_op=ALU.not_equal, fill=1.0,
                                   base=0, pattern=[[-1, P]], channel_multiplier=1).then_inc(a_pool, 1)
                pool.affine_select(out=slt[:, :], in_=slt[:, :], compare_op=ALU.is_ge, fill=0.0,
                                   base=-1, pattern=[[1, P]], channel_multiplier=-1).then_inc(a_pool, 1)
                pool.affine_select(out=mask[:, :], in_=mask[:, :], compare_op=ALU.is_ge, fill=0.0,
                                   base=N - 1, pattern=[[-P, NBLK]], channel_multiplier=-1).then_inc(a_pool, 1)
                pool.affine_select(out=hsel[:, :, :], in_=hsel[:, :, :], compare_op=ALU.not_equal, fill=1.0,
                                   base=0, pattern=[[-NHI, CG], [-1, NHI]], channel_multiplier=1).then_inc(a_pool, 1)
                pool.affine_select(out=dmask[:, :, :], in_=dmask[:, :, :], compare_op=ALU.is_ge, fill=0.0,
                                   base=0, pattern=[[-NHI, CG], [0, NLO]], channel_multiplier=1).then_inc(a_poolc, 1)
                pool.wait_ge(a_poolc, 6)
                pool.affine_select(out=dmask[:, :, :], in_=dmask[:, :, :], compare_op=ALU.is_ge, fill=0.0,
                                   base=NHI - 1, pattern=[[NHI, CG], [0, NLO]], channel_multiplier=-1
                                   ).then_inc(a_pool, 1)
                pool.memset(rec[:, :, :], 0.0).then_inc(a_recz, 1)

            @block.scalar
            def _(act):
                act.wait_ge(a_zero, 1)
                rows_ = NTX * P
                for k in range(zfull):
                    act.dma_start(rec_d[k * P * P:(k + 1) * P * P, :].rearrange("(p r) f -> p (r f)", p=P),
                                  zer[:, :]).then_inc(a_zrec, 16)
                act.dma_start(rec_d[zfull * P * P:rows_, :].rearrange("(p r) f -> p (r f)", p=P),
                              zer[:, 0:NTX * 4 - zfull * 512]).then_inc(a_zrec, 16)
                act.wait_ge(a_zrec, 16 * (zfull + 1))

            @block.tensor
            def _(pe):
                pe.wait_ge(a_pool, NPOOL)
                pe.wait_ge(a_zero, 1)
                nc.tensor.matmul(pc2[:, :, :], onesb[:, 0:CG * NHI], ohz[:, :].rearrange("p (c l) -> p c l", l=NLO),
                                 start=True, stop=False, skip_group_check=True)
                with pe.Fori(0, NCB // 2) as i:
                    for par in range(2):
                        pe.wait_ge(a_oh, 4 * i + 2 * par + 2)
                        for g in range(CB):
                            cols = slice(g * CG, (g + 1) * CG)
                            last = nc.tensor.matmul(pc2[:, :, :], ohh[:, par, cols, :], ohl[:, par, cols, :],
                                                    start=False, stop=False, skip_group_check=True)
                        last.then_inc(a_ohfree[par], 1)
                pe.wait_ge(a_spread, 1)
                nc.tensor.matmul(pcnt[:, :, :], onesf[:, :], cspread[:, :, :], start=True, stop=True).then_inc(a_cnt, 1)

            @block.vector
            def _(dve):
                link = Chain(dve, a_chain)
                nc.vector.memset(srci[:, EFULL:ECOL], NBLK * P)
                nc.vector.memset(dsti[:, EFULL:ECOL], 0)
                nc.vector.memset(wf[:, EFULL:ECOL], 0.0).then_inc(a_pads, 1)
                nc.vector.memset(tblk[0:1, NT:NTX], 0)
                nc.vector.memset(ohz[:, :], 0.0)
                nc.vector.memset(zer[:, :], 0.0).then_inc(a_zero, 1)
                dve.wait_ge(a_src, 32)
                link(nc.vector.tensor_scalar(hi[:, :], srci[:, :], 10, None, ALU.arith_shift_right))
                link(nc.vector.tensor_scalar(lo[:, :], srci[:, :], 7, NLO - 1, ALU.arith_shift_right, ALU.bitwise_and))
                dve.wait_ge(a_pool, NPOOL)
                with dve.Fori(0, NCB // 2) as i:
                    for par in range(2):
                        dve.wait_ge(a_ohfree[par], i)
                        cols = bass.ds((2 * i + par) * (CB * CG), CB * CG)
                        for one, digit, number, n in ((ohh, hi, io13, NHI), (ohl, lo, io8, NLO)):
                            shape = [P, CB * CG, n]
                            nc.vector.tensor_tensor(one[:, par, :, :], digit[:, cols].unsqueeze(2).to_broadcast(shape),
                                                    number[:, :].unsqueeze(1).to_broadcast(shape),
                                                    ALU.is_equal).then_inc(a_oh, 1)
                for par in range(2):
                    dve.wait_ge(a_ohfree[par], NCB // 2)
                link(nc.vector.tensor_tensor(cdiag[:, :, :], pc2[:, :, :], dmask[:, :, :], ALU.mult))
                link(nc.vector.tensor_reduce(csum[:, :], cdiag[:, :, :].rearrange("p c l -> p l c"), AX.X, ALU.add))
                link(nc.vector.tensor_reduce(hmask[:, :], hsel[:, :, :].rearrange("p c h -> p h c"), AX.X, ALU.add))
                shape = [CG * NHI, NHI, NLO]
                nc.vector.tensor_tensor(cspread[:, :, :], csum[:, :].unsqueeze(1).to_broadcast(shape),
                                        hmask[:, :].unsqueeze(2).to_broadcast(shape), ALU.mult).then_inc(a_spread, 1)
                dve.wait_ge(a_cnt, 1)
                count = pcnt[:, :, :].rearrange("p h l -> p (h l)")[:, 0:NBK]
                link(nc.vector.tensor_scalar(ntl[:, :], count, float(P - 1), None, ALU.add))
                link(nc.vector.tensor_scalar(ntl[:, :], ntl[:, :], 7, None, ALU.arith_shift_right))
                link(nc.vector.tensor_copy(ntf[:, :], ntl[:, :]))
                link(nc.vector.tensor_tensor_scan(incl[:, :], onek[:, :], ntf[:, :], 0.0, ALU.mult, ALU.add))
                link(nc.vector.tensor_tensor(excl[:, :], incl[:, :], ntf[:, :], ALU.subtract))
                link(nc.vector.tensor_scalar(base0[:, :], excl[:, :], float(P), None, ALU.mult))
                shape = [P, NT // P, NBLK]
                link(nc.vector.tensor_tensor(tcm[:, :, :], incl[:, 0:NBLK].unsqueeze(1).to_broadcast(shape),
                                             tno[:, :].unsqueeze(2).to_broadcast(shape), ALU.is_le))
                link(nc.vector.tensor_reduce(tbf[:, :], tcm[:, :, :], AX.X, ALU.add))
                nc.vector.tensor_scalar(tbi[:, :], tbf[:, :], float(NBLK - 1), None, ALU.min).then_inc(a_tb, 1)
                link(nc.vector.tensor_tensor(over[:, :], incl[:, 0:NBLK], limit[:, :], ALU.is_gt))
                with nc.allow_low_precision(reason="0 or 1"):
                    link(nc.vector.tensor_reduce(apart[:, :], over[0:1, :], AX.X, ALU.max))
                dve.wait_ge(a_rest, 64)
                dve.wait_ge(a_recz, 1)
                link(nc.vector.tensor_copy(rec[:, :, 0], dsti[:, :]))
                link(nc.vector.tensor_copy(rec[:, :, 2], wf[:, :]))
                link(nc.vector.tensor_scalar(hi[:, :], srci[:, :], 7, None, ALU.arith_shift_right))
                link(nc.vector.tensor_scalar(lo[:, :], srci[:, :], P - 1, None, ALU.bitwise_and))
                link(nc.vector.tensor_copy(blk[:, :], hi[:, :]))
                link(nc.vector.tensor_copy(rec[:, :, 1], lo[:, :]))
        phase.close()

        phase = ExitStack()
        sb, ps = allocator(phase)
        iob_b = iob[:, :].unsqueeze(1).to_broadcast(oh_shape)
        wkv = sb("wkv", [P, KC, 2 * INNER])
        wmean = sb("wmean", [P, KC, 2 * H])
        oh = sb("ohb", [P, GU, GC, NBK], BF16)
        prod = sb("prod", [P, 2, GC, NBK])
        pos = sb("pos", [P, GU, GC], I32)
        recs = sb("recs", [P, GU, GC, 4])
        base = sb("base", [P, 2, NBK])
        xs = sb("xs", [P, D])
        xnb = sb("xnb", [P, D])
        st6 = sb("st6b", [P, 6])
        mv = sb("mvb", [P, 2])
        sd = sb("sdb", [P, 4])
        xnt = sb("xnt", [P, KC, P])
        sq = sb("sq", [P, 2 * H, DH])
        ksb = sb("ksb", [P, INNER])
        vsb = sb("vsb", [P, H, DH])
        ss = sb("ss", [P, 2 * H])
        ms = sb("ms", [P, 2 * H])
        sc = sb("sc", [P, H])
        rt = sb("rt", [P, H])
        rs = sb("rs", [P, H])
        ndots = sb("ndots", [P, NPAIR, P])
        wq = sb("wq", [P, NPAIR, D])
        wot = sb("wot", [P, NPAIR, D])
        at = sb("at", [P, NPAIR, D])
        pr = ps("pr", [P, 2, 512])
        pt = ps("pt", [P, 512])
        pkv = ps("pkv", [P, 2, 512])
        pdots = ps("pdots", [P, 512])
        ptr = ps("ptr", [P, 512])

        def ranks(k):
            return pr[:, k, 0:GC * NBK].rearrange("p (c b) -> p c b", b=NBK)

        b_wkv = sem("b_wkv")
        b_chain = sem("b_chain")
        b_wc = sem("b_wc")
        b_oh = sem("b_oh")
        b_ranks = sem("b_ranks")
        b_total = sem("b_total")
        b_base = sem("b_base")
        b_prod = sems("b_prod", 2)
        b_pos = sems("b_pos", GU)
        b_rec = sems("b_rec", GU)
        b_scat = sems("b_scat", GU)
        b_big = sem("b_big")
        b_xs = sem("b_xs")
        b_stat = sem("b_stat")
        b_var = sem("b_var")
        b_sd = sem("b_sd")
        b_norm = sem("b_norm")
        b_xn = sem("b_xn")
        b_xnst = sem("b_xnst")
        b_tr = sem("b_tr")
        b_xnt = sem("b_xnt")
        b_xst = sem("b_xst")
        b_kv = sem("b_kv")
        b_sq = sem("b_sq")
        b_k = sem("b_k")
        b_ss = sem("b_ss")
        b_ms = sem("b_ms")
        b_sc = sem("b_sc")
        b_rt = sem("b_rt")
        b_rs = sem("b_rs")
        b_vs = sem("b_vs")
        b_dots = sem("b_dots")
        b_w = sem("b_w")
        b_ndz = sem("b_ndz")
        b_nd = sem("b_nd")
        b_at = sem("b_at")
        b_ats = sem("b_ats")
        b_m = sem("b_m")
        with nc.Block() as block:
            @block.sync
            def _(sp):
                def stores(i):
                    sp.wait_ge(b_xn, i + 1)
                    sp.dma_start(xn_d[bass.ds(i * P, P), :], xnb[:, :]).then_inc(b_xnst, 16)
                    sp.wait_ge(b_xnt, i + 1)
                    sp.dma_start(xnt_d[bass.ds(i, 1), :, :].rearrange("o p f -> (o p) f"),
                                 xnt[:, :, :].rearrange("p c n -> p (c n)")).then_inc(b_xst, 16)

                with sp.Fori(0, NBLK - 1) as i:
                    sp.wait_ge(b_xn, i)
                    sp.dma_start(xs[:, :], x[bass.ds(i * P, P), :]).then_inc(b_xs, 16)
                    stores(i)
                sp.wait_ge(b_xn, NBLK - 1)
                sp.dma_start(xs[0:LAST, :], x[N - LAST:N, :]).then_inc(b_xs, 16)
                stores(NBLK - 1)
                sp.wait_ge(b_xnst, 16 * NBLK)
                sp.wait_ge(b_xst, 16 * NBLK)

            @block.gpsimd
            def _(pool):
                with pool.Fori(1, NBLK + 1) as turn:
                    for u in range(GU):
                        pool.wait_ge(a_zrec, 16)
                        pool.wait_ge(b_pos[u], turn)
                        pool.wait_ge(b_rec[u], turn)
                        for c in range(GC):
                            pool.indirect_dma_start(
                                out=rec_d, out_offset=bass.IndirectOffsetOnAxis(ap=pos[:, u, c:c + 1], axis=0),
                                in_=recs[:, u, c, :], in_offset=None).then_inc(b_scat[u], 16)
                for u in range(GU):
                    pool.wait_ge(b_scat[u], 16 * GC * NBLK)

            @block.scalar
            def _(act):
                act.dma_start(wkv[:, :, :], wqkv_t[:, INNER:3 * INNER].rearrange("(c p) n -> p c n", p=P)
                              ).then_inc(b_wkv, 16)
                act.dma_start(wq[:, :, :], wqkv[0:INNER, :].rearrange("(j p) f -> p j f", p=P)).then_inc(b_w, 16)
                act.dma_start(wot[:, :, :], wout_t.rearrange("(j p) f -> p j f", p=P)).then_inc(b_w, 16)
                act.wait_ge(b_total, 1)
                nc.scalar.copy(base[:, 0, :], pt[:, 0:NBK]).then_inc(b_base, 1)
                with act.Fori(0, NBLK) as i:
                    def stage_records(u):
                        act.wait_ge(b_scat[u], 16 * GC * i)
                        nc.scalar.copy(recs[:, u, :, :], rec[:, bass.ds((i * GU + u) * GC, GC), :]
                                       ).then_inc(b_rec[u], 1)

                    def copy_total(u):
                        act.wait_ge(b_total, i * GU + u + 2)
                        nc.scalar.copy(base[:, (u + 1) % 2, :], pt[:, 0:NBK]).then_inc(b_base, 1)

                    stage_records(0)
                    act.wait_ge(b_var, i + 1)
                    act.wait_ge(b_norm, 3 * i)
                    nc.scalar.activation(sd[:, 1:2], sd[:, 0:1], ACT.Sqrt).then_inc(b_sd, 1)
                    copy_total(0)
                    stage_records(1)
                    act.wait_ge(b_tr, i + 1)
                    act.wait_ge(b_kv, i)
                    act.wait_ge(b_xst, 16 * i)
                    nc.scalar.copy(xnt[:, :, :].rearrange("p c n -> p (c n)"), ptr[:, 0:D]).then_inc(b_xnt, 1)
                    copy_total(1)
                    nc.scalar.copy(row_of(i), zer[:, 0:D]).then_inc(b_big, 1)
                    act.wait_ge(b_kv, i + 1)
                    act.wait_ge(b_ss, i)
                    for k in range(2):
                        nc.scalar.activation(sq[:, k * H:(k + 1) * H, :].rearrange("p h d -> p (h d)"), pkv[:, k, :],
                                             ACT.Square).then_inc(b_sq, 1)
                    act.wait_ge(b_dots, i)
                    nc.scalar.copy(ksb[:, :], pkv[:, 0, :]).then_inc(b_k, 1)
                    stage_records(2)
                    copy_total(2)
                    act.wait_ge(b_sc, i + 1)
                    nc.scalar.activation(rt[:, :], sc[:, :], ACT.Sqrt).then_inc(b_rt, 1)
                    stage_records(3)
                    copy_total(3)

            @block.tensor
            def _(pe):
                nc.tensor.matmul(pt[:, 0:NBK], ident[:, :], base0[:, :], start=True, stop=False,
                                 skip_group_check=True).then_inc(b_total, 1)
                nc.tensor.matmul(pdots[:, :], ident[:, :], zer[:, :], start=True, stop=False, skip_group_check=True)
                with pe.Fori(0, NBLK) as i:
                    def rank(u):
                        par, k = u % 2, u // 2
                        r = ranks(par)
                        pe.wait_ge(b_oh, i * GU + u + 1)
                        pe.wait_ge(b_prod[par], 2 * i + k)
                        nc.tensor.matmul(r, slt[:, :], oh[:, u, :, :], start=True, stop=False, skip_group_check=True)
                        for s in range(1, GC):
                            nc.tensor.matmul(r[:, s:GC, :], onesb[:, :], oh[:, u, 0:GC - s, :], start=False, stop=False,
                                             skip_group_check=True)
                        pe.wait_ge(b_base, i * GU + u + 1)
                        nc.tensor.matmul(r, ident[:, :], base[:, u % 2, :].unsqueeze(1).to_broadcast(oh_shape),
                                         start=False, stop=True, skip_group_check=True).then_inc(b_ranks, 1)
                        for c in range(GC):
                            last = nc.tensor.matmul(pt[:, 0:NBK], onesb[:, :], oh[:, u, c, :], start=False, stop=False,
                                                    skip_group_check=True)
                        last.then_inc(b_total, 1)

                    rank(0)
                    pe.wait_ge(b_xn, i + 1)
                    pe.wait_ge(b_xnt, i)
                    for c in range(KC):
                        last = nc.tensor.transpose(ptr[:, c * P:(c + 1) * P], xnb[:, c * P:(c + 1) * P], ident[:, :])
                    last.then_inc(b_tr, 1)
                    rank(1)
                    pe.wait_ge(b_xnt, i + 1)
                    pe.wait_ge(b_k, i)
                    pe.wait_ge(b_vs, i)
                    pe.wait_ge(b_wc, 1)
                    for k in range(2):
                        for c in range(KC):
                            last = nc.tensor.matmul(pkv[:, k, :], xnt[:, c, :], wkv[:, c, k * INNER:(k + 1) * INNER],
                                                    start=(c == 0), stop=(c == KC - 1))
                    last.then_inc(b_kv, 1)
                    rank(2)
                    pe.wait_ge(b_k, i + 1)
                    pe.wait_ge(b_vs, i + 1)
                    for j in range(NPAIR):
                        last = nc.tensor.matmul(pdots[:, j * P:(j + 1) * P], ksb[:, j * P:(j + 1) * P],
                                                vsb[:, 2 * j:2 * j + 2, :], start=False, stop=False,
                                                skip_group_check=True)
                    last.then_inc(b_dots, 1)
                    rank(3)
                pe.wait_ge(b_nd, 1)
                pe.wait_ge(b_w, 32)
                for j in range(NPAIR):
                    pe.wait_ge(b_ats, j)
                    nc.tensor.matmul(ptr[:, 0:D], ndots[:, j, :], wq[:, j, :], start=True, stop=True).then_inc(b_at, 1)
                pe.wait_ge(b_ats, NPAIR)
                for c in range(KC):
                    for j in range(NPAIR):
                        last = nc.tensor.matmul(pkv[:, c, 0:D], at[:, j, c * P:(c + 1) * P], wot[:, j, :],
                                                start=(j == 0), stop=(j == NPAIR - 1))
                last.then_inc(b_m, 1)

            @block.vector
            def _(dve):
                link = Chain(dve, b_chain)
                nc.vector.memset(ndots[:, :, :], 0.0).then_inc(b_ndz, 1)

                def centre_weights():
                    dve.wait_ge(b_wkv, 16)
                    for c in range(KC):
                        w3 = wkv[:, c, :].rearrange("p (h d) -> p h d", d=DH)
                        link(nc.vector.tensor_reduce(wmean[:, c, :], w3, AX.X, ALU.add))
                        link(nc.vector.tensor_scalar(wmean[:, c, :], wmean[:, c, :], -1.0 / DH, None, ALU.mult))
                        link(nc.vector.tensor_tensor(w3, w3, wmean[:, c, :].unsqueeze(2).to_broadcast([P, 2 * H, DH]),
                                                     ALU.add))
                    nc.vector.sem_inc(b_wc, 1)

                centre_weights()
                with dve.Fori(0, NBLK) as i:
                    def place(u):
                        par, k = u % 2, u // 2
                        dve.wait_ge(b_ranks, i * GU + u + 1)
                        nc.vector.tensor_tensor(prod[:, par, :, :], ranks(par), oh[:, u, :, :],
                                                ALU.mult).then_inc(b_prod[par], 1)
                        dve.wait_ge(b_prod[par], 2 * i + k + 1)
                        dve.wait_ge(b_scat[u], 16 * GC * i)
                        with nc.allow_low_precision(reason="one whole number below 2^24 among zeros"):
                            nc.vector.tensor_reduce(pos[:, u, :], prod[:, par, :, :], AX.X, ALU.add
                                                    ).then_inc(b_pos[u], 1)

                    for u in range(GU):
                        if u == 0:
                            dve.wait_ge(b_total, i * GU + 1)
                        cols = blk[:, bass.ds((i * GU + u) * GC, GC)].unsqueeze(2).to_broadcast(oh_shape)
                        nc.vector.tensor_tensor(oh[:, u, :, :], cols, iob_b, ALU.is_equal).then_inc(b_oh, 1)
                    dve.wait_ge(b_xs, 16 * (i + 1))
                    nc.vector.bn_stats(st6[:, :], xs[:, :]).then_inc(b_stat, 1)
                    dve.wait_ge(b_stat, 2 * i + 1)
                    nc.vector.sem_inc(passed, 1)
                    nc.vector.bn_aggr(mv[:, :], st6[:, :]).then_inc(b_stat, 1)
                    dve.wait_ge(b_stat, 2 * i + 2)
                    nc.vector.tensor_scalar(sd[:, 0:1], mv[:, 1:2], EPS, None, ALU.add).then_inc(b_var, 1)
                    place(0)
                    dve.wait_ge(b_sd, i + 1)
                    nc.vector.reciprocal(sd[:, 2:3], sd[:, 1:2]).then_inc(b_norm, 1)
                    dve.wait_ge(b_norm, 3 * i + 1)
                    nc.vector.tensor_tensor(sd[:, 2:3], sd[:, 2:3], mask[:, bass.ds(i, 1)], ALU.mult
                                            ).then_inc(b_norm, 1)
                    dve.wait_ge(b_norm, 3 * i + 2)
                    nc.vector.scalar_tensor_tensor(out=sd[:, 3:4], in0=mv[:, 0:1], scalar=-1.0, in1=sd[:, 2:3],
                                                   op0=ALU.mult, op1=ALU.mult).then_inc(b_norm, 1)
                    dve.wait_ge(b_norm, 3 * i + 3)
                    dve.wait_ge(b_xnst, 16 * i)
                    dve.wait_ge(b_tr, i)
                    nc.vector.tensor_scalar(xnb[:, :], xs[:, :], sd[:, 2:3], sd[:, 3:4], ALU.mult, ALU.add
                                            ).then_inc(b_xn, 1)
                    place(1)
                    dve.wait_ge(b_sq, 2 * i + 2)
                    nc.vector.tensor_reduce(ss[:, :], sq[:, :, :], AX.X, ALU.add).then_inc(b_ss, 1)
                    dve.wait_ge(b_ss, i + 1)
                    nc.vector.tensor_scalar(ms[:, :], ss[:, :], 1.0 / DH, EPS, ALU.mult, ALU.add).then_inc(b_ms, 1)
                    dve.wait_ge(b_ms, i + 1)
                    nc.vector.tensor_tensor(sc[:, :], ms[:, 0:H], ms[:, H:2 * H], ALU.mult).then_inc(b_sc, 1)
                    place(2)
                    dve.wait_ge(b_rt, i + 1)
                    nc.vector.reciprocal(rs[:, :], rt[:, :]).then_inc(b_rs, 1)
                    dve.wait_ge(b_rs, i + 1)
                    dve.wait_ge(b_dots, i)
                    nc.vector.tensor_tensor(vsb[:, :, :], pkv[:, 1, :].rearrange("p (h d) -> p h d", d=DH),
                                            rs[:, :].unsqueeze(2).to_broadcast([P, H, DH]), ALU.mult).then_inc(b_vs, 1)
                    place(3)
                dve.wait_ge(b_dots, NBLK)
                dve.wait_ge(b_ndz, 1)
                for j in range(NPAIR):
                    for a in range(2):
                        q = slice(a * DH, (a + 1) * DH)
                        last = nc.vector.tensor_scalar(ndots[q, j, q], pdots[q, j * P + a * DH:j * P + (a + 1) * DH],
                                                       1.0 / N, None, ALU.mult)
                last.then_inc(b_nd, 1)
                for j in range(NPAIR):
                    dve.wait_ge(b_at, j + 1)
                    nc.vector.tensor_copy(at[:, j, :], ptr[:, 0:D]).then_inc(b_ats, 1)
                dve.wait_ge(b_m, 1)
                nc.vector.tensor_copy(wx1[:, 0, :], pkv[:, 0, 0:D])
                nc.vector.tensor_copy(wx1[:, 1, :], pkv[:, 1, 0:D])
        phase.close()
        edges.close()

        sb, _ = allocator(ctx)
        sfx = sb("sfx", [P, NPAIR, D])
        snorm = sb("snorm", [P, NPAIR])
        pmat = sb("pmat", [P, NPAIR, D])

        phase = ExitStack()
        sb, ps = allocator(phase)
        NCH = NT // P
        gidx = sb("gidx", [P, NTX], I32)
        place_c = sb("place_c", [P, NTX])
        weight_c = sb("weight_c", [P, NTX])
        idxs = sb("idxs", [P, RT], I32)
        wls = sb("wls", [P, KC, INNER])
        b1_3 = sb("b1_3", [3, D], BF16)
        bl_3 = sb("bl_3", [3, INNER], BF16)
        zer = sb("zer_c", [P, INNER])
        first = ExitStack()
        fsb, _ = allocator(first)
        tl = fsb("tl", [P, NCH, P, 4])
        gw = fsb("gw", [P, KC, D])
        diag = fsb("diag", [P, KC])
        wxt = fsb("wxt", [DH, H, D])
        wsl = fsb("wsl", [DH, G])
        bxc = fsb("bxc", [DH, H])
        bx3 = fsb("bx3", [DH, H, 3])
        tmp8 = fsb("tmp8", [P, H])
        rt8 = fsb("rt8", [P, H])
        r1 = fsb("r1", [3, 4, INNER])
        r2 = fsb("r2", [3, 4, D])
        r3 = fsb("r3", [3, 4, D])
        p1 = ExitStack()
        _, fps = allocator(p1)
        ptf = fps("ptf", [P, 3, 512])
        pls = fps("pls", [P, KC, INNER])
        pbl = fps("pbl", [3, INNER])
        c_tl = sems("c_tl", 2)
        c_w = sem("c_w")
        c_bx = sem("c_bx")
        c_fold = sem("c_fold")
        c_chain = sem("c_chain")
        c_tr = sem("c_tr")
        c_ev = sem("c_ev")
        CT = 7
        with nc.Block() as block:
            @block.sync
            def _(sp):
                for k, (c0, c1) in enumerate(((0, CT), (CT, NCH))):
                    sp.dma_start(tl[:, c0:c1, :, :], rec_d[c0 * P * P:c1 * P * P, :].rearrange(
                        "(c t s) f -> t c s f", t=P, s=P)).then_inc(c_tl[k], 16)
                for k in range(2):
                    sp.wait_ge(c_tl[k], 16)

            @block.scalar
            def _(act):
                act.dma_start(gw[:, :, :], gnn_w.rearrange("(c p) n -> p c n", p=P)).then_inc(c_w, 16)
                with nc.allow_non_contiguous_dma("small columns"):
                    act.dma_start(diag[:, :], gnn_diag.rearrange("(c p) -> p c", p=P)).then_inc(c_w, 16)
                    act.dma_start(bxc[:, :], b_x.rearrange("(h d) -> d h", h=H)).then_inc(c_w, 16)
                act.dma_start(wxt[:, :, :], w_x_t.rearrange("(h d) f -> d h f", h=H)).then_inc(c_w, 16)
                act.dma_start(wsl[:, :], w_slice).then_inc(c_w, 16)
                act.dma_start(tmp8[:, :], temp.partition_broadcast(P)).then_inc(c_w, 16)
                act.dma_start(r2[:, 0, :], gnn_b.partition_broadcast(3)).then_inc(c_w, 16)
                act.dma_start(r2[:, 1, :], bout.partition_broadcast(3)).then_inc(c_w, 16)
                act.dma_start(r3[:, 0, :], b_out.partition_broadcast(3)).then_inc(c_w, 16)
                for h in range(H):
                    act.dma_start(r1[:, 0, h * G:(h + 1) * G], b_slice.partition_broadcast(3)).then_inc(c_w, 16)
                act.wait_ge(c_w, 17 * 16)

            @block.tensor
            def _(pe):
                pe.wait_ge(c_w, 17 * 16)
                pe.wait_ge(c_bx, 1)
                for h in range(H):
                    for c in range(KC):
                        nc.tensor.matmul(pls[:, c, h * G:(h + 1) * G], wxt[:, h, c * P:(c + 1) * P], wsl[:, :],
                                         start=True, stop=True)
                    last = nc.tensor.matmul(pbl[:, h * G:(h + 1) * G], bx3[:, h, :], wsl[:, :], start=True, stop=True)
                last.then_inc(c_fold, 1)
                for c in range(NCH):
                    pe.wait_ge(c_tl[c // CT], 16)
                    if c:
                        pe.wait_ge(c_ev, 3 * c + 3)
                    for f in range(3):
                        last = nc.tensor.transpose(ptf[:, f, 0:P], tl[:, c, :, f], ident[:, :])
                    last.then_inc(c_tr, 1)

            @block.vector
            def _(dve):
                link = Chain(dve, c_chain)
                for t in (gidx, place_c, weight_c):
                    nc.vector.memset(t[:, NT:NTX], 0).then_inc(c_ev, 1)
                nc.vector.memset(zer[:, :], 0.0)
                nc.vector.memset(snorm[:, :], 0.0)
                dve.wait_ge(c_w, 17 * 16)
                for h in range(H):
                    last = nc.vector.tensor_copy(bx3[:, h, :], bxc[:, h:h + 1].to_broadcast([DH, 3]))
                last.then_inc(c_bx, 1)
                link(nc.vector.tensor_tensor(wx1[:, 0:KC, :], wx1[:, 0:KC, :], gw[:, :, :], ALU.add))
                link(nc.vector.tensor_scalar(diag[:, :], diag[:, :], 1.0, -1.0, ALU.add, ALU.mult))
                for c in range(KC):
                    nc.vector.tensor_scalar(wx1[:, KC + c, :], gw[:, c, :], diag[:, c:c + 1], None, ALU.mult)
                link(nc.vector.tensor_scalar(tmp8[:, :], tmp8[:, :], 0.1, 5.0, ALU.max, ALU.min))
                link(nc.vector.reciprocal(rt8[:, :], tmp8[:, :]))
                dve.wait_ge(c_fold, 1)
                for c in range(KC):
                    nc.vector.tensor_tensor(wls[:, c, :].rearrange("p (h g) -> p h g", g=G),
                                            pls[:, c, :].rearrange("p (h g) -> p h g", g=G),
                                            rt8[:, :].unsqueeze(2).to_broadcast([P, H, G]), ALU.mult)
                link(nc.vector.tensor_tensor(r1[:, 0, :], pbl[:, :], r1[:, 0, :], ALU.add))
                b3_ = r1[:, 0, :].rearrange("p (h g) -> p h g", g=G)
                link(nc.vector.tensor_tensor(b3_, b3_, rt8[0:3, :].unsqueeze(2).to_broadcast([3, H, G]), ALU.mult))
                link(nc.vector.tensor_tensor(r2[:, 0, :], r2[:, 0, :], r2[:, 1, :], ALU.add))
                for parts, r in ((bl_3, r1), (b1_3, r2), (b2_3, r3)):
                    split_rows(link, nc.vector, parts[:, :], r[:, 0, :], ident, r[:, 1, :], r[:, 2, :], r[:, 3, :])
                for c in range(NCH):
                    dve.wait_ge(c_tr, c + 1)
                    for f, t in enumerate((gidx, place_c, weight_c)):
                        nc.vector.tensor_copy(t[:, c * P:(c + 1) * P], ptf[:, f, 0:P]).then_inc(c_ev, 1)
        first.close()
        p1.close()

        X = sb("X", [P, RT, D])
        ohw = sb("ohw", [P, RT, P])
        xr = sb("xr", [P, D])
        xt = sb("xt", [P, D])
        en = sb("en", [P, D])
        et = sb("et", [P, D])
        st6 = sb("st6c", [P, 6])
        mv = sb("mvc", [P, 2])
        ve = sb("ve", [P, 1])
        sd = sb("sdc", [P, 1])
        iv = sb("iv", [P, 1])
        rs = sb("rsc", [P, 1])
        nm = sb("nm", [P, 1])
        ya = sb("ya", [P, D])
        yb = sb("yb", [P, D])
        yt = sb("yt", [P, D])
        mx = sb("mx", [P, H])
        nmx = sb("nmx", [P, H])
        rcm = sb("rcm", [P, H])
        nsum = sb("nsum", [P, NPAIR])
        ex = sb("ex", [P, H, G])
        sm = sb("sm", [P, H])
        rc = sb("rc", [P, H])
        sw = sb("sw", [P, H, G])
        swt = sb("swt", [P, INNER])
        NPB = 3
        pacc = ps("pacc", [P, NPB, 512])
        ptr = ps("ptrc", [P, 512])[:, 0:D]
        px = ps("px", [P, 512])[:, 0:D]
        pl = ps("pl", [P, 512])
        pS = ps("pS", [P, NPAIR, D])
        HALF = [(0, (RT + 1) // 2), ((RT + 1) // 2, RT)]
        BANK = [u % NPB for u in range(RT)]

        c_idx = sems("c_idx", 2)
        c_g = sems("c_g", RT)
        c_xfree = sems("c_xfree", RT)
        c_oh = sem("c_oh")
        c_acc = sem("c_acc")
        c_apart = sem("c_apart")
        d_x = sem("d_x")
        d_en = sem("d_en")
        d_tr = sem("d_tr")
        d_et = sem("d_et")
        d_mm = sem("d_mm")
        d_x1 = sem("d_x1")
        d_stat = sem("d_stat")
        d_var = sem("d_var")
        d_sd = sem("d_sd")
        d_iv = sem("d_iv")
        d_rs = sem("d_rs")
        d_ln = sem("d_ln")
        e_y = sem("e_y")
        e_yb = sem("e_yb")
        e_yt = sem("e_yt")
        e_yts = sem("e_yts")
        e_log = sem("e_log")
        e_mx = sem("e_mx")
        e_nmx = sem("e_nmx")
        e_nrm = sem("e_nrm")
        e_ex = sem("e_ex")
        e_inv = sem("e_inv")
        e_sw = sem("e_sw")
        e_swt = sem("e_swt")
        e_swts = sem("e_swts")
        e_S = sem("e_S")
        e_st = sem("e_st")

        def rounds(engine, gather, block_steps, first=0, at_end=None):
            def part(steps, k):
                return [(slot - k * RT, f) for slot, f in steps if k * RT <= slot < (k + 1) * RT]

            s0, s1, s2 = [part(block_steps, k) for k in range(3)]
            end0 = part(at_end or block_steps, 0)

            def run(*parts):
                steps = [(slot, f, t) for part, t in parts for slot, f in part]
                for _, f, t in sorted(steps, key=lambda s: s[0]):
                    f(t)

            with engine.Fori(first, first + LAG) as i:
                run((gather, i))
            flag = engine.value_load(apart[0:1, 0:1], min_val=0, max_val=1)
            with engine.If(flag == 0):
                run((gather, first + LAG), (s0, 0))
                run((gather, first + LAG + 1), (s1, 0), (s0, 1))
                with engine.Fori(first + LAG + 2, first + NBLK) as i:
                    t = i - (first + LAG)
                    run((gather, i), (s2, t - 2), (s1, t - 1), (s0, t))
            with engine.Else():
                if gather:
                    with engine.Fori(first + LAG, first + NBLK) as i:
                        run((gather, i))
                run((s0, 0))
                run((s1, 0), (s0, 1))
                with engine.Fori(2, NBLK - LAG) as t:
                    run((s2, t - 2), (s1, t - 1), (s0, t))
            with engine.Fori(NBLK - LAG, NBLK) as t:
                run((s2, t - 2), (s1, t - 1), (end0, t))
            run((s2, NBLK - 2), (s1, NBLK - 1))
            run((s2, NBLK - 1))

        def b3(t):
            return t[:, :].unsqueeze(2).to_broadcast([P, H, G])

        with nc.Block() as block:
            @block.sync
            def _(sp):
                def load(t, rows_):
                    sp.wait_ge(d_mm, t)
                    sp.dma_start(xt[:, :], xnt_d[bass.ds(t, 1), :, :].rearrange("o p f -> (o p) f")).then_inc(d_x, 16)
                    if rows_ == P:
                        sp.dma_start(xr[:, :], x[bass.ds(t * P, P), :]).then_inc(d_x, 16)
                    else:
                        sp.dma_start(xr[0:rows_, :], x[N - rows_:N, :]).then_inc(d_x, 16)

                def store(t):
                    sp.wait_ge(e_swts, t + 1)
                    sp.dma_start(swt_d[bass.ds(t, 1), :, :].rearrange("o p f -> (o p) f"), swt[:, :]).then_inc(e_st, 16)

                with sp.Fori(0, 3) as t:
                    load(t, P)
                with sp.Fori(3, NBLK - 1) as t:
                    load(t, P)
                    store(t - 3)
                load(NBLK - 1, LAST)
                with sp.Fori(NBLK - 4, NBLK) as t:
                    store(t)
                sp.wait_ge(e_st, 16 * NBLK)

            @block.gpsimd
            def _(pool):
                def gather(u):
                    def step(turn):
                        pool.wait_ge(c_apart, 1)
                        for k, (q0, _) in enumerate(HALF):
                            if u == q0:
                                pool.wait_ge(c_idx[k], turn)
                        pool.wait_ge(c_xfree[u], turn)
                        pool.indirect_dma_start(out=X[:, u, :], out_offset=None, in_=xn_d,
                                                in_offset=bass.IndirectOffsetOnAxis(ap=idxs[:, u:u + 1], axis=0)
                                                ).then_inc(c_g[u], 16)
                    return step

                def stage(k, ahead):
                    q0, q1 = HALF[k]

                    def step(turn):
                        r = turn - 1 + ahead
                        for u in range(q0, q1):
                            pool.wait_ge(c_g[u], 16 * r)
                        pool.tensor_copy(idxs[:, q0:q1], gidx[:, bass.ds(r * RT + q0, q1 - q0)]).then_inc(c_idx[k], 1)
                    return step

                stage(0, 0)(1)
                rounds(pool, [(3.5, stage(1, 0)), (12.5, stage(0, 1))] + [(u, gather(u)) for u in range(RT)], [],
                       first=1)

            @block.scalar
            def _(act):
                def sums_out(t):
                    act.wait_ge(c_acc, (t + LAG) * RT + 2)
                    sums_of_block(t)

                def sums_out_at_end(t):
                    act.wait_ge(c_acc, NBLK * RT + 2)
                    sums_of_block(t)

                def sums_of_block(t):
                    act.wait_ge(d_tr, t)
                    nc.scalar.sem_inc(passed, 1)
                    nc.scalar.copy(en[:, :], row_of(t)).then_inc(d_en, 1)

                def sums_t(t):
                    act.wait_ge(d_tr, t + 1)
                    act.wait_ge(d_mm, t)
                    nc.scalar.copy(et[:, :], ptr).then_inc(d_et, 1)

                def keep_x1(t):
                    act.wait_ge(d_mm, t + 1)
                    nc.scalar.sem_inc(passed, 1)
                    nc.scalar.copy(row_of(t), px).then_inc(d_x1, 1)

                def root(t):
                    act.wait_ge(d_var, t + 1)
                    act.wait_ge(d_iv, t)
                    nc.scalar.activation(sd[:, :], ve[:, :], ACT.Sqrt).then_inc(d_sd, 1)

                def y_t(t):
                    act.wait_ge(e_yt, t + 1)
                    act.wait_ge(e_log, t)
                    nc.scalar.copy(yt[:, :], ptr).then_inc(e_yts, 1)

                def exponentials(t):
                    act.wait_ge(e_nmx, t + 1)
                    act.wait_ge(e_sw, t)
                    for h in range(H):
                        last = nc.scalar.activation(ex[:, h, :], pl[:, h * G:(h + 1) * G], ACT.Exp,
                                                    bias=nmx[:, h:h + 1], accum_out=sm[:, h:h + 1])
                    last.then_inc(e_ex, 1)

                def copy_y(t):
                    act.wait_ge(e_y, t + 1)
                    act.wait_ge(e_S, t)
                    nc.scalar.copy(yb[:, :], ya[:, :]).then_inc(e_yb, 1)

                def weights_t(t):
                    act.wait_ge(e_swt, t + 1)
                    act.wait_ge(e_st, 16 * t)
                    act.wait_ge(e_nrm, t)
                    for j in range(NPAIR):
                        q = slice(j * P, (j + 1) * P)
                        last = nc.scalar.activation(swt[:, q], pl[:, q], ACT.Copy, accum_out=nsum[:, j:j + 1])
                    last.then_inc(e_swts, 1)

                rest = [(2 * RT + 2, exponentials), (6, sums_t), (10.2, keep_x1), (RT + 10.6, y_t),
                        (2 * RT + 14, weights_t), (RT + 13.4, copy_y), (14.6, root)]
                rounds(act, [], [(1, sums_out)] + rest, at_end=[(1, sums_out_at_end)] + rest)

            @block.tensor
            def _(pe):
                def tile(u):
                    def step(i):
                        pe.wait_ge(c_oh, i * RT + u + 1)
                        ago = next(k for k in range(1, RT + 1) if BANK[u - k] == BANK[u])
                        pe.wait_ge(c_acc, i * RT + u + 3 - min(ago, NPB))
                        pe.wait_ge(c_g[u], 16 * (i + 1))
                        nc.tensor.matmul(pacc[:, BANK[u], 0:D], ohw[:, u, :], X[:, u, :], start=True, stop=True
                                         ).then_inc(c_xfree[u], 1)
                    return step

                def transpose_sums(t):
                    pe.wait_ge(d_en, t + 1)
                    for c in range(KC):
                        last = nc.tensor.transpose(ptr[:, c * P:(c + 1) * P], en[:, c * P:(c + 1) * P], ident[:, :])
                    last.then_inc(d_tr, 1)

                def x1(t):
                    pe.wait_ge(e_y, t)
                    pe.wait_ge(d_x1, t)
                    pe.wait_ge(d_stat, 2 * t)
                    nc.tensor.matmul(px, ones3[:, :], b1_3[:, :], start=True, stop=False)
                    pe.wait_ge(d_x, 32 * (t + 1))
                    nc.tensor.matmul(px, ident[:, :], xr[:, :], start=False, stop=False)
                    for c in range(KC):
                        nc.tensor.matmul(px, xt[:, c * P:(c + 1) * P], wx1[:, c, :], start=False, stop=False)

                def x1_sums(t):
                    pe.wait_ge(d_et, t + 1)
                    for c in range(KC):
                        last = nc.tensor.matmul(px, et[:, c * P:(c + 1) * P], wx1[:, KC + c, :],
                                                start=False, stop=(c == KC - 1))
                    last.then_inc(d_mm, 1)

                def transpose_y(t):
                    pe.wait_ge(e_y, t + 1)
                    for c in range(KC):
                        last = nc.tensor.transpose(ptr[:, c * P:(c + 1) * P], ya[:, c * P:(c + 1) * P], ident[:, :])
                    last.then_inc(e_yt, 1)

                def logits(t):
                    pe.wait_ge(e_swts, t)
                    nc.tensor.matmul(pl[:, :], ones3[:, :], bl_3[:, :], start=True, stop=False)
                    pe.wait_ge(e_yts, t + 1)
                    nc.tensor.matmul(pl[:, :], yt[:, 0:P], wls[:, 0, :], start=False, stop=False)

                def logits_rest(t):
                    for c in range(1, KC):
                        last = nc.tensor.matmul(pl[:, :], yt[:, c * P:(c + 1) * P], wls[:, c, :],
                                                start=False, stop=(c == KC - 1))
                    last.then_inc(e_log, 1)

                def pair_sum(j):
                    return nc.tensor.matmul(pS[:, j, :], sw[:, 2 * j:2 * j + 2, :], yb[:, :],
                                            start=False, stop=False, skip_group_check=True)

                def slice_sums(t):
                    pe.wait_ge(e_sw, t + 1)
                    pe.wait_ge(e_yb, t + 1)
                    for j in range(2):
                        pair_sum(j)

                def slice_sums_rest(t):
                    for j in range(2, NPAIR):
                        last = pair_sum(j)
                    last.then_inc(e_S, 1)

                def transpose_weights(t):
                    pe.wait_ge(e_sw, t + 1)
                    for j in range(NPAIR):
                        last = nc.tensor.transpose(pl[:, j * P:(j + 1) * P], sw[:, 2 * j:2 * j + 2, :], ident[:, :])
                    last.then_inc(e_swt, 1)

                for k in range(2):
                    nc.tensor.matmul(pS[:, 2 * k:2 * k + 2, :], ident[:, :], zer[:, :], start=True, stop=False,
                                     skip_group_check=True)
                for u in range(RT):
                    nc.tensor.sem_inc(c_xfree[u], 1)
                rounds(pe, [(u, tile(u)) for u in range(RT)],
                       [(3.5, transpose_sums), (6.5, x1), (8.5, x1_sums), (RT + 9.6, transpose_y),
                        (RT + 14.7, logits), (RT + 15.7, logits_rest), (2 * RT + 11, slice_sums),
                        (2 * RT + 12.2, slice_sums_rest), (2 * RT + 13.2, transpose_weights)])

            @block.vector
            def _(dve):
                def onehot(t, u):
                    nc.vector.tensor_scalar(ohw[:, u, :], ion[:, :], place_c[:, bass.ds(t, 1)],
                                            weight_c[:, bass.ds(t, 1)], ALU.is_equal, ALU.mult).then_inc(c_oh, 1)

                state = {}

                def blocks(u0, u1):
                    def step(i):
                        _, state["blocks"] = nc.values_load_multi_w_load_instructions(
                            tblk[0:1, bass.ds(i * RT + u0, u1 - u0)], engines=[mybir.EngineType.DVE],
                            min_val=0, max_val=NBLK - 1,
                            skip_runtime_bounds_check_because="the tiles' blocks are cut to NBLK - 1")
                        state["first"] = u0
                    return step

                def add(u):
                    def step(i):
                        to = row_of(state["blocks"][u - state["first"]])
                        dve.wait_ge(c_xfree[u], i + 2)
                        dve.wait_ge(c_acc, i * RT + u + 2)
                        nc.vector.tensor_tensor(to, pacc[:, BANK[u], 0:D], to, ALU.add).then_inc(c_acc, 1)
                        onehot((i + 1) * RT + u, u)
                    return step

                def stats(t):
                    dve.wait_ge(d_x1, t + 1)
                    nc.vector.bn_stats(st6[:, :], px).then_inc(d_stat, 1)

                def mean_var(t):
                    dve.wait_ge(d_stat, 2 * t + 1)
                    nc.vector.sem_inc(passed, 1)
                    nc.vector.bn_aggr(mv[:, :], st6[:, :]).then_inc(d_stat, 1)

                def var_eps(t):
                    dve.wait_ge(d_stat, 2 * t + 2)
                    nc.vector.tensor_scalar(ve[:, :], mv[:, 1:2], EPS, None, ALU.add).then_inc(d_var, 1)

                def inverse(t):
                    dve.wait_ge(d_sd, t + 1)
                    nc.vector.reciprocal(iv[:, :], sd[:, :]).then_inc(d_iv, 1)

                def masked_rstd(t):
                    dve.wait_ge(d_iv, t + 1)
                    dve.wait_ge(e_y, t)
                    nc.vector.tensor_tensor(rs[:, :], iv[:, :], mask[:, bass.ds(t, 1)], ALU.mult).then_inc(d_rs, 1)

                def shift(t):
                    dve.wait_ge(d_rs, t + 1)
                    nc.vector.scalar_tensor_tensor(out=nm[:, :], in0=mv[:, 0:1], scalar=-1.0, in1=rs[:, :],
                                                   op0=ALU.mult, op1=ALU.mult).then_inc(d_ln, 1)

                def normalise(t):
                    dve.wait_ge(d_ln, t + 1)
                    dve.wait_ge(e_yts, t)
                    dve.wait_ge(e_yb, t)
                    nc.vector.tensor_scalar(ya[:, :], px, rs[:, :], nm[:, :], ALU.mult, ALU.add).then_inc(e_y, 1)

                lg = pl[:, :].rearrange("p (h g) -> p h g", g=G)

                def maxima(t):
                    dve.wait_ge(e_log, t + 1)
                    nc.vector.tensor_reduce(mx[:, :], lg, AX.X, ALU.max).then_inc(e_mx, 1)

                def minus_maxima(t):
                    dve.wait_ge(e_mx, t + 1)
                    dve.wait_ge(e_ex, t)
                    nc.vector.tensor_scalar(nmx[:, :], mx[:, :], -1.0, None, ALU.mult).then_inc(e_nmx, 1)

                def inverses(t):
                    dve.wait_ge(e_ex, t + 1)
                    nc.vector.reciprocal(rc[:, :], sm[:, :]).then_inc(e_inv, 1)

                def masked_inverses(t):
                    dve.wait_ge(e_inv, 2 * t + 1)
                    nc.vector.tensor_scalar(rcm[:, :], rc[:, :], mask[:, bass.ds(t, 1)], None, ALU.mult
                                            ).then_inc(e_inv, 1)

                def add_norms(t):
                    dve.wait_ge(e_swts, t + 1)
                    dve.wait_ge(e_nrm, t)
                    nc.vector.tensor_tensor(snorm[:, :], snorm[:, :], nsum[:, :], ALU.add).then_inc(e_nrm, 1)

                def slice_weights(t):
                    dve.wait_ge(e_inv, 2 * t + 2)
                    dve.wait_ge(e_swt, t)
                    nc.vector.tensor_tensor(sw[:, :, :], ex[:, :, :], b3(rcm), ALU.mult).then_inc(e_sw, 1)

                nc.vector.sem_inc(c_apart, 1)
                nc.vector.sem_inc(c_acc, 2)
                for u in range(RT):
                    onehot(u, u)
                mid = RT // 2 + 1
                rounds(dve, [(-0.5, blocks(0, mid)), (mid - 0.5, blocks(mid, RT))] + [(u, add(u)) for u in range(RT)],
                       [(11, stats), (12, mean_var), (13, var_eps), (RT + 0.2, inverse),
                        (RT + 1.1, masked_rstd), (RT + 1.3, shift), (RT + 2.3, normalise),
                        (RT + 16.9, maxima), (2 * RT + 1.6, minus_maxima), (2 * RT + 6, inverses),
                        (2 * RT + 7, masked_inverses), (2 * RT + 8, slice_weights), (2 * RT + 15, add_norms)])
                dve.wait_ge(e_S, NBLK)
                nc.vector.tensor_copy(sfx[:, :, :], pS[:, :, :])
                dve.wait_ge(e_nrm, NBLK)
        phase.close()

        phase = ExitStack()
        sb, ps = allocator(phase)
        wfx = sb("wfx", [P, KC, INNER])
        bfx = sb("bfx", [P, INNER])
        wo = sb("wo", [P, NPAIR, D])
        w2 = sb("w2", [P, 3, P])
        st_ = sb("st_", [P, KC, P])
        tok = sb("tok", [P, P])
        tb2 = sb("tb2", [P, P])
        den = sb("den", [P, NPAIR])
        rden = sb("rden", [P, NPAIR])
        tt = sb("tt", [P, P])
        qt = sb("qt", [P, 3, P])
        am = sb("am", [P, G])
        mxf = sb("mxf", [P, 1])
        smf = sb("smf", [P, 1])
        rcf = sb("rcf", [P, 1])
        ab = sb("ab", [P, P])
        abt = sb("abt", [P, P])
        vw = sb("vw", [P, D])
        pa = ps("pa", [P, 512])
        pb = ps("pb", [P, 512])
        pc = ps("pc", [P, 512])
        f_w = sem("f_w")
        f_z = sem("f_z")
        f_pe = sem("f_pe")
        f_chain = sem("f_chain")
        f_exp = sem("f_exp")
        f_sh = sem("f_sh")
        with nc.Block() as block:
            @block.sync
            def _(sp):
                sp.dma_start(wfx[:, :, :], w_fx.rearrange("(c p) n -> p c n", p=P)).then_inc(f_w, 16)
                sp.dma_start(bfx[:, :], b_fx.partition_broadcast(P)).then_inc(f_w, 16)
                sp.dma_start(wo[:, :, :], w_out.rearrange("(j p) n -> p j n", p=P)).then_inc(f_w, 16)
                sp.wait_ge(f_z, 1)
                for k, w in enumerate((w_q, w_k, w_v)):
                    for a in range(2):
                        q = slice(a * DH, (a + 1) * DH)
                        sp.dma_start(w2[q, k, q], w).then_inc(f_w, 16)
                sp.wait_ge(f_w, 9 * 16)

            TURNS = 7

            @block.tensor
            def _(pe):
                pe.wait_ge(f_w, 9 * 16)
                for j in range(NPAIR):
                    def turn(k):
                        pe.wait_ge(f_sh, j * TURNS + k)

                    turn(0)
                    for c in range(KC):
                        last = nc.tensor.transpose(pa[:, c * P:(c + 1) * P], sfx[:, j, c * P:(c + 1) * P], ident[:, :])
                    last.then_inc(f_pe, 1)
                    turn(1)
                    for c in range(KC):
                        last = nc.tensor.matmul(pb[:, 0:P], st_[:, c, :], wfx[:, c, j * P:(j + 1) * P],
                                                start=(c == 0), stop=(c == KC - 1))
                    last.then_inc(f_pe, 1)
                    turn(2)
                    nc.tensor.transpose(pa[:, 0:P], tb2[:, :], ident[:, :]).then_inc(f_pe, 1)
                    turn(3)
                    for k in range(3):
                        last = nc.tensor.matmul(pb[:, k * P:(k + 1) * P], w2[:, k, :], tt[:, :], start=True, stop=True)
                    last.then_inc(f_pe, 1)
                    turn(4)
                    nc.tensor.matmul(pa[:, 0:P], qt[:, 0, :], qt[:, 1, :], start=True, stop=True)
                    nc.tensor.matmul(pc[:, 0:D], qt[:, 2, :], wo[:, j, :], start=True, stop=True).then_inc(f_pe, 1)
                    turn(5)
                    nc.tensor.transpose(pb[:, 0:P], ab[:, :], ident[:, :]).then_inc(f_pe, 1)
                    turn(6)
                    nc.tensor.matmul(pa[:, 0:D], abt[:, :], vw[:, :], start=True, stop=True).then_inc(f_pe, 1)

            @block.scalar
            def _(act):
                for j in range(NPAIR):
                    act.wait_ge(f_exp, 2 * j + 1)
                    nc.scalar.activation(am[:, :], am[:, :], ACT.Exp).then_inc(f_exp, 1)

            @block.vector
            def _(dve):
                link = Chain(dve, f_chain)
                nc.vector.memset(w2[:, :, :], 0.0).then_inc(f_z, 1)
                nc.vector.memset(tb2[:, :], 0.0)
                link(nc.vector.memset(ab[:, :], 0.0))
                dve.wait_ge(f_w, 9 * 16)
                link(nc.vector.tensor_scalar(den[:, :], snorm[:, :], EPS, None, ALU.add))
                link(nc.vector.reciprocal(rden[:, :], den[:, :]))
                for j in range(NPAIR):
                    def turn(k):
                        dve.wait_ge(f_pe, j * TURNS + k + 1)

                    turn(0)
                    nc.vector.tensor_copy(st_[:, :, :].rearrange("p c n -> p (c n)"), pa[:, 0:D]).then_inc(f_sh, 1)
                    turn(1)
                    link(nc.vector.scalar_tensor_tensor(out=tok[:, :], in0=bfx[:, j * P:(j + 1) * P],
                                                        scalar=snorm[:, j:j + 1], in1=pb[:, 0:P],
                                                        op0=ALU.mult, op1=ALU.add))
                    for a in range(2):
                        q = slice(a * DH, (a + 1) * DH)
                        last = nc.vector.tensor_scalar(tb2[q, q], tok[q, q], rden[q, j:j + 1], None, ALU.mult)
                    last.then_inc(f_sh, 1)
                    turn(2)
                    nc.vector.tensor_copy(tt[:, :], pa[:, 0:P]).then_inc(f_sh, 1)
                    turn(3)
                    nc.vector.tensor_copy(qt[:, :, :].rearrange("p c n -> p (c n)"), pb[:, 0:3 * P]).then_inc(f_sh, 1)
                    turn(4)
                    link(nc.vector.tensor_copy(vw[:, :], pc[:, 0:D]))
                    for a in range(2):
                        q = slice(a * DH, (a + 1) * DH)
                        link(nc.vector.tensor_scalar(am[q, :], pa[q, a * DH:(a + 1) * DH], DH ** -0.5, None, ALU.mult))
                    link(nc.vector.tensor_reduce(mxf[:, :], am[:, :], AX.X, ALU.max))
                    nc.vector.tensor_scalar(am[:, :], am[:, :], mxf[:, :], None, ALU.subtract).then_inc(f_exp, 1)
                    dve.wait_ge(f_exp, 2 * j + 2)
                    link(nc.vector.tensor_reduce(smf[:, :], am[:, :], AX.X, ALU.add))
                    link(nc.vector.reciprocal(rcf[:, :], smf[:, :]))
                    for a in range(2):
                        q = slice(a * DH, (a + 1) * DH)
                        last = nc.vector.tensor_scalar(ab[q, q], am[q, :], rcf[q, :], None, ALU.mult)
                    last.then_inc(f_sh, 1)
                    turn(5)
                    nc.vector.tensor_copy(abt[:, :], pb[:, 0:P]).then_inc(f_sh, 1)
                    turn(6)
                    nc.vector.tensor_copy(pmat[:, j, :], pa[:, 0:D]).then_inc(f_sh, 1)
        phase.close()

        phase = ExitStack()
        sb, ps = allocator(phase)
        NB4 = 4
        st4 = sb("st4", [P, NB4, INNER])
        ob = sb("ob", [P, 2, D])
        po = ps("po", [P, 2, 512])
        g_l = sems("g_l", NB4)
        g_mm = sem("g_mm")
        g_o = sem("g_o")
        g_st = sems("g_st", 2)
        NG4 = NBLK // NB4
        with nc.Block() as block:
            @block.sync
            def _(sp):
                def load(t, q):
                    sp.dma_start(st4[:, q, :], swt_d[bass.ds(t, 1), :, :].rearrange("o p f -> (o p) f")
                                 ).then_inc(g_l[q], 16)

                for q in range(NB4):
                    load(q, q)
                with sp.Fori(0, NG4 - 1) as i:
                    for q in range(NB4):
                        sp.wait_ge(g_mm, i * NB4 + q + 1)
                        load(i * NB4 + q + NB4, q)
                for q in range(NBLK - NG4 * NB4):
                    sp.wait_ge(g_mm, (NG4 - 1) * NB4 + q + 1)
                    load(NG4 * NB4 + q, q)

            @block.gpsimd
            def _(pool):
                def store(t, par, n, rows_):
                    pool.wait_ge(g_o, n)
                    pool.wait_ge(g_l[0], 16)
                    if rows_ == P:
                        pool.dma_start(out[bass.ds(t * P, P), :], ob[:, par, :]).then_inc(g_st[par], 16)
                    else:
                        pool.dma_start(out[N - rows_:N, :], ob[0:rows_, par, :]).then_inc(g_st[par], 16)

                with pool.Fori(0, NBLK // 2 - 1) as i:
                    for par in range(2):
                        store(2 * i + par, par, 2 * i + par + 1, P)
                store(NBLK - 2, 0, NBLK - 1, P)
                store(NBLK - 1, 1, NBLK, LAST)
                for par in range(2):
                    pool.wait_ge(g_st[par], 16 * (NBLK // 2))

            def product(pe, t, q, n):
                if not isinstance(t, int) or t > 1:
                    pe.wait_ge(g_o, t - 1)
                nc.tensor.matmul(po[:, q % 2, 0:D], ones3[:, :], b2_3[:, :], start=True, stop=False)
                pe.wait_ge(g_l[q], n)
                for j in range(NPAIR):
                    last = nc.tensor.matmul(po[:, q % 2, 0:D], st4[:, q, j * P:(j + 1) * P], pmat[:, j, :],
                                            start=False, stop=(j == NPAIR - 1))
                last.then_inc(g_mm, 1)

            @block.tensor
            def _(pe):
                for q in range(NB4):
                    product(pe, q, q, 16)
                with pe.Fori(1, NG4) as i:
                    for q in range(NB4):
                        product(pe, i * NB4 + q, q, 16 * (i + 1))
                for q in range(NBLK - NG4 * NB4):
                    product(pe, NG4 * NB4 + q, q, 16 * (NG4 + 1))

            @block.vector
            def _(dve):
                with dve.Fori(0, NBLK // 2) as i:
                    for par in range(2):
                        t = 2 * i + par
                        dve.wait_ge(g_mm, t + 1)
                        dve.wait_ge(g_st[par], 16 * i)
                        nc.vector.tensor_tensor(ob[:, par, :], po[:, par, 0:D],
                                                big[:, bass.ds(t, 1), :].rearrange("p a b -> p (a b)"), ALU.add
                                                ).then_inc(g_o, 1)
        phase.close()


def kernel(**inputs):
    import numpy as np
    import concourse.bacc as bacc
    from concourse.bass_utils import run_bass_kernel_spmd

    a = {k.replace("L0_", ""): np.asarray(v) for k, v in inputs.items()}
    wqkv = a["mix_Wqkv"]
    arrays = {
        "x": a["x"], "src": a["src"], "dst": a["dst"], "edge_weight": a["edge_weight"],
        "gnn_w": a["gnn_weight"], "gnn_diag": a["gnn_learnable_diag"], "gnn_b": a["gnn_bias"],
        "wqkv": wqkv, "wqkv_t": wqkv.T, "wout_t": a["mix_Wout"].T, "bout": a["mix_bout"],
        "w_fx": a["ffn_W_fx"], "b_fx": a["ffn_b_fx"], "w_x_t": a["ffn_W_x"].T, "b_x": a["ffn_b_x"],
        "w_slice": a["ffn_W_slice"], "b_slice": a["ffn_b_slice"], "w_q": a["ffn_W_q"], "w_k": a["ffn_W_k"],
        "w_v": a["ffn_W_v"], "w_out": a["ffn_W_out"], "b_out": a["ffn_b_out"],
        "temp": a["ffn_temperature"].reshape(-1),
    }
    nc = bacc.Bacc("TRN2", target_bir_lowering=False, num_devices=1)
    arrays = {f"in_{k}": np.ascontiguousarray(v) for k, v in arrays.items()}
    aps = [nc.dram_tensor(k, v.shape, mybir.dt.from_np(v.dtype), kind="ExternalInput").ap() for k, v in arrays.items()]
    out = nc.dram_tensor("out_x", (N, D), F32, kind="ExternalOutput").ap()
    gps_layer(nc, *aps, out)
    r = run_bass_kernel_spmd(nc, [arrays], core_ids=[0])
    return r.results[0]["out_x"]
```

```python
from contextlib import ExitStack

import concourse.bass as bass
from concourse import mybir

F32 = mybir.dt.float32
BF16 = mybir.dt.bfloat16
I32 = mybir.dt.int32
ALU = mybir.AluOpType
ACT = mybir.ActivationFunctionType
AX = mybir.AxisListType

P = 128
N, D = 12500, 256
E = 200000
H, DH, G = 8, 64, 64
INNER = H * DH
NPAIR = H // 2
NBLK = -(-N // P)
LAST = N - (NBLK - 1) * P
NPAD = NBLK * P
EPS = 1e-5
KC = D // P

GC = 4
GU = 4
NGRP = NBLK * GU
ECOL = NGRP * GC
EFULL = E // P
NBK = NBLK + 1
NLO = 8
NHI = -(-NBK // NLO)
CG = 8
TMAX = (E + NBLK * (P - 1)) // P
RT = -(-TMAX // NBLK)
NTILE = NBLK * RT
NT = -(-TMAX // P) * P
NTX = NT + 2 * RT
LAG = 2
assert (ECOL * P - E) // P + 1 + TMAX <= NTX and NTILE + RT <= NTX
assert ECOL >= EFULL + 1 and ECOL % (2 * CG) == 0


class Chain:

    def __init__(self, engine, sem):
        self.engine, self.sem, self.n = engine, sem, 0

    def __call__(self, instruction):
        self.n += 1
        instruction.then_inc(self.sem, 1)
        self.engine.wait_ge(self.sem, self.n)


def split_rows(link, vec, out, rows, masks, t1, t2, acc):
    n = rows.shape[1]
    b = out
    link(vec.tensor_copy(b, rows))
    link(vec.tensor_tensor(t1, rows, b, ALU.subtract))
    link(vec.tensor_scalar(acc, b, masks[0:3, 0:1], None, ALU.mult))
    link(vec.tensor_copy(b, t1))
    link(vec.tensor_tensor(t2, t1, b, ALU.subtract))
    for k, part in ((1, b), (2, t2)):
        link(vec.tensor_scalar(t1, part, masks[0:3, k:k + 1], None, ALU.mult))
        link(vec.tensor_tensor(acc, acc, t1, ALU.add))
    link(vec.tensor_copy(b, acc))


def gps_layer(nc, x, src, dst, edge_weight, gnn_w, gnn_diag, gnn_b, wqkv, wqkv_t, wout_t, bout,
              w_fx, b_fx, w_x_t, b_x, w_slice, b_slice, w_q, w_k, w_v, w_out, b_out, temp, out):
    with ExitStack() as ctx:
        def allocator(stack):
            def sb(name, shape, dt=F32):
                return stack.enter_context(nc.sbuf_tensor(name, shape, dt))

            def ps(name, shape, dt=F32):
                return stack.enter_context(nc.psum_tensor(name, shape, dt))
            return sb, ps

        def sem(name):
            return ctx.enter_context(nc.semaphore(name))

        def sems(name, n):
            return [sem(f"{name}{k}") for k in range(n)]

        xn_d = nc.dram_tensor("xn_table", (NPAD, D), F32).ap()
        xnt_d = nc.dram_tensor("xn_transposed", (NBLK, P, D), F32).ap()
        rec_d = nc.dram_tensor("sorted_edges", (NTX * P, 4), F32).ap()
        tb_d = nc.dram_tensor("tile_blocks", (NTX,), I32).ap()
        swt_d = nc.dram_tensor("slice_weights_t", (NBLK, P, INNER), F32).ap()

        def pipeline(engine, count, width, steps):
            depth = max(int(slot // width) for slot, _ in steps)
            order = sorted(steps, key=lambda q: q[0] % width)

            def round_(i, has):
                for slot, step in order:
                    late = int(slot // width)
                    if has(late):
                        step(i - late)

            for i in range(depth):
                round_(i, lambda late: late <= i)
            with engine.Fori(depth, count) as i:
                round_(i, lambda late: True)
            for i in range(count, count + depth):
                round_(i, lambda late: i - late < count)

        sb, _ = allocator(ctx)
        big = sb("big", [P, NBLK, D])
        ident = sb("ident", [P, P])
        ones3 = sb("ones3", [3, P], BF16)
        mask = sb("mask", [P, NBLK])
        tblk = sb("tblk", [1, NTX], I32)
        apart = sb("apart", [1, 1], I32)
        base0 = sb("base0", [P, NBK])
        slt = sb("slt", [P, P], BF16)
        onesb = sb("onesb", [P, P], BF16)
        iob = sb("iob", [P, NBK], BF16)
        ion = sb("ion", [P, P])
        wx1 = sb("wx1", [P, 2 * KC, D])
        b2_3 = sb("b2_3", [3, D], BF16)

        def row_of(t):
            return big[:, bass.ds(t, 1), :].rearrange("p a b -> p (a b)")

        passed = sem("passed")

        edges = ExitStack()
        esb, _ = allocator(edges)
        rec = esb("rec", [P, ECOL, 4])
        blk = esb("blk", [P, ECOL + GU * GC], BF16)
        zer = esb("zer", [P, 512])
        ohz = esb("ohz", [P, CG * NLO], BF16)
        oh_shape = [P, GC, NBK]

        phase = ExitStack()
        sb, ps = allocator(phase)
        NCG = ECOL // CG
        CB = 14
        NCB = NCG // CB
        assert NCB * CB == NCG and NCB % 2 == 0
        srci = sb("srci", [P, ECOL], I32)
        dsti = sb("dsti", [P, ECOL], I32)
        wf = sb("wf", [P, ECOL])
        hi = sb("hi", [P, ECOL], I32)
        lo = sb("lo", [P, ECOL], I32)
        ohh = sb("ohh", [P, 2, CB * CG, NHI], BF16)
        ohl = sb("ohl", [P, 2, CB * CG, NLO], BF16)
        io13 = sb("io13", [P, NHI])
        io8 = sb("io8", [P, NLO])
        dmask = sb("dmask", [CG * NHI, CG, NLO])
        hsel = sb("hsel", [CG * NHI, CG, NHI])
        hmask = sb("hmask", [CG * NHI, NHI])
        cdiag = sb("cdiag", [CG * NHI, CG, NLO])
        csum = sb("csum", [CG * NHI, NLO])
        cspread = sb("cspread", [CG * NHI, NHI, NLO])
        onesf = sb("onesf", [CG * NHI, P])
        ntl = sb("ntl", [P, NBK], I32)
        ntf = sb("ntf", [P, NBK])
        incl = sb("incl", [P, NBK])
        excl = sb("excl", [P, NBK])
        onek = sb("onek", [P, NBK])
        limit = sb("limit", [P, NBLK])
        over = sb("over", [P, NBLK])
        tno = sb("tno", [P, NT // P])
        tcm = sb("tcm", [P, NT // P, NBLK])
        tbf = sb("tbf", [P, NT // P])
        tbi = sb("tbi", [P, NT // P], I32)
        pc2 = ps("pc2", [CG * NHI, CG, NLO])
        pcnt = ps("pcnt", [P, NHI, NLO])

        a_src = sem("a_src")
        a_rest = sem("a_rest")
        a_pads = sem("a_pads")
        a_zero = sem("a_zero")
        a_zrec = sem("a_zrec")
        a_pool = sem("a_pool")
        a_poolc = sem("a_poolc")
        a_recz = sem("a_recz")
        a_chain = sem("a_chain")
        a_oh = sem("a_oh")
        a_ohfree = sems("a_ohfree", 2)
        a_spread = sem("a_spread")
        a_cnt = sem("a_cnt")
        a_tb = sem("a_tb")
        a_tbd = sem("a_tbd")
        NPOOL = 15
        zfull = NTX * 4 // 512

        with nc.Block() as block:
            @block.sync
            def _(sp):
                sp.dma_start(srci[:, 0:EFULL], src[0:EFULL * P].rearrange("(p c) -> p c", p=P)).then_inc(a_src, 16)
                sp.wait_ge(a_pads, 1)
                sp.dma_start(srci[0:E - EFULL * P, EFULL:EFULL + 1],
                             src[EFULL * P:E].rearrange("(p o) -> p o", o=1)).then_inc(a_src, 16)
                sp.dma_start(dsti[:, 0:EFULL], dst[0:EFULL * P].rearrange("(p c) -> p c", p=P)).then_inc(a_rest, 16)
                sp.dma_start(dsti[0:E - EFULL * P, EFULL:EFULL + 1],
                             dst[EFULL * P:E].rearrange("(p o) -> p o", o=1)).then_inc(a_rest, 16)
                sp.dma_start(wf[:, 0:EFULL],
                             edge_weight[0:EFULL * P].rearrange("(p c) -> p c", p=P)).then_inc(a_rest, 16)
                sp.dma_start(wf[0:E - EFULL * P, EFULL:EFULL + 1],
                             edge_weight[EFULL * P:E].rearrange("(p o) -> p o", o=1)).then_inc(a_rest, 16)
                sp.wait_ge(a_tb, 1)
                sp.dma_start(tb_d[0:NT].rearrange("(p j) -> p j", p=P), tbi[:, :]).then_inc(a_tbd, 16)
                sp.wait_ge(a_tbd, 16)
                sp.dma_start(tblk[0:1, 0:NT], tb_d[0:NT].rearrange("(o t) -> o t", o=1)).then_inc(a_tbd, 16)
                sp.wait_ge(a_tbd, 32)

            @block.gpsimd
            def _(pool):
                def number(out_, n, step=0):
                    pool.iota(out_, pattern=[[1, n]], base=0, channel_multiplier=step,
                              allow_small_or_imprecise_dtypes=True).then_inc(a_pool, 1)

                number(io13[:, :], NHI)
                number(io8[:, :], NLO)
                number(iob[:, :], NBK)
                number(ion[:, :], P)
                number(tno[:, :], NT // P, NT // P)
                pool.iota(limit[:, :], pattern=[[RT, NBLK]], base=RT * LAG, channel_multiplier=0,
                          allow_small_or_imprecise_dtypes=True).then_inc(a_pool, 1)
                pool.memset(onesb[:, :], 1.0).then_inc(a_pool, 1)
                pool.memset(onesf[:, :], 1.0).then_inc(a_pool, 1)
                pool.memset(ones3[:, :], 1.0).then_inc(a_pool, 1)
                pool.memset(onek[:, :], 1.0).then_inc(a_pool, 1)
                pool.memset(ident[:, :], 0.0).then_inc(a_poolc, 1)
                pool.memset(slt[:, :], 1.0).then_inc(a_poolc, 1)
                pool.memset(mask[:, :], 1.0).then_inc(a_poolc, 1)
                pool.memset(hsel[:, :, :], 0.0).then_inc(a_poolc, 1)
                pool.memset(dmask[:, :, :], 1.0).then_inc(a_poolc, 1)
                pool.wait_ge(a_poolc, 5)
                pool.affine_select(out=ident[:, :], in_=ident[:, :], compare_op=ALU.not_equal, fill=1.0,
                                   base=0, pattern=[[-1, P]], channel_multiplier=1).then_inc(a_pool, 1)
                pool.affine_select(out=slt[:, :], in_=slt[:, :], compare_op=ALU.is_ge, fill=0.0,
                                   base=-1, pattern=[[1, P]], channel_multiplier=-1).then_inc(a_pool, 1)
                pool.affine_select(out=mask[:, :], in_=mask[:, :], compare_op=ALU.is_ge, fill=0.0,
                                   base=N - 1, pattern=[[-P, NBLK]], channel_multiplier=-1).then_inc(a_pool, 1)
                pool.affine_select(out=hsel[:, :, :], in_=hsel[:, :, :], compare_op=ALU.not_equal, fill=1.0,
                                   base=0, pattern=[[-NHI, CG], [-1, NHI]], channel_multiplier=1).then_inc(a_pool, 1)
                pool.affine_select(out=dmask[:, :, :], in_=dmask[:, :, :], compare_op=ALU.is_ge, fill=0.0,
                                   base=0, pattern=[[-NHI, CG], [0, NLO]], channel_multiplier=1).then_inc(a_poolc, 1)
                pool.wait_ge(a_poolc, 6)
                pool.affine_select(out=dmask[:, :, :], in_=dmask[:, :, :], compare_op=ALU.is_ge, fill=0.0,
                                   base=NHI - 1, pattern=[[NHI, CG], [0, NLO]], channel_multiplier=-1
                                   ).then_inc(a_pool, 1)
                pool.memset(rec[:, :, :], 0.0).then_inc(a_recz, 1)

            @block.scalar
            def _(act):
                act.wait_ge(a_zero, 1)
                rows_ = NTX * P
                for k in range(zfull):
                    act.dma_start(rec_d[k * P * P:(k + 1) * P * P, :].rearrange("(p r) f -> p (r f)", p=P),
                                  zer[:, :]).then_inc(a_zrec, 16)
                act.dma_start(rec_d[zfull * P * P:rows_, :].rearrange("(p r) f -> p (r f)", p=P),
                              zer[:, 0:NTX * 4 - zfull * 512]).then_inc(a_zrec, 16)
                act.wait_ge(a_rest, 64)
                act.wait_ge(a_recz, 1)
                nc.scalar.copy(rec[:, :, 0], dsti[:, :])
                nc.scalar.copy(rec[:, :, 2], wf[:, :])
                act.wait_ge(a_zrec, 16 * (zfull + 1))

            @block.tensor
            def _(pe):
                pe.wait_ge(a_pool, NPOOL)
                pe.wait_ge(a_zero, 1)
                nc.tensor.matmul(pc2[:, :, :], onesb[:, 0:CG * NHI], ohz[:, :].rearrange("p (c l) -> p c l", l=NLO),
                                 start=True, stop=False, skip_group_check=True)
                with pe.Fori(0, NCB // 2) as i:
                    for par in range(2):
                        pe.wait_ge(a_oh, 4 * i + 2 * par + 2)
                        for g in range(CB):
                            cols = slice(g * CG, (g + 1) * CG)
                            last = nc.tensor.matmul(pc2[:, :, :], ohh[:, par, cols, :], ohl[:, par, cols, :],
                                                    start=False, stop=False, skip_group_check=True)
                        last.then_inc(a_ohfree[par], 1)
                pe.wait_ge(a_spread, 1)
                nc.tensor.matmul(pcnt[:, :, :], onesf[:, :], cspread[:, :, :], start=True, stop=True).then_inc(a_cnt, 1)

            @block.vector
            def _(dve):
                link = Chain(dve, a_chain)
                nc.vector.memset(srci[:, EFULL:ECOL], NBLK * P)
                nc.vector.memset(dsti[:, EFULL:ECOL], 0)
                nc.vector.memset(wf[:, EFULL:ECOL], 0.0).then_inc(a_pads, 1)
                nc.vector.memset(tblk[0:1, NT:NTX], 0)
                nc.vector.memset(ohz[:, :], 0.0)
                nc.vector.memset(zer[:, :], 0.0).then_inc(a_zero, 1)
                dve.wait_ge(a_src, 32)
                link(nc.vector.tensor_scalar(hi[:, :], srci[:, :], 10, None, ALU.arith_shift_right))
                link(nc.vector.tensor_scalar(lo[:, :], srci[:, :], 7, NLO - 1, ALU.arith_shift_right, ALU.bitwise_and))
                dve.wait_ge(a_pool, NPOOL)
                with dve.Fori(0, NCB // 2) as i:
                    for par in range(2):
                        dve.wait_ge(a_ohfree[par], i)
                        cols = bass.ds((2 * i + par) * (CB * CG), CB * CG)
                        for one, digit, number, n in ((ohh, hi, io13, NHI), (ohl, lo, io8, NLO)):
                            shape = [P, CB * CG, n]
                            nc.vector.tensor_tensor(one[:, par, :, :], digit[:, cols].unsqueeze(2).to_broadcast(shape),
                                                    number[:, :].unsqueeze(1).to_broadcast(shape),
                                                    ALU.is_equal).then_inc(a_oh, 1)
                for par in range(2):
                    dve.wait_ge(a_ohfree[par], NCB // 2)
                link(nc.vector.tensor_tensor(cdiag[:, :, :], pc2[:, :, :], dmask[:, :, :], ALU.mult))
                link(nc.vector.tensor_reduce(csum[:, :], cdiag[:, :, :].rearrange("p c l -> p l c"), AX.X, ALU.add))
                link(nc.vector.tensor_reduce(hmask[:, :], hsel[:, :, :].rearrange("p c h -> p h c"), AX.X, ALU.add))
                shape = [CG * NHI, NHI, NLO]
                nc.vector.tensor_tensor(cspread[:, :, :], csum[:, :].unsqueeze(1).to_broadcast(shape),
                                        hmask[:, :].unsqueeze(2).to_broadcast(shape), ALU.mult).then_inc(a_spread, 1)
                dve.wait_ge(a_cnt, 1)
                count = pcnt[:, :, :].rearrange("p h l -> p (h l)")[:, 0:NBK]
                link(nc.vector.tensor_scalar(ntl[:, :], count, float(P - 1), None, ALU.add))
                link(nc.vector.tensor_scalar(ntl[:, :], ntl[:, :], 7, None, ALU.arith_shift_right))
                link(nc.vector.tensor_copy(ntf[:, :], ntl[:, :]))
                link(nc.vector.tensor_tensor_scan(incl[:, :], onek[:, :], ntf[:, :], 0.0, ALU.mult, ALU.add))
                link(nc.vector.tensor_tensor(excl[:, :], incl[:, :], ntf[:, :], ALU.subtract))
                link(nc.vector.tensor_scalar(base0[:, :], excl[:, :], float(P), None, ALU.mult))
                shape = [P, NT // P, NBLK]
                link(nc.vector.tensor_tensor(tcm[:, :, :], incl[:, 0:NBLK].unsqueeze(1).to_broadcast(shape),
                                             tno[:, :].unsqueeze(2).to_broadcast(shape), ALU.is_le))
                link(nc.vector.tensor_reduce(tbf[:, :], tcm[:, :, :], AX.X, ALU.add))
                nc.vector.tensor_scalar(tbi[:, :], tbf[:, :], float(NBLK - 1), None, ALU.min).then_inc(a_tb, 1)
                link(nc.vector.tensor_tensor(over[:, :], incl[:, 0:NBLK], limit[:, :], ALU.is_gt))
                with nc.allow_low_precision(reason="0 or 1"):
                    link(nc.vector.tensor_reduce(apart[:, :], over[0:1, :], AX.X, ALU.max))
                dve.wait_ge(a_recz, 1)
                link(nc.vector.tensor_scalar(hi[:, :], srci[:, :], 7, None, ALU.arith_shift_right))
                link(nc.vector.tensor_scalar(lo[:, :], srci[:, :], P - 1, None, ALU.bitwise_and))
                link(nc.vector.tensor_copy(blk[:, 0:ECOL], hi[:, :]))
                link(nc.vector.memset(blk[:, ECOL:ECOL + GU * GC], 0.0))
                link(nc.vector.tensor_copy(rec[:, :, 1], lo[:, :]))
        phase.close()

        phase = ExitStack()
        sb, ps = allocator(phase)
        iob_b = iob[:, :].unsqueeze(1).to_broadcast(oh_shape)
        wkv = sb("wkv", [P, KC, 2 * INNER])
        wmean = sb("wmean", [P, KC, 2 * H])
        oh = sb("ohb", [P, GU, GC, NBK], BF16)
        prod = sb("prod", [P, 2, GC, NBK])
        pos = sb("pos", [P, GU, GC], I32)
        recs = sb("recs", [P, GU, GC, 4])
        base = sb("base", [P, 2, NBK])
        xs = sb("xs", [P, D])
        xnb = sb("xnb", [P, D])
        st6 = sb("st6b", [P, 6])
        mv = sb("mvb", [P, 2])
        sd = sb("sdb", [P, 4])
        xnt = sb("xnt", [P, KC, P])
        sq = sb("sq", [P, 2 * H, DH])
        ksb = sb("ksb", [P, INNER])
        vsb = sb("vsb", [P, H, DH])
        ss = sb("ss", [P, 2 * H])
        ms = sb("ms", [P, 2 * H])
        sc = sb("sc", [P, H])
        rt = sb("rt", [P, H])
        rs = sb("rs", [P, H])
        ndots = sb("ndots", [P, NPAIR, P])
        wq = sb("wq", [P, NPAIR, D])
        wot = sb("wot", [P, NPAIR, D])
        at = sb("at", [P, NPAIR, D])
        pr = ps("pr", [P, 2, 512])
        pt = ps("pt", [P, 512])
        pkv = ps("pkv", [P, 2, 512])
        pdots = ps("pdots", [P, 512])
        ptr = ps("ptr", [P, 512])

        def ranks(k):
            return pr[:, k, 0:GC * NBK].rearrange("p (c b) -> p c b", b=NBK)

        b_wkv = sem("b_wkv")
        b_chain = sem("b_chain")
        b_wc = sem("b_wc")
        b_oh = sem("b_oh")
        b_ranks = sem("b_ranks")
        b_total = sem("b_total")
        b_base = sem("b_base")
        b_prod = sems("b_prod", 2)
        b_pos = sems("b_pos", GU)
        b_rec = sems("b_rec", GU)
        b_scat = sems("b_scat", GU)
        b_xs = sem("b_xs")
        b_stat = sem("b_stat")
        b_var = sem("b_var")
        b_sd = sem("b_sd")
        b_norm = sem("b_norm")
        b_xn = sem("b_xn")
        b_xnst = sem("b_xnst")
        b_tr = sem("b_tr")
        b_xnt = sem("b_xnt")
        b_xst = sem("b_xst")
        b_kv = sem("b_kv")
        b_sq = sem("b_sq")
        b_k = sem("b_k")
        b_ss = sem("b_ss")
        b_ms = sem("b_ms")
        b_sc = sem("b_sc")
        b_rt = sem("b_rt")
        b_rs = sem("b_rs")
        b_vs = sem("b_vs")
        b_dots = sem("b_dots")
        b_w = sem("b_w")
        b_ndz = sem("b_ndz")
        b_nd = sem("b_nd")
        b_at = sem("b_at")
        b_ats = sem("b_ats")
        b_m = sem("b_m")
        with nc.Block() as block:
            @block.sync
            def _(sp):
                def load(t, rows_):
                    sp.wait_ge(b_xn, t)
                    if rows_ == P:
                        sp.dma_start(xs[:, :], x[bass.ds(t * P, P), :]).then_inc(b_xs, 16)
                    else:
                        sp.dma_start(xs[0:rows_, :], x[N - rows_:N, :]).then_inc(b_xs, 16)

                def store_rows(t):
                    sp.wait_ge(b_xn, t + 1)
                    sp.dma_start(xn_d[bass.ds(t * P, P), :], xnb[:, :]).then_inc(b_xnst, 16)

                def store_transposed(t):
                    sp.wait_ge(b_xnt, t + 1)
                    sp.dma_start(xnt_d[bass.ds(t, 1), :, :].rearrange("o p f -> (o p) f"),
                                 xnt[:, :, :].rearrange("p c n -> p (c n)")).then_inc(b_xst, 16)

                sp.dma_start(xs[:, :], x[0:P, :]).then_inc(b_xs, 16)
                with sp.Fori(0, NBLK - 2) as t:
                    store_rows(t)
                    load(t + 1, P)
                    store_transposed(t)
                store_rows(NBLK - 2)
                load(NBLK - 1, LAST)
                store_transposed(NBLK - 2)
                store_rows(NBLK - 1)
                store_transposed(NBLK - 1)
                sp.wait_ge(b_xnst, 16 * NBLK)
                sp.wait_ge(b_xst, 16 * NBLK)

            @block.gpsimd
            def _(pool):
                with pool.Fori(1, NBLK + 1) as turn:
                    for u in range(GU):
                        pool.wait_ge(a_zrec, 16)
                        pool.wait_ge(b_pos[u], turn)
                        pool.wait_ge(b_rec[u], turn)
                        for c in range(GC):
                            pool.indirect_dma_start(
                                out=rec_d, out_offset=bass.IndirectOffsetOnAxis(ap=pos[:, u, c:c + 1], axis=0),
                                in_=recs[:, u, c, :], in_offset=None).then_inc(b_scat[u], 16)
                for u in range(GU):
                    pool.wait_ge(b_scat[u], 16 * GC * NBLK)

            @block.scalar
            def _(act):
                act.dma_start(wkv[:, :, :], wqkv_t[:, INNER:3 * INNER].rearrange("(c p) n -> p c n", p=P)
                              ).then_inc(b_wkv, 16)
                act.dma_start(wq[:, :, :], wqkv[0:INNER, :].rearrange("(j p) f -> p j f", p=P)).then_inc(b_w, 16)
                act.dma_start(wot[:, :, :], wout_t.rearrange("(j p) f -> p j f", p=P)).then_inc(b_w, 16)
                act.wait_ge(b_total, 1)
                nc.scalar.copy(base[:, 0, :], pt[:, 0:NBK]).then_inc(b_base, 1)

                def stage_records(u):
                    def step(i):
                        act.wait_ge(b_scat[u], 16 * GC * i)
                        nc.scalar.copy(recs[:, u, :, :], rec[:, bass.ds((i * GU + u) * GC, GC), :]
                                       ).then_inc(b_rec[u], 1)
                    return step

                def copy_total(u):
                    def step(i):
                        act.wait_ge(b_total, i * GU + u + 2)
                        nc.scalar.copy(base[:, (u + 1) % 2, :], pt[:, 0:NBK]).then_inc(b_base, 1)
                    return step

                def root(t):
                    act.wait_ge(b_var, t + 1)
                    act.wait_ge(b_norm, 3 * t)
                    nc.scalar.activation(sd[:, 1:2], sd[:, 0:1], ACT.Sqrt).then_inc(b_sd, 1)

                def xn_t(t):
                    act.wait_ge(b_tr, t + 1)
                    act.wait_ge(b_kv, t)
                    act.wait_ge(b_xst, 16 * t)
                    nc.scalar.copy(xnt[:, :, :].rearrange("p c n -> p (c n)"), ptr[:, 0:D]).then_inc(b_xnt, 1)

                def clear_sums(t):
                    nc.scalar.copy(row_of(t), zer[:, 0:D])

                def squares(t):
                    act.wait_ge(b_kv, t + 1)
                    act.wait_ge(b_ss, t)
                    for k in range(2):
                        nc.scalar.activation(sq[:, k * H:(k + 1) * H, :].rearrange("p h d -> p (h d)"), pkv[:, k, :],
                                             ACT.Square).then_inc(b_sq, 1)

                def keep_keys(t):
                    act.wait_ge(b_dots, t)
                    nc.scalar.copy(ksb[:, :], pkv[:, 0, :]).then_inc(b_k, 1)

                def root_kv(t):
                    act.wait_ge(b_sc, t + 1)
                    act.wait_ge(b_rs, t)
                    nc.scalar.activation(rt[:, :], sc[:, :], ACT.Sqrt).then_inc(b_rt, 1)

                pipeline(act, NBLK, GU, [(u + 0.1, stage_records(u)) for u in range(GU)]
                         + [(u + 0.5, copy_total(u)) for u in range(GU)]
                         + [(1.6, root), (2.6, clear_sums), (3.8, xn_t), (GU + 2.1, squares), (GU + 2.2, keep_keys),
                            (GU + 3.7, root_kv)])

            @block.tensor
            def _(pe):
                nc.tensor.matmul(pt[:, 0:NBK], ident[:, :], base0[:, :], start=True, stop=False,
                                 skip_group_check=True).then_inc(b_total, 1)
                nc.tensor.matmul(pdots[:, :], ident[:, :], zer[:, :], start=True, stop=False, skip_group_check=True)

                def rank(u):
                    par, k = u % 2, u // 2
                    r = ranks(par)

                    def step(i):
                        pe.wait_ge(b_oh, i * GU + u + 1)
                        pe.wait_ge(b_prod[par], 2 * i + k)
                        nc.tensor.matmul(r, slt[:, :], oh[:, u, :, :], start=True, stop=False, skip_group_check=True)
                        for s in range(1, GC):
                            nc.tensor.matmul(r[:, s:GC, :], onesb[:, :], oh[:, u, 0:GC - s, :], start=False, stop=False,
                                             skip_group_check=True)
                        pe.wait_ge(b_base, i * GU + u + 1)
                        nc.tensor.matmul(r, ident[:, :], base[:, u % 2, :].unsqueeze(1).to_broadcast(oh_shape),
                                         start=False, stop=True, skip_group_check=True).then_inc(b_ranks, 1)
                        for c in range(GC):
                            last = nc.tensor.matmul(pt[:, 0:NBK], onesb[:, :], oh[:, u, c, :], start=False, stop=False,
                                                    skip_group_check=True)
                        last.then_inc(b_total, 1)
                    return step

                def transpose_xn(t):
                    pe.wait_ge(b_xn, t + 1)
                    pe.wait_ge(b_xnt, t)
                    for c in range(KC):
                        last = nc.tensor.transpose(ptr[:, c * P:(c + 1) * P], xnb[:, c * P:(c + 1) * P], ident[:, :])
                    last.then_inc(b_tr, 1)

                def keys_values(k):
                    for c in range(KC):
                        last = nc.tensor.matmul(pkv[:, k, :], xnt[:, c, :], wkv[:, c, k * INNER:(k + 1) * INNER],
                                                start=(c == 0), stop=(c == KC - 1))
                    return last

                def keys(t):
                    pe.wait_ge(b_xnt, t + 1)
                    pe.wait_ge(b_k, t)
                    pe.wait_ge(b_wc, 1)
                    keys_values(0)

                def values(t):
                    pe.wait_ge(b_vs, t)
                    keys_values(1).then_inc(b_kv, 1)

                def dots(t):
                    pe.wait_ge(b_k, t + 1)
                    pe.wait_ge(b_vs, t + 1)
                    for j in range(NPAIR):
                        last = nc.tensor.matmul(pdots[:, j * P:(j + 1) * P], ksb[:, j * P:(j + 1) * P],
                                                vsb[:, 2 * j:2 * j + 2, :], start=False, stop=False,
                                                skip_group_check=True)
                    last.then_inc(b_dots, 1)

                pipeline(pe, NBLK, GU, [(u, rank(u)) for u in range(GU)]
                         + [(3.5, transpose_xn), (GU + 0.5, keys), (GU + 1.5, values), (2 * GU + 1.7, dots)])
                pe.wait_ge(b_nd, 1)
                pe.wait_ge(b_w, 32)
                for j in range(NPAIR):
                    q = slice(j % 2 * D, (j % 2 + 1) * D)
                    last = nc.tensor.matmul(pkv[:, j // 2, q], ndots[:, j, :], wq[:, j, :], start=True, stop=True)
                    if j % 2:
                        last.then_inc(b_at, 1)
                pe.wait_ge(b_ats, 2)
                for c, pm in enumerate((pdots, ptr)):
                    for j in range(NPAIR):
                        last = nc.tensor.matmul(pm[:, 0:D], at[:, j, c * P:(c + 1) * P], wot[:, j, :],
                                                start=(j == 0), stop=(j == NPAIR - 1))
                last.then_inc(b_m, 1)

            @block.vector
            def _(dve):
                link = Chain(dve, b_chain)
                nc.vector.memset(ndots[:, :, :], 0.0).then_inc(b_ndz, 1)

                def centre_weights():
                    dve.wait_ge(b_wkv, 16)
                    for c in range(KC):
                        w3 = wkv[:, c, :].rearrange("p (h d) -> p h d", d=DH)
                        link(nc.vector.tensor_reduce(wmean[:, c, :], w3, AX.X, ALU.add))
                        link(nc.vector.tensor_scalar(wmean[:, c, :], wmean[:, c, :], -1.0 / DH, None, ALU.mult))
                        link(nc.vector.tensor_tensor(w3, w3, wmean[:, c, :].unsqueeze(2).to_broadcast([P, 2 * H, DH]),
                                                     ALU.add))
                    nc.vector.sem_inc(b_wc, 1)

                def onehot(i, u):
                    cols = blk[:, bass.ds((i * GU + u) * GC, GC)].unsqueeze(2).to_broadcast(oh_shape)
                    nc.vector.tensor_tensor(oh[:, u, :, :], cols, iob_b, ALU.is_equal).then_inc(b_oh, 1)

                def own_rank(u):
                    def step(i):
                        dve.wait_ge(b_ranks, i * GU + u + 1)
                        nc.vector.tensor_tensor(prod[:, u % 2, :, :], ranks(u % 2), oh[:, u, :, :],
                                                ALU.mult).then_inc(b_prod[u % 2], 1)
                    return step

                def next_onehot(u):
                    def step(i):
                        dve.wait_ge(b_prod[u % 2], 2 * i + u // 2 + 1)
                        dve.wait_ge(b_total, i * GU + u + 2)
                        onehot(i + 1, u)
                    return step

                def place(u):
                    def step(i):
                        dve.wait_ge(b_prod[u % 2], 2 * i + u // 2 + 1)
                        dve.wait_ge(b_scat[u], 16 * GC * i)
                        with nc.allow_low_precision(reason="one whole number below 2^24 among zeros"):
                            nc.vector.tensor_reduce(pos[:, u, :], prod[:, u % 2, :, :], AX.X, ALU.add
                                                    ).then_inc(b_pos[u], 1)
                    return step

                def stats(t):
                    dve.wait_ge(b_xs, 16 * (t + 1))
                    nc.vector.bn_stats(st6[:, :], xs[:, :]).then_inc(b_stat, 1)

                def mean_var(t):
                    dve.wait_ge(b_stat, 2 * t + 1)
                    nc.vector.sem_inc(passed, 1)
                    nc.vector.bn_aggr(mv[:, :], st6[:, :]).then_inc(b_stat, 1)

                def var_eps(t):
                    dve.wait_ge(b_stat, 2 * t + 2)
                    nc.vector.tensor_scalar(sd[:, 0:1], mv[:, 1:2], EPS, None, ALU.add).then_inc(b_var, 1)

                def inverse(t):
                    dve.wait_ge(b_sd, t + 1)
                    nc.vector.reciprocal(sd[:, 2:3], sd[:, 1:2]).then_inc(b_norm, 1)

                def masked_rstd(t):
                    dve.wait_ge(b_norm, 3 * t + 1)
                    nc.vector.tensor_tensor(sd[:, 2:3], sd[:, 2:3], mask[:, bass.ds(t, 1)], ALU.mult
                                            ).then_inc(b_norm, 1)

                def shift(t):
                    dve.wait_ge(b_norm, 3 * t + 2)
                    nc.vector.scalar_tensor_tensor(out=sd[:, 3:4], in0=mv[:, 0:1], scalar=-1.0, in1=sd[:, 2:3],
                                                   op0=ALU.mult, op1=ALU.mult).then_inc(b_norm, 1)

                def normalise(t):
                    dve.wait_ge(b_norm, 3 * t + 3)
                    dve.wait_ge(b_xnst, 16 * t)
                    dve.wait_ge(b_tr, t)
                    nc.vector.tensor_scalar(xnb[:, :], xs[:, :], sd[:, 2:3], sd[:, 3:4], ALU.mult, ALU.add
                                            ).then_inc(b_xn, 1)

                def square_sums(t):
                    dve.wait_ge(b_sq, 2 * t + 2)
                    nc.vector.tensor_reduce(ss[:, :], sq[:, :, :], AX.X, ALU.add).then_inc(b_ss, 1)

                def variances(t):
                    dve.wait_ge(b_ss, t + 1)
                    nc.vector.tensor_scalar(ms[:, :], ss[:, :], 1.0 / DH, EPS, ALU.mult, ALU.add).then_inc(b_ms, 1)

                def products(t):
                    dve.wait_ge(b_ms, t + 1)
                    nc.vector.tensor_tensor(sc[:, :], ms[:, 0:H], ms[:, H:2 * H], ALU.mult).then_inc(b_sc, 1)

                def inverse_kv(t):
                    dve.wait_ge(b_rt, t + 1)
                    nc.vector.reciprocal(rs[:, :], rt[:, :]).then_inc(b_rs, 1)

                def scaled_values(t):
                    dve.wait_ge(b_rs, t + 1)
                    dve.wait_ge(b_dots, t)
                    nc.vector.tensor_tensor(vsb[:, :, :], pkv[:, 1, :].rearrange("p (h d) -> p h d", d=DH),
                                            rs[:, :].unsqueeze(2).to_broadcast([P, H, DH]), ALU.mult).then_inc(b_vs, 1)

                for u in range(GU):
                    onehot(0, u)
                def centre_at_first(t):
                    if isinstance(t, int) and t == 0:
                        centre_weights()

                pipeline(dve, NBLK, GU, [(2.5, centre_at_first)] + [(u, own_rank(u)) for u in range(GU)]
                         + [(u + 1.2, next_onehot(u)) for u in range(GU)] + [(u + 0.4, place(u)) for u in range(GU)]
                         + [(0.4, stats), (0.7, mean_var), (1.2, var_eps), (2.2, inverse), (2.4, masked_rstd),
                            (2.7, shift), (3.1, normalise), (GU + 2.7, square_sums), (GU + 3.1, variances),
                            (GU + 3.4, products), (2 * GU + 0.4, inverse_kv), (2 * GU + 0.7, scaled_values)])
                dve.wait_ge(b_dots, NBLK)
                dve.wait_ge(b_ndz, 1)
                for j in range(NPAIR):
                    for a in range(2):
                        q = slice(a * DH, (a + 1) * DH)
                        last = nc.vector.tensor_scalar(ndots[q, j, q], pdots[q, j * P + a * DH:j * P + (a + 1) * DH],
                                                       1.0 / N, None, ALU.mult)
                last.then_inc(b_nd, 1)
                for k in range(2):
                    dve.wait_ge(b_at, k + 1)
                    nc.vector.tensor_copy(at[:, 2 * k:2 * k + 2, :].rearrange("p j f -> p (j f)"), pkv[:, k, :]
                                          ).then_inc(b_ats, 1)
                dve.wait_ge(b_m, 1)
                nc.vector.tensor_copy(wx1[:, 0, :], pdots[:, 0:D])
                nc.vector.tensor_copy(wx1[:, 1, :], ptr[:, 0:D])
        phase.close()
        edges.close()

        sb, _ = allocator(ctx)
        sfx = sb("sfx", [P, NPAIR, D])
        snorm = sb("snorm", [P, NPAIR])
        pmat = sb("pmat", [P, NPAIR, D])

        phase = ExitStack()
        sb, ps = allocator(phase)
        NCH = NT // P
        gidx = sb("gidx", [P, NTX], I32)
        place_c = sb("place_c", [P, NTX])
        weight_c = sb("weight_c", [P, NTX])
        idxs = sb("idxs", [P, RT], I32)
        wls = sb("wls", [P, KC, INNER])
        b1_3 = sb("b1_3", [3, D], BF16)
        bl_3 = sb("bl_3", [3, INNER], BF16)
        zer = sb("zer_c", [P, INNER])
        first = ExitStack()
        fsb, _ = allocator(first)
        tl = fsb("tl", [P, NCH, P, 4])
        gw = fsb("gw", [P, KC, D])
        diag = fsb("diag", [P, KC])
        wxt = fsb("wxt", [DH, H, D])
        wsl = fsb("wsl", [DH, G])
        bxc = fsb("bxc", [DH, H])
        bx3 = fsb("bx3", [DH, H, 3])
        tmp8 = fsb("tmp8", [P, H])
        rt8 = fsb("rt8", [P, H])
        r1 = fsb("r1", [3, 4, INNER])
        r2 = fsb("r2", [3, 4, D])
        r3 = fsb("r3", [3, 4, D])
        p1 = ExitStack()
        _, fps = allocator(p1)
        ptf = fps("ptf", [P, 2, 512])
        pls = fps("pls", [P, KC, INNER])
        pbl = fps("pbl", [3, INNER])
        c_tl = sems("c_tl", 2)
        c_w = sem("c_w")
        c_bx = sem("c_bx")
        c_fold = sem("c_fold")
        c_chain = sem("c_chain")
        c_tr = sem("c_tr")
        c_even = sem("c_even")
        c_odd = sem("c_odd")
        c_plchain = sem("c_plchain")
        CT = 7
        with nc.Block() as block:
            @block.sync
            def _(sp):
                for k, (c0, c1) in enumerate(((0, CT), (CT, NCH))):
                    sp.dma_start(tl[:, c0:c1, :, :], rec_d[c0 * P * P:c1 * P * P, :].rearrange(
                        "(c t s) f -> t c s f", t=P, s=P)).then_inc(c_tl[k], 16)
                for k in range(2):
                    sp.wait_ge(c_tl[k], 16)

            @block.scalar
            def _(act):
                act.dma_start(gw[:, :, :], gnn_w.rearrange("(c p) n -> p c n", p=P)).then_inc(c_w, 16)
                with nc.allow_non_contiguous_dma("small columns"):
                    act.dma_start(diag[:, :], gnn_diag.rearrange("(c p) -> p c", p=P)).then_inc(c_w, 16)
                    act.dma_start(bxc[:, :], b_x.rearrange("(h d) -> d h", h=H)).then_inc(c_w, 16)
                act.dma_start(wxt[:, :, :], w_x_t.rearrange("(h d) f -> d h f", h=H)).then_inc(c_w, 16)
                act.dma_start(wsl[:, :], w_slice).then_inc(c_w, 16)
                act.dma_start(tmp8[:, :], temp.partition_broadcast(P)).then_inc(c_w, 16)
                act.dma_start(r2[:, 0, :], gnn_b.partition_broadcast(3)).then_inc(c_w, 16)
                act.dma_start(r2[:, 1, :], bout.partition_broadcast(3)).then_inc(c_w, 16)
                act.dma_start(r3[:, 0, :], b_out.partition_broadcast(3)).then_inc(c_w, 16)
                for h in range(H):
                    act.dma_start(r1[:, 0, h * G:(h + 1) * G], b_slice.partition_broadcast(3)).then_inc(c_w, 16)
                for c in range(1, NCH, 2):
                    act.wait_ge(c_tr, c + 1)
                    for f, t in enumerate((gidx, place_c, weight_c)):
                        last = nc.scalar.copy(t[:, c * P:(c + 1) * P], ptf[:, 1, f * P:(f + 1) * P])
                    last.then_inc(c_odd, 1)
                act.wait_ge(c_w, 17 * 16)

            @block.tensor
            def _(pe):
                for c in range(NCH):
                    pe.wait_ge(c_tl[c // CT], 16)
                    if c > 1:
                        pe.wait_ge(c_odd if c % 2 else c_even, c // 2)
                    for f in range(3):
                        last = nc.tensor.transpose(ptf[:, c % 2, f * P:(f + 1) * P], tl[:, c, :, f], ident[:, :])
                    last.then_inc(c_tr, 1)
                pe.wait_ge(c_w, 17 * 16)
                pe.wait_ge(c_bx, 1)
                for h in range(H):
                    for c in range(KC):
                        nc.tensor.matmul(pls[:, c, h * G:(h + 1) * G], wxt[:, h, c * P:(c + 1) * P], wsl[:, :],
                                         start=True, stop=True)
                    last = nc.tensor.matmul(pbl[:, h * G:(h + 1) * G], bx3[:, h, :], wsl[:, :], start=True, stop=True)
                last.then_inc(c_fold, 1)

            @block.gpsimd
            def _(pool):
                link = Chain(pool, c_plchain)
                pool.wait_ge(c_w, 17 * 16)
                link(pool.tensor_tensor(r2[:, 0, :], r2[:, 0, :], r2[:, 1, :], ALU.add))
                for parts, r in ((b1_3, r2), (b2_3, r3)):
                    split_rows(link, pool, parts[:, :], r[:, 0, :], ident, r[:, 1, :], r[:, 2, :], r[:, 3, :])

            @block.vector
            def _(dve):
                link = Chain(dve, c_chain)
                for t in (gidx, place_c, weight_c):
                    nc.vector.memset(t[:, NT:NTX], 0)
                nc.vector.memset(zer[:, :], 0.0)
                nc.vector.memset(snorm[:, :], 0.0)
                for c in range(0, NCH, 2):
                    dve.wait_ge(c_tr, c + 1)
                    for f, t in enumerate((gidx, place_c, weight_c)):
                        last = nc.vector.tensor_copy(t[:, c * P:(c + 1) * P], ptf[:, 0, f * P:(f + 1) * P])
                    last.then_inc(c_even, 1)
                dve.wait_ge(c_w, 17 * 16)
                for h in range(H):
                    last = nc.vector.tensor_copy(bx3[:, h, :], bxc[:, h:h + 1].to_broadcast([DH, 3]))
                last.then_inc(c_bx, 1)
                link(nc.vector.tensor_tensor(wx1[:, 0:KC, :], wx1[:, 0:KC, :], gw[:, :, :], ALU.add))
                link(nc.vector.tensor_scalar(diag[:, :], diag[:, :], 1.0, -1.0, ALU.add, ALU.mult))
                for c in range(KC):
                    nc.vector.tensor_scalar(wx1[:, KC + c, :], gw[:, c, :], diag[:, c:c + 1], None, ALU.mult)
                link(nc.vector.tensor_scalar(tmp8[:, :], tmp8[:, :], 0.1, 5.0, ALU.max, ALU.min))
                link(nc.vector.reciprocal(rt8[:, :], tmp8[:, :]))
                dve.wait_ge(c_fold, 1)
                for c in range(KC):
                    nc.vector.tensor_tensor(wls[:, c, :].rearrange("p (h g) -> p h g", g=G),
                                            pls[:, c, :].rearrange("p (h g) -> p h g", g=G),
                                            rt8[:, :].unsqueeze(2).to_broadcast([P, H, G]), ALU.mult)
                link(nc.vector.tensor_tensor(r1[:, 0, :], pbl[:, :], r1[:, 0, :], ALU.add))
                b3_ = r1[:, 0, :].rearrange("p (h g) -> p h g", g=G)
                link(nc.vector.tensor_tensor(b3_, b3_, rt8[0:3, :].unsqueeze(2).to_broadcast([3, H, G]), ALU.mult))
                split_rows(link, nc.vector, bl_3[:, :], r1[:, 0, :], ident, r1[:, 1, :], r1[:, 2, :], r1[:, 3, :])
        first.close()
        p1.close()

        X = sb("X", [P, RT, D])
        ohw = sb("ohw", [P, RT, P])
        xr = sb("xr", [P, D])
        xt = sb("xt", [P, D])
        en = sb("en", [P, D])
        et = sb("et", [P, D])
        st6 = sb("st6c", [P, 6])
        mv = sb("mvc", [P, 2])
        ve = sb("ve", [P, 1])
        sd = sb("sdc", [P, 1])
        iv = sb("iv", [P, 1])
        rs = sb("rsc", [P, 1])
        nm = sb("nm", [P, 1])
        ya = sb("ya", [P, D])
        yb = sb("yb", [P, D])
        yt = sb("yt", [P, D])
        mx = sb("mx", [P, H])
        nmx = sb("nmx", [P, H])
        rcm = sb("rcm", [P, H])
        nsum = sb("nsum", [P, NPAIR])
        ex = sb("ex", [P, H, G])
        sm = sb("sm", [P, H])
        rc = sb("rc", [P, H])
        sw = sb("sw", [P, H, G])
        swt = sb("swt", [P, INNER])
        NPB = 3
        pacc = ps("pacc", [P, NPB, 512])
        ptr = ps("ptrc", [P, 512])[:, 0:D]
        px = ps("px", [P, 512])[:, 0:D]
        pl = ps("pl", [P, 512])
        pS = ps("pS", [P, NPAIR, D])
        HALF = [(0, (RT + 1) // 2), ((RT + 1) // 2, RT)]
        BANK = [u % NPB for u in range(RT)]

        c_idx = sems("c_idx", 2)
        c_g = sems("c_g", RT)
        c_xfree = sems("c_xfree", RT)
        c_oh = sem("c_oh")
        c_acc = sem("c_acc")
        c_apart = sem("c_apart")
        d_x = sem("d_x")
        d_en = sem("d_en")
        d_tr = sem("d_tr")
        d_et = sem("d_et")
        d_mm = sem("d_mm")
        d_x1 = sem("d_x1")
        d_stat = sem("d_stat")
        d_var = sem("d_var")
        d_sd = sem("d_sd")
        d_iv = sem("d_iv")
        d_rs = sem("d_rs")
        d_ln = sem("d_ln")
        e_y = sem("e_y")
        e_yb = sem("e_yb")
        e_yt = sem("e_yt")
        e_yts = sem("e_yts")
        e_log = sem("e_log")
        e_mx = sem("e_mx")
        e_nmx = sem("e_nmx")
        e_nrm = sem("e_nrm")
        e_ex = sem("e_ex")
        e_inv = sem("e_inv")
        e_sw = sem("e_sw")
        e_swt = sem("e_swt")
        e_swts = sem("e_swts")
        e_S = sem("e_S")
        e_st = sem("e_st")

        def rounds(engine, gather, block_steps, first=0, at_end=None):
            def part(steps, k):
                return [(slot - k * RT, f) for slot, f in steps if k * RT <= slot < (k + 1) * RT]

            s0, s1, s2 = [part(block_steps, k) for k in range(3)]
            end0 = part(at_end or block_steps, 0)

            def run(*parts):
                steps = [(slot, f, t) for part, t in parts for slot, f in part]
                for _, f, t in sorted(steps, key=lambda s: s[0]):
                    f(t)

            with engine.Fori(first, first + LAG) as i:
                run((gather, i))
            flag = engine.value_load(apart[0:1, 0:1], min_val=0, max_val=1)
            with engine.If(flag == 0):
                run((gather, first + LAG), (s0, 0))
                run((gather, first + LAG + 1), (s1, 0), (s0, 1))
                with engine.Fori(first + LAG + 2, first + NBLK) as i:
                    t = i - (first + LAG)
                    run((gather, i), (s2, t - 2), (s1, t - 1), (s0, t))
            with engine.Else():
                if gather:
                    with engine.Fori(first + LAG, first + NBLK) as i:
                        run((gather, i))
                run((end0, 0))
                run((s1, 0), (end0, 1))
                with engine.Fori(2, NBLK - LAG) as t:
                    run((s2, t - 2), (s1, t - 1), (end0, t))
            with engine.Fori(NBLK - LAG, NBLK) as t:
                run((s2, t - 2), (s1, t - 1), (end0, t))
            run((s2, NBLK - 2), (s1, NBLK - 1))
            run((s2, NBLK - 1))

        def b3(t):
            return t[:, :].unsqueeze(2).to_broadcast([P, H, G])

        with nc.Block() as block:
            @block.sync
            def _(sp):
                def load(t, rows_):
                    sp.wait_ge(d_mm, t)
                    sp.dma_start(xt[:, :], xnt_d[bass.ds(t, 1), :, :].rearrange("o p f -> (o p) f")).then_inc(d_x, 16)
                    if rows_ == P:
                        sp.dma_start(xr[:, :], x[bass.ds(t * P, P), :]).then_inc(d_x, 16)
                    else:
                        sp.dma_start(xr[0:rows_, :], x[N - rows_:N, :]).then_inc(d_x, 16)

                def store(t):
                    sp.wait_ge(e_swts, t + 1)
                    sp.dma_start(swt_d[bass.ds(t, 1), :, :].rearrange("o p f -> (o p) f"), swt[:, :]).then_inc(e_st, 16)

                with sp.Fori(0, 3) as t:
                    load(t, P)
                with sp.Fori(3, NBLK - 1) as t:
                    load(t, P)
                    store(t - 3)
                load(NBLK - 1, LAST)
                with sp.Fori(NBLK - 4, NBLK) as t:
                    store(t)
                sp.wait_ge(e_st, 16 * NBLK)

            @block.gpsimd
            def _(pool):
                def gather(u):
                    def step(turn):
                        pool.wait_ge(c_apart, 1)
                        for k, (q0, _) in enumerate(HALF):
                            if u == q0:
                                pool.wait_ge(c_idx[k], turn)
                        pool.wait_ge(c_xfree[u], turn)
                        pool.indirect_dma_start(out=X[:, u, :], out_offset=None, in_=xn_d,
                                                in_offset=bass.IndirectOffsetOnAxis(ap=idxs[:, u:u + 1], axis=0)
                                                ).then_inc(c_g[u], 16)
                    return step

                rounds(pool, [(u, gather(u)) for u in range(RT)], [], first=1)

            @block.scalar
            def _(act):
                def stage(k, ahead):
                    q0, q1 = HALF[k]

                    def step(i):
                        r = i + ahead
                        for u in range(q0, q1):
                            act.wait_ge(c_g[u], 16 * r)
                        nc.scalar.copy(idxs[:, q0:q1], gidx[:, bass.ds(r * RT + q0, q1 - q0)]).then_inc(c_idx[k], 1)
                    return step

                def sums_out(t):
                    act.wait_ge(c_acc, (t + LAG) * RT + 2)
                    sums_of_block(t)

                def sums_out_at_end(t):
                    act.wait_ge(c_acc, NBLK * RT + 2)
                    sums_of_block(t)

                def sums_of_block(t):
                    act.wait_ge(d_tr, t)
                    nc.scalar.sem_inc(passed, 1)
                    nc.scalar.copy(en[:, :], row_of(t)).then_inc(d_en, 1)

                def sums_t(t):
                    act.wait_ge(d_tr, t + 1)
                    act.wait_ge(d_mm, t)
                    nc.scalar.copy(et[:, :], ptr).then_inc(d_et, 1)

                def keep_x1(t):
                    act.wait_ge(d_mm, t + 1)
                    nc.scalar.sem_inc(passed, 1)
                    nc.scalar.copy(row_of(t), px).then_inc(d_x1, 1)

                def root(t):
                    act.wait_ge(d_var, t + 1)
                    act.wait_ge(d_iv, t)
                    nc.scalar.activation(sd[:, :], ve[:, :], ACT.Sqrt).then_inc(d_sd, 1)

                def y_t(t):
                    act.wait_ge(e_yt, t + 1)
                    act.wait_ge(e_log, t)
                    nc.scalar.copy(yt[:, :], ptr).then_inc(e_yts, 1)

                def exponentials(t):
                    act.wait_ge(e_nmx, t + 1)
                    act.wait_ge(e_sw, t)
                    for h in range(H):
                        last = nc.scalar.activation(ex[:, h, :], pl[:, h * G:(h + 1) * G], ACT.Exp,
                                                    bias=nmx[:, h:h + 1], accum_out=sm[:, h:h + 1])
                    last.then_inc(e_ex, 1)

                def copy_y(t):
                    act.wait_ge(e_y, t + 1)
                    act.wait_ge(e_S, t)
                    nc.scalar.copy(yb[:, :], ya[:, :]).then_inc(e_yb, 1)

                def weights_t(t):
                    act.wait_ge(e_swt, t + 1)
                    act.wait_ge(e_st, 16 * t)
                    act.wait_ge(e_nrm, t)
                    for j in range(NPAIR):
                        q = slice(j * P, (j + 1) * P)
                        last = nc.scalar.activation(swt[:, q], pl[:, q], ACT.Copy, accum_out=nsum[:, j:j + 1])
                    last.then_inc(e_swts, 1)

                rest = [(2 * RT + 2, exponentials), (6, sums_t), (10.2, keep_x1), (RT + 10.6, y_t),
                        (2 * RT + 14, weights_t), (RT + 13.4, copy_y), (14.6, root)]
                stage(0, 0)(0)
                rounds(act, [(0.5, stage(1, 0)), (9.5, stage(0, 1))], [(1, sums_out)] + rest,
                       at_end=[(1, sums_out_at_end)] + rest)

            @block.tensor
            def _(pe):
                def tile(u):
                    def step(i):
                        pe.wait_ge(c_oh, i * RT + u + 1)
                        ago = next(k for k in range(1, RT + 1) if BANK[u - k] == BANK[u])
                        pe.wait_ge(c_acc, i * RT + u + 3 - min(ago, NPB))
                        pe.wait_ge(c_g[u], 16 * (i + 1))
                        nc.tensor.matmul(pacc[:, BANK[u], 0:D], ohw[:, u, :], X[:, u, :], start=True, stop=True
                                         ).then_inc(c_xfree[u], 1)
                    return step

                def transpose_sums(t):
                    pe.wait_ge(d_en, t + 1)
                    for c in range(KC):
                        last = nc.tensor.transpose(ptr[:, c * P:(c + 1) * P], en[:, c * P:(c + 1) * P], ident[:, :])
                    last.then_inc(d_tr, 1)

                def x1(t):
                    pe.wait_ge(e_y, t)
                    pe.wait_ge(d_x1, t)
                    pe.wait_ge(d_stat, 2 * t)
                    nc.tensor.matmul(px, ones3[:, :], b1_3[:, :], start=True, stop=False)
                    pe.wait_ge(d_x, 32 * (t + 1))
                    nc.tensor.matmul(px, ident[:, :], xr[:, :], start=False, stop=False)
                    for c in range(KC):
                        nc.tensor.matmul(px, xt[:, c * P:(c + 1) * P], wx1[:, c, :], start=False, stop=False)

                def x1_sums(t):
                    pe.wait_ge(d_et, t + 1)
                    for c in range(KC):
                        last = nc.tensor.matmul(px, et[:, c * P:(c + 1) * P], wx1[:, KC + c, :],
                                                start=False, stop=(c == KC - 1))
                    last.then_inc(d_mm, 1)

                def transpose_y(t):
                    pe.wait_ge(e_y, t + 1)
                    for c in range(KC):
                        last = nc.tensor.transpose(ptr[:, c * P:(c + 1) * P], ya[:, c * P:(c + 1) * P], ident[:, :])
                    last.then_inc(e_yt, 1)

                def logits(t):
                    pe.wait_ge(e_swts, t)
                    nc.tensor.matmul(pl[:, :], ones3[:, :], bl_3[:, :], start=True, stop=False)
                    pe.wait_ge(e_yts, t + 1)
                    nc.tensor.matmul(pl[:, :], yt[:, 0:P], wls[:, 0, :], start=False, stop=False)

                def logits_rest(t):
                    for c in range(1, KC):
                        last = nc.tensor.matmul(pl[:, :], yt[:, c * P:(c + 1) * P], wls[:, c, :],
                                                start=False, stop=(c == KC - 1))
                    last.then_inc(e_log, 1)

                def pair_sum(j):
                    return nc.tensor.matmul(pS[:, j, :], sw[:, 2 * j:2 * j + 2, :], yb[:, :],
                                            start=False, stop=False, skip_group_check=True)

                def slice_sums(t):
                    pe.wait_ge(e_sw, t + 1)
                    pe.wait_ge(e_yb, t + 1)
                    for j in range(2):
                        pair_sum(j)

                def slice_sums_rest(t):
                    for j in range(2, NPAIR):
                        last = pair_sum(j)
                    last.then_inc(e_S, 1)

                def transpose_weights(t):
                    pe.wait_ge(e_sw, t + 1)
                    for j in range(NPAIR):
                        last = nc.tensor.transpose(pl[:, j * P:(j + 1) * P], sw[:, 2 * j:2 * j + 2, :], ident[:, :])
                    last.then_inc(e_swt, 1)

                for k in range(2):
                    nc.tensor.matmul(pS[:, 2 * k:2 * k + 2, :], ident[:, :], zer[:, :], start=True, stop=False,
                                     skip_group_check=True)
                for u in range(RT):
                    nc.tensor.sem_inc(c_xfree[u], 1)
                rounds(pe, [(u, tile(u)) for u in range(RT)],
                       [(3.5, transpose_sums), (6.5, x1), (8.5, x1_sums), (RT + 9.6, transpose_y),
                        (RT + 14.7, logits), (RT + 15.7, logits_rest), (2 * RT + 11, slice_sums),
                        (2 * RT + 12.2, slice_sums_rest), (2 * RT + 13.2, transpose_weights)])

            @block.vector
            def _(dve):
                def onehot(t, u):
                    nc.vector.tensor_scalar(ohw[:, u, :], ion[:, :], place_c[:, bass.ds(t, 1)],
                                            weight_c[:, bass.ds(t, 1)], ALU.is_equal, ALU.mult).then_inc(c_oh, 1)

                state = {}

                def blocks(u0, u1):
                    def step(i):
                        _, state["blocks"] = nc.values_load_multi_w_load_instructions(
                            tblk[0:1, bass.ds(i * RT + u0, u1 - u0)], engines=[mybir.EngineType.DVE],
                            min_val=0, max_val=NBLK - 1,
                            skip_runtime_bounds_check_because="the tiles' blocks are cut to NBLK - 1")
                        state["first"] = u0
                    return step

                def add(u):
                    def step(i):
                        to = row_of(state["blocks"][u - state["first"]])
                        dve.wait_ge(c_xfree[u], i + 2)
                        dve.wait_ge(c_acc, i * RT + u + 2)
                        nc.vector.tensor_tensor(to, pacc[:, BANK[u], 0:D], to, ALU.add).then_inc(c_acc, 1)
                        onehot((i + 1) * RT + u, u)
                    return step

                def stats(t):
                    dve.wait_ge(d_x1, t + 1)
                    nc.vector.bn_stats(st6[:, :], px).then_inc(d_stat, 1)

                def mean_var(t):
                    dve.wait_ge(d_stat, 2 * t + 1)
                    nc.vector.sem_inc(passed, 1)
                    nc.vector.bn_aggr(mv[:, :], st6[:, :]).then_inc(d_stat, 1)

                def var_eps(t):
                    dve.wait_ge(d_stat, 2 * t + 2)
                    nc.vector.tensor_scalar(ve[:, :], mv[:, 1:2], EPS, None, ALU.add).then_inc(d_var, 1)

                def inverse(t):
                    dve.wait_ge(d_sd, t + 1)
                    nc.vector.reciprocal(iv[:, :], sd[:, :]).then_inc(d_iv, 1)

                def masked_rstd(t):
                    dve.wait_ge(d_iv, t + 1)
                    dve.wait_ge(e_y, t)
                    nc.vector.tensor_tensor(rs[:, :], iv[:, :], mask[:, bass.ds(t, 1)], ALU.mult).then_inc(d_rs, 1)

                def shift(t):
                    dve.wait_ge(d_rs, t + 1)
                    nc.vector.scalar_tensor_tensor(out=nm[:, :], in0=mv[:, 0:1], scalar=-1.0, in1=rs[:, :],
                                                   op0=ALU.mult, op1=ALU.mult).then_inc(d_ln, 1)

                def normalise(t):
                    dve.wait_ge(d_ln, t + 1)
                    dve.wait_ge(e_yts, t)
                    dve.wait_ge(e_yb, t)
                    nc.vector.tensor_scalar(ya[:, :], px, rs[:, :], nm[:, :], ALU.mult, ALU.add).then_inc(e_y, 1)

                lg = pl[:, :].rearrange("p (h g) -> p h g", g=G)

                def maxima(t):
                    dve.wait_ge(e_log, t + 1)
                    nc.vector.tensor_reduce(mx[:, :], lg, AX.X, ALU.max).then_inc(e_mx, 1)

                def minus_maxima(t):
                    dve.wait_ge(e_mx, t + 1)
                    dve.wait_ge(e_ex, t)
                    nc.vector.tensor_scalar(nmx[:, :], mx[:, :], -1.0, None, ALU.mult).then_inc(e_nmx, 1)

                def inverses(t):
                    dve.wait_ge(e_ex, t + 1)
                    nc.vector.reciprocal(rc[:, :], sm[:, :]).then_inc(e_inv, 1)

                def masked_inverses(t):
                    dve.wait_ge(e_inv, 2 * t + 1)
                    nc.vector.tensor_scalar(rcm[:, :], rc[:, :], mask[:, bass.ds(t, 1)], None, ALU.mult
                                            ).then_inc(e_inv, 1)

                def add_norms(t):
                    dve.wait_ge(e_swts, t + 1)
                    dve.wait_ge(e_nrm, t)
                    nc.vector.tensor_tensor(snorm[:, :], snorm[:, :], nsum[:, :], ALU.add).then_inc(e_nrm, 1)

                def slice_weights(t):
                    dve.wait_ge(e_inv, 2 * t + 2)
                    dve.wait_ge(e_swt, t)
                    nc.vector.tensor_tensor(sw[:, :, :], ex[:, :, :], b3(rcm), ALU.mult).then_inc(e_sw, 1)

                nc.vector.sem_inc(c_apart, 1)
                nc.vector.sem_inc(c_acc, 2)
                for u in range(RT):
                    onehot(u, u)
                mid = RT // 2 + 1
                rounds(dve, [(-0.5, blocks(0, mid)), (mid - 0.5, blocks(mid, RT))] + [(u, add(u)) for u in range(RT)],
                       [(11, stats), (12, mean_var), (13, var_eps), (RT + 0.2, inverse),
                        (RT + 1.1, masked_rstd), (RT + 1.3, shift), (RT + 2.3, normalise),
                        (RT + 16.9, maxima), (2 * RT + 1.6, minus_maxima), (2 * RT + 6, inverses),
                        (2 * RT + 7, masked_inverses), (2 * RT + 8, slice_weights), (2 * RT + 15, add_norms)])
                dve.wait_ge(e_S, NBLK)
                nc.vector.tensor_copy(sfx[:, :, :], pS[:, :, :])
                dve.wait_ge(e_nrm, NBLK)
        phase.close()

        phase = ExitStack()
        sb, ps = allocator(phase)
        wfx = sb("wfx", [P, KC, INNER])
        bfx = sb("bfx", [P, NPAIR, P])
        wo = sb("wo", [P, NPAIR, D])
        w2 = sb("w2", [P, 3, P])
        st_ = sb("st_", [P, NPAIR, KC, P])
        tok = sb("tok", [P, NPAIR, P])
        tb2 = sb("tb2", [P, NPAIR, P])
        den = sb("den", [P, NPAIR])
        rden = sb("rden", [P, NPAIR])
        tt = sb("tt", [P, NPAIR, P])
        qt = sb("qt", [P, 3, NPAIR, P])
        am = sb("am", [P, NPAIR, G])
        mxf = sb("mxf", [P, NPAIR])
        smf = sb("smf", [P, NPAIR])
        rcf = sb("rcf", [P, NPAIR])
        ab = sb("ab", [P, NPAIR, P])
        abt = sb("abt", [P, NPAIR, P])
        vw = sb("vw", [P, NPAIR, D])
        pa = ps("pa", [P, 3, NPAIR, P])
        pb = ps("pb", [P, NPAIR, P])
        pc = ps("pc", [P, NPAIR, P])
        pd = ps("pd", [P, NPAIR, D])
        f_w = sem("f_w")
        f_z = sem("f_z")
        f_pe = sem("f_pe")
        f_chain = sem("f_chain")
        f_exp = sem("f_exp")
        f_sh = sem("f_sh")
        wide = pa[:, 0:2, :, :].rearrange("p a j n -> p (a j n)")
        with nc.Block() as block:
            @block.sync
            def _(sp):
                sp.dma_start(wfx[:, :, :], w_fx.rearrange("(c p) n -> p c n", p=P)).then_inc(f_w, 16)
                sp.dma_start(bfx[:, :, :].rearrange("p j n -> p (j n)"), b_fx.partition_broadcast(P)).then_inc(f_w, 16)
                sp.dma_start(wo[:, :, :], w_out.rearrange("(j p) n -> p j n", p=P)).then_inc(f_w, 16)
                sp.wait_ge(f_z, 1)
                for k, w in enumerate((w_q, w_k, w_v)):
                    for a in range(2):
                        q = slice(a * DH, (a + 1) * DH)
                        sp.dma_start(w2[q, k, q], w).then_inc(f_w, 16)
                sp.wait_ge(f_w, 9 * 16)

            @block.tensor
            def _(pe):
                for j in range(NPAIR):
                    for c in range(KC):
                        k = j * KC + c
                        last = nc.tensor.transpose(wide[:, k * P:(k + 1) * P], sfx[:, j, c * P:(c + 1) * P],
                                                   ident[:, :])
                last.then_inc(f_pe, 1)
                pe.wait_ge(f_w, 9 * 16)
                pe.wait_ge(f_sh, 1)
                for j in range(NPAIR):
                    for c in range(KC):
                        last = nc.tensor.matmul(pb[:, j, :], st_[:, j, c, :], wfx[:, c, j * P:(j + 1) * P],
                                                start=(c == 0), stop=(c == KC - 1))
                last.then_inc(f_pe, 1)
                pe.wait_ge(f_sh, 2)
                for j in range(NPAIR):
                    last = nc.tensor.transpose(pc[:, j, :], tb2[:, j, :], ident[:, :])
                last.then_inc(f_pe, 1)
                pe.wait_ge(f_sh, 3)
                for k in range(3):
                    last = nc.tensor.matmul(pa[:, k, :, :], w2[:, k, :], tt[:, :, :], start=True, stop=True)
                last.then_inc(f_pe, 1)
                pe.wait_ge(f_sh, 4)
                for j in range(NPAIR):
                    nc.tensor.matmul(pb[:, j, :], qt[:, 0, j, :], qt[:, 1, j, :], start=True, stop=True)
                for j in range(NPAIR):
                    last = nc.tensor.matmul(pd[:, j, :], qt[:, 2, j, :], wo[:, j, :], start=True, stop=True)
                last.then_inc(f_pe, 1)
                pe.wait_ge(f_sh, 5)
                for j in range(NPAIR):
                    last = nc.tensor.transpose(pc[:, j, :], ab[:, j, :], ident[:, :])
                last.then_inc(f_pe, 1)
                pe.wait_ge(f_sh, 6)
                for j in range(NPAIR):
                    last = nc.tensor.matmul(pd[:, j, :], abt[:, j, :], vw[:, j, :], start=True, stop=True)
                last.then_inc(f_pe, 1)

            @block.scalar
            def _(act):
                act.wait_ge(f_exp, 1)
                nc.scalar.activation(am[:, :, :], am[:, :, :], ACT.Exp).then_inc(f_exp, 1)

            @block.vector
            def _(dve):
                link = Chain(dve, f_chain)
                halves = [slice(a * DH, (a + 1) * DH) for a in range(2)]
                nc.vector.memset(w2[:, :, :], 0.0).then_inc(f_z, 1)
                nc.vector.memset(tb2[:, :, :], 0.0)
                link(nc.vector.memset(ab[:, :, :], 0.0))
                link(nc.vector.tensor_scalar(den[:, :], snorm[:, :], EPS, None, ALU.add))
                link(nc.vector.reciprocal(rden[:, :], den[:, :]))
                dve.wait_ge(f_pe, 1)
                nc.vector.tensor_copy(st_[:, :, :, :].rearrange("p j c n -> p (j c n)"), wide).then_inc(f_sh, 1)
                dve.wait_ge(f_w, 9 * 16)
                link(nc.vector.tensor_tensor(tok[:, :, :], bfx[:, :, :],
                                             snorm[:, :].unsqueeze(2).to_broadcast([P, NPAIR, P]), ALU.mult))
                dve.wait_ge(f_pe, 2)
                link(nc.vector.tensor_tensor(tok[:, :, :], tok[:, :, :], pb[:, :, :], ALU.add))
                for q in halves:
                    last = nc.vector.tensor_tensor(tb2[q, :, q], tok[q, :, q],
                                                   rden[q, :].unsqueeze(2).to_broadcast([DH, NPAIR, DH]), ALU.mult)
                last.then_inc(f_sh, 1)
                dve.wait_ge(f_pe, 3)
                nc.vector.tensor_copy(tt[:, :, :], pc[:, :, :]).then_inc(f_sh, 1)
                dve.wait_ge(f_pe, 4)
                nc.vector.tensor_copy(qt[:, :, :, :].rearrange("p k j n -> p (k j n)"),
                                      pa[:, :, :, :].rearrange("p k j n -> p (k j n)")).then_inc(f_sh, 1)
                dve.wait_ge(f_pe, 5)
                for q in halves:
                    link(nc.vector.tensor_scalar(am[q, :, :], pb[q, :, q], DH ** -0.5, None, ALU.mult))
                link(nc.vector.tensor_reduce(mxf[:, :], am[:, :, :], AX.X, ALU.max))
                nc.vector.tensor_tensor(am[:, :, :], am[:, :, :], mxf[:, :].unsqueeze(2).to_broadcast([P, NPAIR, G]),
                                        ALU.subtract).then_inc(f_exp, 1)
                link(nc.vector.tensor_copy(vw[:, :, :], pd[:, :, :]))
                dve.wait_ge(f_exp, 2)
                link(nc.vector.tensor_reduce(smf[:, :], am[:, :, :], AX.X, ALU.add))
                link(nc.vector.reciprocal(rcf[:, :], smf[:, :]))
                for q in halves:
                    last = nc.vector.tensor_tensor(ab[q, :, q], am[q, :, :],
                                                   rcf[q, :].unsqueeze(2).to_broadcast([DH, NPAIR, G]), ALU.mult)
                last.then_inc(f_sh, 1)
                dve.wait_ge(f_pe, 6)
                nc.vector.tensor_copy(abt[:, :, :], pc[:, :, :]).then_inc(f_sh, 1)
                dve.wait_ge(f_pe, 7)
                nc.vector.tensor_copy(pmat[:, :, :], pd[:, :, :])
        phase.close()

        phase = ExitStack()
        sb, ps = allocator(phase)
        NB4 = 4
        st4 = sb("st4", [P, NB4, INNER])
        ob = sb("ob", [P, 2, D])
        po = ps("po", [P, 2, 512])
        g_l = sems("g_l", NB4)
        g_mm = sem("g_mm")
        g_o = sem("g_o")
        g_st = sems("g_st", 2)
        NG4 = NBLK // NB4
        with nc.Block() as block:
            @block.sync
            def _(sp):
                def load(t, q):
                    sp.dma_start(st4[:, q, :], swt_d[bass.ds(t, 1), :, :].rearrange("o p f -> (o p) f")
                                 ).then_inc(g_l[q], 16)

                for q in range(NB4):
                    load(q, q)
                with sp.Fori(0, NG4 - 1) as i:
                    for q in range(NB4):
                        sp.wait_ge(g_mm, i * NB4 + q + 1)
                        load(i * NB4 + q + NB4, q)
                for q in range(NBLK - NG4 * NB4):
                    sp.wait_ge(g_mm, (NG4 - 1) * NB4 + q + 1)
                    load(NG4 * NB4 + q, q)

            @block.gpsimd
            def _(pool):
                def store(t, par, n, rows_):
                    pool.wait_ge(g_o, n)
                    pool.wait_ge(g_l[0], 16)
                    if rows_ == P:
                        pool.dma_start(out[bass.ds(t * P, P), :], ob[:, par, :]).then_inc(g_st[par], 16)
                    else:
                        pool.dma_start(out[N - rows_:N, :], ob[0:rows_, par, :]).then_inc(g_st[par], 16)

                with pool.Fori(0, NBLK // 2 - 1) as i:
                    for par in range(2):
                        store(2 * i + par, par, 2 * i + par + 1, P)
                store(NBLK - 2, 0, NBLK - 1, P)
                store(NBLK - 1, 1, NBLK, LAST)
                for par in range(2):
                    pool.wait_ge(g_st[par], 16 * (NBLK // 2))

            def product(pe, t, q, n):
                if not isinstance(t, int) or t > 1:
                    pe.wait_ge(g_o, t - 1)
                nc.tensor.matmul(po[:, q % 2, 0:D], ones3[:, :], b2_3[:, :], start=True, stop=False)
                pe.wait_ge(g_l[q], n)
                for j in range(NPAIR):
                    last = nc.tensor.matmul(po[:, q % 2, 0:D], st4[:, q, j * P:(j + 1) * P], pmat[:, j, :],
                                            start=False, stop=(j == NPAIR - 1))
                last.then_inc(g_mm, 1)

            @block.tensor
            def _(pe):
                for q in range(NB4):
                    product(pe, q, q, 16)
                with pe.Fori(1, NG4) as i:
                    for q in range(NB4):
                        product(pe, i * NB4 + q, q, 16 * (i + 1))
                for q in range(NBLK - NG4 * NB4):
                    product(pe, NG4 * NB4 + q, q, 16 * (NG4 + 1))

            @block.vector
            def _(dve):
                with dve.Fori(0, NBLK // 2) as i:
                    for par in range(2):
                        t = 2 * i + par
                        dve.wait_ge(g_mm, t + 1)
                        dve.wait_ge(g_st[par], 16 * i)
                        nc.vector.tensor_tensor(ob[:, par, :], po[:, par, 0:D],
                                                big[:, bass.ds(t, 1), :].rearrange("p a b -> p (a b)"), ALU.add
                                                ).then_inc(g_o, 1)
        phase.close()


def kernel(**inputs):
    import numpy as np
    import concourse.bacc as bacc
    from concourse.bass_utils import run_bass_kernel_spmd

    a = {k.replace("L0_", ""): np.asarray(v) for k, v in inputs.items()}
    wqkv = a["mix_Wqkv"]
    arrays = {
        "x": a["x"], "src": a["src"], "dst": a["dst"], "edge_weight": a["edge_weight"],
        "gnn_w": a["gnn_weight"], "gnn_diag": a["gnn_learnable_diag"], "gnn_b": a["gnn_bias"],
        "wqkv": wqkv, "wqkv_t": wqkv.T, "wout_t": a["mix_Wout"].T, "bout": a["mix_bout"],
        "w_fx": a["ffn_W_fx"], "b_fx": a["ffn_b_fx"], "w_x_t": a["ffn_W_x"].T, "b_x": a["ffn_b_x"],
        "w_slice": a["ffn_W_slice"], "b_slice": a["ffn_b_slice"], "w_q": a["ffn_W_q"], "w_k": a["ffn_W_k"],
        "w_v": a["ffn_W_v"], "w_out": a["ffn_W_out"], "b_out": a["ffn_b_out"],
        "temp": a["ffn_temperature"].reshape(-1),
    }
    nc = bacc.Bacc("TRN2", target_bir_lowering=False, num_devices=1)
    arrays = {f"in_{k}": np.ascontiguousarray(v) for k, v in arrays.items()}
    aps = [nc.dram_tensor(k, v.shape, mybir.dt.from_np(v.dtype), kind="ExternalInput").ap() for k, v in arrays.items()]
    out = nc.dram_tensor("out_x", (N, D), F32, kind="ExternalOutput").ap()
    gps_layer(nc, *aps, out)
    r = run_bass_kernel_spmd(nc, [arrays], core_ids=[0])
    return r.results[0]["out_x"]
```
